# Optimizing a Trainium2 kernel written in Bass

```python
import numpy as np
import jax
import jax.numpy as jnp

def _softmax(x, axis=-1):
    return jax.nn.softmax(x, axis=axis)

def _gelu(x):
    return jax.nn.gelu(x, approximate=True)

def _silu(x):
    return jax.nn.silu(x)

def _sigmoid(x):
    return jax.nn.sigmoid(x)

def _layernorm(x, axis=-1, eps=1e-05):
    m = jnp.mean(x, axis=axis, keepdims=True)
    v = jnp.var(x, axis=axis, keepdims=True)
    return (x - m) / jnp.sqrt(v + eps)

def _scatter_add(tgt, idx, src, axis=0):
    return tgt.at[idx].add(src)

def _segment_sum(src, seg, n):
    return jax.ops.segment_sum(src, seg, n)
kernel_name = 'mk_macaron_d1_jaxref_r4_7f045b'

def setup_inputs(seed: int=0):
    np.random.seed(seed)
    _w = jnp.asarray

    def _L0_attn_setup():
        import jax, jax.numpy as jnp
        import numpy as np
        H = 256
        D = 64
        CHUNK = 128
        LR = 0.1
        GRAD_SCALE = 0.1
        MAX_GRAD_NORM = 1.0
        EPS = 1e-06
        P = 2 * D * D

        def _xavier(k, shape, gain=0.1):
            fan_out, fan_in = shape
            a = gain * np.sqrt(6.0 / (fan_in + fan_out))
            return jax.random.uniform(k, shape, jnp.float32, -a, a)

        def _causal_dwconv(x, w, b):
            T = x.shape[1]
            xp = jnp.pad(x, ((0, 0), (3, 0), (0, 0)))
            y = b
            for j in range(4):
                y = y + xp[:, j:j + T, :] * w[:, j]
            return y

        def _mem_loss(p, k_t, v_t):
            W1 = p[:D * D].reshape(D, D)
            W2 = p[D * D:].reshape(D, D)
            pred = jax.nn.silu(k_t @ W1.T) @ W2.T
            return jnp.sum((pred - v_t) ** 2)
        _grad_fn = jax.vmap(jax.vmap(jax.grad(_mem_loss), in_axes=(None, 0, 0)), in_axes=(0, 0, 0))

        def _forward(hidden, Wk, Wv, Wq, Wo, ckw, ckb, cvw, cvb, cqw, cqb, mW1, mW2, aW, ab, eW, eb, tW, tb, norm_g, gW, gb):
            B, S, _ = hidden.shape
            k = _causal_dwconv(hidden @ Wk.T, ckw, ckb)
            v = _causal_dwconv(hidden @ Wv.T, cvw, cvb)
            q = _causal_dwconv(hidden @ Wq.T, cqw, cqb)
            alpha = (jax.nn.sigmoid(hidden @ aW.T + ab) * 0.1).mean(-1)
            eta = (jax.nn.sigmoid(hidden @ eW.T + eb) * 0.9 + 0.05).mean(-1)
            theta = (jax.nn.softplus(hidden @ tW.T + tb) * LR).mean(-1)
            W_state = jnp.tile(jnp.concatenate([mW1.ravel(), mW2.ravel()])[None], (B, 1))
            S_state = jnp.zeros_like(W_state)

            def step(carry, xs):
                Sm, Wm = carry
                gt, et, tt, at = xs
                Sm = et[:, None] * Sm - tt[:, None] * gt
                Wm = (1.0 - at[:, None]) * Wm + Sm
                return ((Sm, Wm), Wm)
            outs = []
            for c0 in range(0, S, CHUNK):
                sl = slice(c0, c0 + CHUNK)
                g = _grad_fn(W_state, k[:, sl], v[:, sl]) * GRAD_SCALE
                gn = jnp.maximum(jnp.linalg.norm(g, axis=-1, keepdims=True), EPS)
                g = g * jnp.minimum(MAX_GRAD_NORM / gn, 1.0)
                g = jax.lax.stop_gradient(g)
                xs = (jnp.swapaxes(g, 0, 1), eta[:, sl].T, theta[:, sl].T, alpha[:, sl].T)
                (S_state, W_state), Wtraj = jax.lax.scan(step, (S_state, W_state), xs)
                Wtraj = jnp.swapaxes(Wtraj, 0, 1)
                T = Wtraj.shape[1]
                W1t = Wtraj[..., :D * D].reshape(B, T, D, D)
                W2t = Wtraj[..., D * D:].reshape(B, T, D, D)
                h = jax.nn.silu(jnp.einsum('btd,btod->bto', q[:, sl], W1t))
                outs.append(jnp.einsum('bto,btpo->btp', h, W2t))
            retrieved = jnp.concatenate(outs, axis=1)
            out = retrieved @ Wo.T
            out = out * jax.lax.rsqrt(jnp.mean(out * out, -1, keepdims=True) + EPS) * norm_g
            gate = hidden @ gW.T + gb
            return out * gate
        key = jax.random.key(seed)
        ks = jax.random.split(key, 24)
        B, S = (1, 256)
        return {'hidden': jax.random.normal(ks[0], (B, S, H), jnp.float32), 'Wk': _xavier(ks[1], (D, H)), 'Wv': _xavier(ks[2], (D, H)), 'Wq': _xavier(ks[3], (D, H)), 'Wo': _xavier(ks[4], (H, D)), 'ckw': jax.random.normal(ks[5], (D, 4), jnp.float32) * 0.05, 'ckb': jnp.zeros((D,), jnp.float32), 'cvw': jax.random.normal(ks[6], (D, 4), jnp.float32) * 0.05, 'cvb': jnp.zeros((D,), jnp.float32), 'cqw': jax.random.normal(ks[7], (D, 4), jnp.float32) * 0.05, 'cqb': jnp.zeros((D,), jnp.float32), 'mW1': _xavier(ks[8], (D, D)), 'mW2': _xavier(ks[9], (D, D)), 'aW': jax.random.normal(ks[10], (D, H), jnp.float32) * 0.02, 'ab': jnp.zeros((D,), jnp.float32), 'eW': jax.random.normal(ks[11], (D, H), jnp.float32) * 0.02, 'eb': jnp.zeros((D,), jnp.float32), 'tW': jax.random.normal(ks[12], (D, H), jnp.float32) * 0.02, 'tb': jnp.zeros((D,), jnp.float32), 'norm_g': jnp.ones((H,), jnp.float32), 'gW': jnp.zeros((H, H), jnp.float32), 'gb': jnp.ones((H,), jnp.float32)}
    _L0_attn_in = _L0_attn_setup()

    def _L0_ffn_setup():
        import jax, jax.numpy as jnp
        import numpy as np
        B, S, D = (4, 512, 256)
        E = 8
        F = 1024
        T = B * S
        CAP = 320
        key = jax.random.key(seed)
        k1, k2, k3, k4 = jax.random.split(key, 4)
        inputs = jax.random.normal(k1, (B, S, D), dtype=jnp.float32)
        gate_w = jax.random.normal(k2, (D, E), dtype=jnp.float32) / np.sqrt(D)
        w1 = jax.random.normal(k3, (E, D, F), dtype=jnp.float32) / np.sqrt(D)
        w2 = jax.random.normal(k4, (E, F, D), dtype=jnp.float32) / np.sqrt(F)
        return {'inputs': inputs, 'gate_w': gate_w, 'w1': w1, 'w2': w2}
    _L0_ffn_in = _L0_ffn_setup()
    _d = {'L0_attn_hidden': _L0_attn_in['hidden'], 'L0_attn_Wk': _L0_attn_in['Wk'], 'L0_attn_Wv': _L0_attn_in['Wv'], 'L0_attn_Wq': _L0_attn_in['Wq'], 'L0_attn_Wo': _L0_attn_in['Wo'], 'L0_attn_ckw': _L0_attn_in['ckw'], 'L0_attn_ckb': _L0_attn_in['ckb'], 'L0_attn_cvw': _L0_attn_in['cvw'], 'L0_attn_cvb': _L0_attn_in['cvb'], 'L0_attn_cqw': _L0_attn_in['cqw'], 'L0_attn_cqb': _L0_attn_in['cqb'], 'L0_attn_mW1': _L0_attn_in['mW1'], 'L0_attn_mW2': _L0_attn_in['mW2'], 'L0_attn_aW': _L0_attn_in['aW'], 'L0_attn_ab': _L0_attn_in['ab'], 'L0_attn_eW': _L0_attn_in['eW'], 'L0_attn_eb': _L0_attn_in['eb'], 'L0_attn_tW': _L0_attn_in['tW'], 'L0_attn_tb': _L0_attn_in['tb'], 'L0_attn_norm_g': _L0_attn_in['norm_g'], 'L0_attn_gW': _L0_attn_in['gW'], 'L0_attn_gb': _L0_attn_in['gb'], 'L0_ffn_gate_w': _L0_ffn_in['gate_w'], 'L0_ffn_w1': _L0_ffn_in['w1'], 'L0_ffn_w2': _L0_ffn_in['w2']}
    _x0 = _d['L0_attn_hidden']
    _d['L0_attn_hidden'] = jax.random.normal(jax.random.fold_in(jax.random.key(seed), 1), (8, 1024, 256), dtype=_x0.dtype)
    del _x0
    return _d

def reference(L0_attn_hidden, L0_attn_Wk, L0_attn_Wv, L0_attn_Wq, L0_attn_Wo, L0_attn_ckw, L0_attn_ckb, L0_attn_cvw, L0_attn_cvb, L0_attn_cqw, L0_attn_cqb, L0_attn_mW1, L0_attn_mW2, L0_attn_aW, L0_attn_ab, L0_attn_eW, L0_attn_eb, L0_attn_tW, L0_attn_tb, L0_attn_norm_g, L0_attn_gW, L0_attn_gb, L0_ffn_gate_w, L0_ffn_w1, L0_ffn_w2):

    def _L0_attn_ref(hidden, Wk, Wv, Wq, Wo, ckw, ckb, cvw, cvb, cqw, cqb, mW1, mW2, aW, ab, eW, eb, tW, tb, norm_g, gW, gb):
        import jax, jax.numpy as jnp
        import numpy as np
        H = 256
        D = 64
        CHUNK = 128
        LR = 0.1
        GRAD_SCALE = 0.1
        MAX_GRAD_NORM = 1.0
        EPS = 1e-06
        P = 2 * D * D

        def _xavier(k, shape, gain=0.1):
            fan_out, fan_in = shape
            a = gain * np.sqrt(6.0 / (fan_in + fan_out))
            return jax.random.uniform(k, shape, jnp.float32, -a, a)

        def _causal_dwconv(x, w, b):
            T = x.shape[1]
            xp = jnp.pad(x, ((0, 0), (3, 0), (0, 0)))
            y = b
            for j in range(4):
                y = y + xp[:, j:j + T, :] * w[:, j]
            return y

        def _mem_loss(p, k_t, v_t):
            W1 = p[:D * D].reshape(D, D)
            W2 = p[D * D:].reshape(D, D)
            pred = jax.nn.silu(k_t @ W1.T) @ W2.T
            return jnp.sum((pred - v_t) ** 2)
        _grad_fn = jax.vmap(jax.vmap(jax.grad(_mem_loss), in_axes=(None, 0, 0)), in_axes=(0, 0, 0))

        def _forward(hidden, Wk, Wv, Wq, Wo, ckw, ckb, cvw, cvb, cqw, cqb, mW1, mW2, aW, ab, eW, eb, tW, tb, norm_g, gW, gb):
            B, S, _ = hidden.shape
            k = _causal_dwconv(hidden @ Wk.T, ckw, ckb)
            v = _causal_dwconv(hidden @ Wv.T, cvw, cvb)
            q = _causal_dwconv(hidden @ Wq.T, cqw, cqb)
            alpha = (jax.nn.sigmoid(hidden @ aW.T + ab) * 0.1).mean(-1)
            eta = (jax.nn.sigmoid(hidden @ eW.T + eb) * 0.9 + 0.05).mean(-1)
            theta = (jax.nn.softplus(hidden @ tW.T + tb) * LR).mean(-1)
            W_state = jnp.tile(jnp.concatenate([mW1.ravel(), mW2.ravel()])[None], (B, 1))
            S_state = jnp.zeros_like(W_state)

            def step(carry, xs):
                Sm, Wm = carry
                gt, et, tt, at = xs
                Sm = et[:, None] * Sm - tt[:, None] * gt
                Wm = (1.0 - at[:, None]) * Wm + Sm
                return ((Sm, Wm), Wm)
            outs = []
            for c0 in range(0, S, CHUNK):
                sl = slice(c0, c0 + CHUNK)
                g = _grad_fn(W_state, k[:, sl], v[:, sl]) * GRAD_SCALE
                gn = jnp.maximum(jnp.linalg.norm(g, axis=-1, keepdims=True), EPS)
                g = g * jnp.minimum(MAX_GRAD_NORM / gn, 1.0)
                g = jax.lax.stop_gradient(g)
                xs = (jnp.swapaxes(g, 0, 1), eta[:, sl].T, theta[:, sl].T, alpha[:, sl].T)
                (S_state, W_state), Wtraj = jax.lax.scan(step, (S_state, W_state), xs)
                Wtraj = jnp.swapaxes(Wtraj, 0, 1)
                T = Wtraj.shape[1]
                W1t = Wtraj[..., :D * D].reshape(B, T, D, D)
                W2t = Wtraj[..., D * D:].reshape(B, T, D, D)
                h = jax.nn.silu(jnp.einsum('btd,btod->bto', q[:, sl], W1t))
                outs.append(jnp.einsum('bto,btpo->btp', h, W2t))
            retrieved = jnp.concatenate(outs, axis=1)
            out = retrieved @ Wo.T
            out = out * jax.lax.rsqrt(jnp.mean(out * out, -1, keepdims=True) + EPS) * norm_g
            gate = hidden @ gW.T + gb
            return out * gate
        return _forward(hidden, Wk, Wv, Wq, Wo, ckw, ckb, cvw, cvb, cqw, cqb, mW1, mW2, aW, ab, eW, eb, tW, tb, norm_g, gW, gb)

    def _L0_ffn_ref(inputs, gate_w, w1, w2):
        import jax, jax.numpy as jnp
        import numpy as np
        B, S, D = (4, 512, 256)
        E = 8
        F = 1024
        T = B * S
        CAP = 320
        tokens = inputs.reshape(-1, D)
        logits = tokens @ gate_w
        probs = jax.nn.softmax(logits, axis=-1)
        expert_idx = jnp.argmax(probs, axis=-1)
        mask1 = jax.nn.one_hot(expert_idx, E, dtype=tokens.dtype)
        pos = (jnp.cumsum(mask1, axis=0) - 1.0).astype(jnp.int32)
        sec_mask = mask1[:, :, None] * jax.nn.one_hot(pos, CAP, dtype=tokens.dtype)
        combine_weights = probs[:, :, None] * sec_mask
        expert_input = jnp.einsum('tec,td->ecd', sec_mask, tokens)
        h = jax.nn.relu(jnp.einsum('ecd,edf->ecf', expert_input, w1))
        expert_output = jnp.einsum('ecf,efd->ecd', h, w2)
        out = jnp.einsum('tec,ecd->td', combine_weights, expert_output)
        return out.reshape(inputs.shape)
    x = L0_attn_hidden
    x = x + 0.5 * _L0_ffn_ref(_layernorm(x, axis=-1), L0_ffn_gate_w, L0_ffn_w1, L0_ffn_w2)
    x = x + _L0_attn_ref(_layernorm(x, axis=-1), L0_attn_Wk, L0_attn_Wv, L0_attn_Wq, L0_attn_Wo, L0_attn_ckw, L0_attn_ckb, L0_attn_cvw, L0_attn_cvb, L0_attn_cqw, L0_attn_cqb, L0_attn_mW1, L0_attn_mW2, L0_attn_aW, L0_attn_ab, L0_attn_eW, L0_attn_eb, L0_attn_tW, L0_attn_tb, L0_attn_norm_g, L0_attn_gW, L0_attn_gb)
    x = x + 0.5 * _L0_ffn_ref(_layernorm(x, axis=-1), L0_ffn_gate_w, L0_ffn_w1, L0_ffn_w2)
    return x

_drawn_inputs = setup_inputs


def setup_inputs(seed=0):
    import zlib

    import numpy as np

    out = dict(_drawn_inputs(seed))
    spreads = {'L0_attn_ckb': (0.0, 0.8),
     'L0_attn_cvb': (0.0, 0.8),
     'L0_attn_cqb': (0.0, 0.8),
     'L0_attn_ab': (0.0, 2.0),
     'L0_attn_eb': (0.0, 0.8),
     'L0_attn_tb': (0.0, 0.8),
     'L0_attn_norm_g': (1.0, 0.6),
     'L0_attn_gW': (0.0, 0.8),
     'L0_attn_gb': (1.0, 0.6)}
    factors = {'L0_attn_Wk': 8.0,
     'L0_attn_Wv': 8.0,
     'L0_attn_Wq': 8.0,
     'L0_attn_Wo': 8.0,
     'L0_attn_ckw': 8.0,
     'L0_attn_cvw': 8.0,
     'L0_attn_cqw': 8.0,
     'L0_attn_mW1': 8.0,
     'L0_attn_mW2': 8.0,
     'L0_attn_aW': 8.0,
     'L0_attn_eW': 8.0,
     'L0_attn_tW': 8.0}
    for name, (base, spread) in spreads.items():
        noise = np.random.default_rng([zlib.crc32(name.encode()), seed]).standard_normal(out[name].shape)
        drawn = base * np.exp(spread * noise) if base else spread * noise
        out[name] = jnp.asarray(drawn.astype(out[name].dtype))
    for name, factor in factors.items():
        out[name] = (out[name] * factor).astype(out[name].dtype)
    return out
```

```python
from contextlib import ExitStack

import concourse.bass as bass
from concourse import mybir

F32 = mybir.dt.float32
BF16 = mybir.dt.bfloat16
I32 = mybir.dt.int32
ALU = mybir.AluOpType
ACT = mybir.ActivationFunctionType
AX = mybir.AxisListType

P = 128
B, S, H = 8, 1024, 256
D = 64
CH = 128
NCH = S // CH
TOK = B * S
NT = TOK // P
KH = H // P
E, F, CAP = 8, 1024, 320
SLOTS = E * CAP
ST = SLOTS // P
PAIRS = E // 2
PT = ST // PAIRS
KF = F // P
LN_EPS = 1e-5
EPS = 1e-6
BIG = 16384.0
TAPS = 4
BW = B * CH


class Semaphores(dict):

    def __init__(self, nc, ctx, prefix):
        self.nc, self.ctx, self.prefix = nc, ctx, prefix

    def __missing__(self, name):
        self[name] = self.ctx.enter_context(self.nc.semaphore(self.prefix + name))
        return self[name]


def bc(ap, shape):
    return ap.broadcast_to(shape)


def route(nc, sems, ctx, ps, t, name):

    def sem(n):
        return sems[n]

    def sb(n, shape, dt):
        return ctx.enter_context(nc.sbuf_tensor(f"{name}_{n}", shape, dt))

    logits, ones_row = t["logits"], t["ones_row"]
    top = sb("top", [P, NT], F32)
    hit = sb("hit", [P, NT, E], F32)
    rank = sb("rank", [P, NT], F32)
    onehot = sb("onehot", [P, NT, E], BF16)
    total = sb("total", [P, NT, E], F32)
    running = sb("running", [P, NT, E], F32)
    place = sb("place", [P, NT, E], F32)
    pos = sb("pos", [P, NT], F32)
    over = sb("over", [P, NT], F32)
    slot = sb("slot", [P, NT], F32)
    slot_i = sb("slot_i", [P, NT], I32)
    row_i = sb("row_i", [P, NT], I32)
    col_i = sb("col_i", [P, NT], I32)
    row = sb("row", [P, NT], F32)
    col = sb("col", [P, NT], F32)
    row_hot = sb("row_hot", [P, NT, P], BF16)
    col_hot = sb("col_hot", [P, NT, 3, ST], BF16)
    found = sb("found", [P, 3, ST], F32)
    token = sb("token", [P, ST], F32)
    empty = sb("empty", [P, ST], F32)
    sc_f = sb("sc_f", [P, ST], F32)
    cum_ps = ps[:, 0, :].rearrange("p (n e) -> p n e", e=E)
    tot_ps = ps[:, 1, :].rearrange("p (n e) -> p n e", e=E)
    tab_ps = ps[:, 2, 0:3 * ST]
    QUARTER = NT // 4

    chain = sem("dve_done")
    onehot_ready = sem("onehot_ready")
    counts_ready = sem("counts_ready")
    col_hot_ready = sem("col_hot_ready")
    row_hot_ready = sem("row_hot_ready")
    table_ready = sem("table_ready")
    with nc.Block() as block:

        @block.vector
        def _(dve):
            v = nc.vector
            v.tensor_reduce(top[:], logits[:], AX.X, ALU.max).then_inc(chain, 1)
            dve.wait_ge(chain, 1)
            v.tensor_tensor(hit[:], logits[:], bc(top[:].unsqueeze(2), [P, NT, E]), ALU.is_equal).then_inc(chain, 1)
            dve.wait_ge(chain, 2)
            v.tensor_tensor(hit[:], hit[:], bc(t["rank_of_expert"][:].unsqueeze(1), [P, NT, E]),
                            ALU.mult).then_inc(chain, 1)
            dve.wait_ge(chain, 3)
            v.tensor_reduce(rank[:], hit[:], AX.X, ALU.max).then_inc(chain, 1)
            dve.wait_ge(chain, 4)
            v.tensor_tensor(onehot[:], hit[:], bc(rank[:].unsqueeze(2), [P, NT, E]),
                            ALU.is_equal).then_inc(onehot_ready, 1)
            dve.wait_ge(counts_ready, 1)
            v.tensor_copy(total[:], tot_ps).then_inc(chain, 1)
            dve.wait_ge(chain, 5)
            for e in range(E):
                last = v.tensor_tensor_scan(running[:, :, e], ones_row[:, 0:NT], total[:, :, e], 0.0,
                                            ALU.mult, ALU.add)
            last.then_inc(chain, 1)
            dve.wait_ge(chain, 6)
            v.tensor_tensor(running[:], running[:], total[:], ALU.subtract).then_inc(chain, 1)
            dve.wait_ge(chain, 7)
            v.tensor_tensor(place[:], cum_ps, running[:], ALU.add).then_inc(chain, 1)
            dve.wait_ge(chain, 8)
            v.tensor_tensor(place[:], place[:], onehot[:], ALU.mult).then_inc(chain, 1)
            dve.wait_ge(chain, 9)
            v.tensor_reduce(pos[:], place[:], AX.X, ALU.add).then_inc(chain, 1)
            dve.wait_ge(chain, 10)
            v.tensor_scalar(over[:], pos[:], float(CAP), BIG, ALU.is_gt, ALU.mult).then_inc(chain, 1)
            v.tensor_scalar(slot[:], rank[:], -float(CAP), float(E * CAP) - 1.0, ALU.mult, ALU.add).then_inc(chain, 1)
            dve.wait_ge(chain, 12)
            v.tensor_tensor(slot[:], slot[:], pos[:], ALU.add).then_inc(chain, 1)
            dve.wait_ge(chain, 13)
            v.tensor_tensor(slot_i[:], slot[:], over[:], ALU.add).then_inc(chain, 1)
            dve.wait_ge(chain, 14)
            v.tensor_scalar(row_i[:], slot_i[:], P - 1, None, ALU.bitwise_and).then_inc(chain, 1)
            v.tensor_scalar(col_i[:], slot_i[:], 7, None, ALU.logical_shift_right).then_inc(chain, 1)
            dve.wait_ge(chain, 16)
            v.tensor_copy(row[:], row_i[:]).then_inc(chain, 1)
            v.tensor_copy(col[:], col_i[:]).then_inc(chain, 1)
            dve.wait_ge(chain, 18)
            v.tensor_tensor(col_hot[:, :, 0, :], bc(col[:].unsqueeze(2), [P, NT, ST]),
                            bc(t["iota"][:, 0:ST].unsqueeze(1), [P, NT, ST]), ALU.is_equal).then_inc(chain, 1)
            dve.wait_ge(chain, 19)
            v.tensor_tensor(col_hot[:, :, 1, :], col_hot[:, :, 0, :],
                            bc(t["iota"][:, 0:NT].unsqueeze(2), [P, NT, ST]), ALU.mult)
            v.tensor_scalar(col_hot[:, :, 2, :], col_hot[:, :, 0, :], t["partition"][:, 0:1], None,
                            ALU.mult).then_inc(col_hot_ready, 1)
            for i in range(4):
                n = slice(i * QUARTER, (i + 1) * QUARTER)
                v.tensor_tensor(row_hot[:, n, :], bc(row[:, n].unsqueeze(2), [P, QUARTER, P]),
                                bc(t["iota"][:].unsqueeze(1), [P, QUARTER, P]),
                                ALU.is_equal).then_inc(row_hot_ready, 1)
            dve.wait_ge(table_ready, 1)
            v.tensor_copy(found[:], tab_ps.rearrange("p (a s) -> p a s", a=3)).then_inc(chain, 1)
            dve.wait_ge(chain, 20)
            v.scalar_tensor_tensor(token[:], found[:, 1, :], float(P), found[:, 2, :], ALU.mult,
                                   ALU.add).then_inc(chain, 1)
            v.tensor_scalar(empty[:], found[:, 0, :], -BIG, BIG, ALU.mult, ALU.add).then_inc(chain, 1)
            dve.wait_ge(chain, 22)
            v.tensor_copy(t["gather_index"][:], token[:]).then_inc(chain, 1)
            v.tensor_tensor(t["scatter_index"][:], token[:], empty[:], ALU.add).then_inc(chain, 1)

        @block.tensor
        def _(pe):
            pe.wait_ge(onehot_ready, 1)
            nc.tensor.matmul(ps[:, 0, :], t["upper"][:], onehot[:].rearrange("p n e -> p (n e)"), start=True, stop=True)
            nc.tensor.matmul(ps[:, 1, :], t["ones_bf"][:], onehot[:].rearrange("p n e -> p (n e)"), start=True,
                             stop=True).then_inc(counts_ready, 1)
            pe.wait_ge(col_hot_ready, 1)
            for n in range(NT):
                if n % QUARTER == 0:
                    pe.wait_ge(row_hot_ready, n // QUARTER + 1)
                last = nc.tensor.matmul(tab_ps, row_hot[:, n, :], col_hot[:, n, :, :].rearrange("p a s -> p (a s)"),
                                        start=(n == 0), stop=(n == NT - 1))
            last.then_inc(table_ready, 1)


def experts(nc, sems, ctx, ps, t, name, rows_dram, result_dram):

    def sem(n):
        return sems[n]

    def sb(n, shape, dt=F32):
        return ctx.enter_context(nc.sbuf_tensor(f"{name}_{n}", shape, dt))

    rows = sb("rows", [P, ST, H])
    stats = sb("stats", [P, PT, 6])
    moments = sb("moments", [P, PT, 2])
    rstd = sb("rstd", [P, PT])
    var_eps = sb("var_eps", [P, PT])
    spare = sb("spare", [P, 1])
    normed = sb("normed", [P, PT, H])
    normedT = sb("normedT", [P, KH, PT * P])
    lg = sb("lg", [P, PT, E])
    lmax = sb("lmax", [P, PT])
    ex = sb("ex", [P, PT, E])
    den = sb("den", [P, PT])
    prob = sb("prob", [P, PT])
    w1 = [sb(f"w1_{i}", [P, KH, F]) for i in range(2)]
    w2 = [sb(f"w2_{i}", [P, KF, H]) for i in range(2)]
    hidden = [sb(f"hidden{i}", [P, KF, CAP]) for i in range(2)]

    gathered = sem("pool_dma_gathered_" + name)
    w1_loaded = [sem(f"w1_loaded{i}") for i in range(2)]
    w2_loaded = [sem(f"w2_loaded{i}") for i in range(2)]
    stats_done = sem("stats_done")
    moments_done = sem("moments_done")
    rstd_done = sem("rstd_done")
    var_done = sem("var_done")
    normed_ready = sem("normed_ready")
    turned = sem("turned")
    turned_copied = sem("turned_copied")
    logits_done = sem("logits_done")
    lg_copied = sem("lg_copied")
    lmax_done = sem("lmax_done")
    lg_shifted = sem("lg_shifted")
    exp_done = sem("exp_done")
    den_done = sem("den_done")
    inv_done = sem("inv_done")
    prob_ready = sem("prob_ready")
    up_done = [sem(f"up_done{i}") for i in range(2)]
    relu_done = sem("relu_done")
    y_done = [sem(f"y_done{i}") for i in range(2)]
    y_read = sem("y_read")
    scattered = sem("pool_dma_scattered_" + name)

    YS = [[(0, 0, P, 0), (1, 0, P, P), (2, 0, D, 2 * P)], [(2, D, D, 0), (3, 0, P, D), (4, 0, P, D + P)]]
    NY = len(YS[0])

    with nc.Block() as block:

        @block.sync
        def _(sp):
            def load_up(g, i):
                sp.dma_start(w1[i][:], t["w1"][bass.ds(g * 2 + i, 1), :, :].rearrange("o (k p) f -> p (o k) f", p=P)
                             ).then_inc(w1_loaded[i], 16)

            def load_down(g, i):
                sp.dma_start(w2[i][:], t["w2"][bass.ds(g * 2 + i, 1), :, :].rearrange("o (k p) h -> p (o k) h", p=P)
                             ).then_inc(w2_loaded[i], 16)

            for i in range(2):
                load_up(0, i)
                load_down(0, i)
            with sp.Fori(1, PAIRS) as g:
                for i in range(2):
                    sp.wait_ge(up_done[i], g * KF)
                    load_up(g, i)
                for i in range(2):
                    sp.wait_ge(y_done[i], g * NY)
                    load_down(g, i)

        @block.gpsimd
        def _(pool):
            def gather(g):
                for j in range(g * PT, (g + 1) * PT):
                    nc.gpsimd.indirect_dma_start(rows[:, j, :], None, rows_dram,
                                                 bass.IndirectOffsetOnAxis(t["gather_index"][:, j:j + 1], 0),
                                                 bounds_check=TOK - 1, oob_is_err=False).then_inc(gathered, 16)

            def power(g):
                pool.wait_ge(var_done, g + 1)
                nc.gpsimd.tensor_tensor(rstd[:], var_eps[:], t["minus_half"][:, 0:PT], ALU.pow).then_inc(rstd_done, 1)

            def scatter(g):
                for i in range(PT):
                    j = g * PT + i
                    pool.wait_ge(y_read, 2 * NY * g + (i + 1 if i < 2 else i + 2))
                    nc.gpsimd.indirect_dma_start(result_dram,
                                                 bass.IndirectOffsetOnAxis(t["scatter_index"][:, j:j + 1], 0),
                                                 rows[:, j, :], None,
                                                 bounds_check=TOK - 1, oob_is_err=False).then_inc(scattered, 16)

            for g in range(PAIRS):
                gather(g)
                if g == 1:
                    power(0)
                pool.wait_ge(gathered, 16 * PT * (g + 1))
            for g in range(PAIRS):
                if g + 1 < PAIRS:
                    power(g + 1)
                scatter(g)
            pool.wait_ge(scattered, 16 * ST)

        @block.vector
        def _(dve):
            v = nc.vector

            def norm(g):
                dve.wait_ge(gathered, 16 * PT * (g + 1))
                for i in range(PT):
                    v.bn_stats(stats[:, i, :], rows[:, bass.ds(g * PT + i, 1), :].rearrange("p o h -> p (o h)")
                               ).then_inc(stats_done, 1)
                dve.wait_ge(stats_done, PT * (g + 1))
                v.memset(spare[:], 0.0)
                for i in range(PT):
                    v.bn_aggr(moments[:, i, :], stats[:, i, :]).then_inc(moments_done, 1)
                dve.wait_ge(moments_done, PT * (g + 1))
                v.tensor_scalar(var_eps[:], moments[:, :, 1], LN_EPS, None, ALU.add).then_inc(var_done, 1)
                dve.wait_ge(rstd_done, g + 1)
                for i in range(PT):
                    v.tensor_scalar(normed[:, i, :], rows[:, bass.ds(g * PT + i, 1), :].rearrange("p o h -> p (o h)"),
                                    moments[:, i, 0:1], rstd[:, i:i + 1], ALU.subtract,
                                    ALU.mult).then_inc(normed_ready, 1)

            def probability(g):
                dve.wait_ge(logits_done, g + 1)
                v.tensor_copy(lg[:], ps[:, 5, 0:PT * E].rearrange("p (i e) -> p i e", e=E)).then_inc(lg_copied, 1)
                dve.wait_ge(lg_copied, g + 1)
                v.tensor_reduce(lmax[:], lg[:], AX.X, ALU.max).then_inc(lmax_done, 1)
                dve.wait_ge(lmax_done, g + 1)
                v.tensor_tensor(lg[:], lg[:], bc(lmax[:].unsqueeze(2), [P, PT, E]),
                                ALU.subtract).then_inc(lg_shifted, 1)
                dve.wait_ge(exp_done, g + 1)
                v.tensor_reduce(den[:], ex[:], AX.X, ALU.add).then_inc(den_done, 1)
                dve.wait_ge(den_done, g + 1)
                v.reciprocal(prob[:], den[:]).then_inc(inv_done, 1)
                dve.wait_ge(inv_done, g + 1)
                v.tensor_scalar(prob[:], prob[:], 0.5, None, ALU.mult).then_inc(prob_ready, 1)
                dve.wait_ge(prob_ready, g + 1)

            def finish(g):
                for i in range(2):
                    for j, (tile, p0, n, _) in enumerate(YS[i]):
                        dve.wait_ge(y_done[i], NY * g + j + 1)
                        r = rows[p0:p0 + n, bass.ds(g * PT + tile, 1), :].rearrange("p o h -> p (o h)")
                        v.scalar_tensor_tensor(r, ps[p0:p0 + n, 6 + (NY * i + j) % 2, 0:H],
                                               prob[p0:p0 + n, tile:tile + 1], r, ALU.mult,
                                               ALU.add).then_inc(y_read, 1)

            norm(0)
            with dve.Fori(0, PAIRS - 1) as g:
                probability(g)
                dve.wait_ge(turned, PT * (g + 1))
                norm(g + 1)
                finish(g)
            probability(PAIRS - 1)
            finish(PAIRS - 1)

        @block.scalar
        def _(act):
            s = nc.scalar

            def turn(g, first):
                if not first:
                    act.wait_ge(up_done[1], KF * g)
                for i in range(PT):
                    act.wait_ge(turned, PT * g + i + 1)
                    s.copy(normedT[:, :, i * P:(i + 1) * P],
                           ps[:, i % 2, 0:H].rearrange("p (k c) -> p k c", k=KH)).then_inc(turned_copied, 1)
                act.wait_ge(lg_shifted, g + 1)
                s.activation(ex[:], lg[:], ACT.Exp).then_inc(exp_done, 1)
                for i in range(2):
                    if not first:
                        act.wait_ge(y_done[i], NY * g)
                    for f in range(KF):
                        act.wait_ge(up_done[i], KF * g + f + 1)
                        s.activation(hidden[i][:, f, :], ps[:, 2 + (KF * i + f) % 3, 0:CAP], ACT.Relu).then_inc(relu_done, 1)

            turn(0, True)
            with act.Fori(1, PAIRS) as g:
                turn(g, False)

        @block.tensor
        def _(pe):
            def logits(g, i):
                pe.wait_ge(turned_copied, PT * g + i + 1)
                for k in range(KH):
                    last = nc.tensor.matmul(ps[:, 5, i * E:(i + 1) * E], normedT[:, k, i * P:(i + 1) * P],
                                            t["gate_w"][:, k, :], start=(k == 0), stop=(k == KH - 1))
                return last

            def turn(g, first):
                for i in range(PT):
                    pe.wait_ge(normed_ready, PT * g + i + 1)
                    if not first or i >= 2:
                        pe.wait_ge(turned_copied, PT * g + i - 1)
                    if i == 0 and not first:
                        pe.wait_ge(lg_copied, g)
                    for k in range(KH):
                        last = nc.tensor.transpose(ps[:, i % 2, k * P:(k + 1) * P], normed[:, i, k * P:(k + 1) * P],
                                                   t["ident"][:])
                    last.then_inc(turned, 1)
                    if i:
                        logits(g, i - 1)
                logits(g, PT - 1).then_inc(logits_done, 1)
                for i in range(2):
                    pe.wait_ge(w1_loaded[i], 16 * g + 16)
                    for f in range(KF):
                        if KF * i + f >= 3:
                            pe.wait_ge(relu_done, 2 * KF * g + KF * i + f - 2)
                        for k in range(KH):
                            last = nc.tensor.matmul(ps[:, 2 + (KF * i + f) % 3, 0:CAP], w1[i][:, k, f * P:(f + 1) * P],
                                                    normedT[:, k, i * CAP:(i + 1) * CAP], start=(k == 0),
                                                    stop=(k == KH - 1))
                        last.then_inc(up_done[i], 1)
                for i in range(2):
                    pe.wait_ge(w2_loaded[i], 16 * g + 16)
                    pe.wait_ge(relu_done, 2 * KF * g + KF * (i + 1))
                    for j, (_, p0, n, c0) in enumerate(YS[i]):
                        if not first or NY * i + j >= 2:
                            pe.wait_ge(y_read, 2 * NY * g + NY * i + j - 1)
                        for f in range(KF):
                            last = nc.tensor.matmul(ps[p0:p0 + n, 6 + (NY * i + j) % 2, 0:H],
                                                    hidden[i][:, f, c0:c0 + n], w2[i][:, f, :],
                                                    start=(f == 0), stop=(f == KF - 1))
                        last.then_inc(y_done[i], 1)

            turn(0, True)
            with pe.Fori(1, PAIRS) as g:
                turn(g, False)


def first_logits(nc, sems, ctx, ps, t, x_dram, xT_dram, x1_dram):

    def sem(n):
        return sems[n]

    GROUP = 1024
    PER = GROUP // P
    xt = [ctx.enter_context(nc.sbuf_tensor(f"xt{i}", [P, KH, GROUP], F32)) for i in range(2)]
    mean = ctx.enter_context(nc.sbuf_tensor("gate_mean", [P, E], F32))
    stage = ctx.enter_context(nc.sbuf_tensor("stage", [P, 2, P], F32))
    consts = sem("consts")
    x_copied = sem("x_copied")
    loaded = [sem(f"loaded{i}") for i in range(2)]
    mean_done = sem("mean_done")
    mean_copied = sem("mean_copied")
    centred = sem("centred")
    made = sem("made")
    read = sem("read")
    cast = sem("cast")
    loads = [(t["ident"][:], t["d_ident"]), (t["iota"][:], t["d_iota"]), (t["partition"][:], t["d_partition"]),
             (t["rank_of_expert"][:], t["d_rank"]), (t["gate_w"][:], t["d_gate_w"].rearrange("(k p) e -> p k e", p=P)),
             (stage[:, 0, :], t["d_upper"]), (t["mean_w"][:], t["d_mean_w"]), (stage[:, 1, :], t["d_ones"])]

    with nc.Block() as block:

        @block.sync
        def _(sp):
            def load(n, i):
                sp.dma_start(xt[i][:], xT_dram[:, bass.ds(n * GROUP, GROUP)].rearrange("(k p) n -> p k n", p=P)
                             ).then_inc(loaded[i], 16)

            for dst, src in loads:
                sp.dma_start(dst, src).then_inc(consts, 16)
            load(0, 0)
            load(1, 1)
            with sp.Fori(1, TOK // GROUP // 2) as n:
                for i in range(2):
                    sp.wait_ge(made, n * 2 + i - 1)
                    load(n * 2 + i, i)

        @block.gpsimd
        def _(pool):
            pool.dma_start(x1_dram.rearrange("(a b) h -> a (b h)", a=P), x_dram.rearrange("(a b) h -> a (b h)", a=P)
                           ).then_inc(x_copied, 16)
            pool.wait_ge(x_copied, 16)

        @block.vector
        def _(dve):
            v = nc.vector
            dve.wait_ge(consts, 16 * len(loads))
            v.tensor_copy(t["upper"][:], stage[:, 0, :]).then_inc(cast, 1)
            v.tensor_copy(t["ones_bf"][:], stage[:, 1, :]).then_inc(cast, 1)
            v.memset(t["ones_row"][:], 1.0).then_inc(cast, 1)
            v.memset(t["minus_half"][:], -0.5).then_inc(cast, 1)
            dve.wait_ge(mean_done, 1)
            v.tensor_copy(mean[:], ps[:, 2, 0:E]).then_inc(mean_copied, 1)
            dve.wait_ge(mean_copied, 1)
            v.tensor_tensor(t["gate_c"][:], t["gate_w"][:], bc(mean[:].unsqueeze(1), [P, KH, E]),
                            ALU.subtract).then_inc(centred, 1)
            with dve.Fori(0, TOK // GROUP // 2) as n:
                for i in range(2):
                    dve.wait_ge(made, n * 2 + i + 1)
                    v.tensor_copy(t["logits"][:, bass.ds(n * (2 * PER) + i * PER, PER), :],
                                  ps[:, i, 0:PER * E].rearrange("p (n e) -> p n e", e=E)).then_inc(read, 1)

        @block.tensor
        def _(pe):
            pe.wait_ge(consts, 16 * len(loads))
            for k in range(KH):
                last = nc.tensor.matmul(ps[:, 2, 0:E], t["mean_w"][:], t["gate_w"][:, k, :], start=(k == 0),
                                        stop=(k == KH - 1))
            last.then_inc(mean_done, 1)
            pe.wait_ge(centred, 1)

            def group(n, i, first):
                pe.wait_ge(loaded[i], n * 16 + 16)
                if not first:
                    pe.wait_ge(read, n * 2 + i - 1)
                for j in range(PER):
                    for k in range(KH):
                        last = nc.tensor.matmul(ps[:, i, j * E:(j + 1) * E], xt[i][:, k, j * P:(j + 1) * P],
                                                t["gate_c"][:, k, :], start=(k == 0), stop=(k == KH - 1))
                last.then_inc(made, 1)

            for i in range(2):
                group(0, i, True)
            with pe.Fori(1, TOK // GROUP // 2) as n:
                for i in range(2):
                    group(n, i, False)


def memory_attention(nc, sems, ctx, ps, t, x_dram, out_dram, d):

    def sem(n):
        return sems[n]

    def sb(n, shape, dt=F32):
        return ctx.enter_context(nc.sbuf_tensor(f"att_{n}", shape, dt))

    def two(n, shape):
        return [sb(f"{n}{i}", shape) for i in range(2)]

    HALF = B // 2
    HW = HALF * CH
    w_kv, w_qq, w_ae = sb("w_kv", [P, KH, P]), sb("w_qq", [P, KH, P]), sb("w_ae", [P, KH, P])
    w_gt = sb("w_gt", [P, KH, H + D])
    w_o = sb("w_o", [D, H])
    conv_kv, conv_q = sb("conv_kv", [P, TAPS + 1]), sb("conv_q", [P, TAPS + 1])
    b_ae, b_t, b_g, norm_g = sb("b_ae", [P, 1]), sb("b_t", [P, D]), sb("b_g", [P, H]), sb("norm_g", [P, H])
    mean_a, mean_e = sb("mean_a", [P, P]), sb("mean_e", [P, P])
    fold, fold_low = sb("fold", [P, D]), sb("fold_low", [P, D])
    x_norm = sb("x_norm", [P, B, H])
    stats, moments, var_eps, rstd = sb("stats", [P, B, 6]), sb("moments", [P, B, 2]), sb("var_eps", [P, B]), sb("rstd", [P, B])
    xT = sb("xT", [P, KH, BW])
    raw_kv, raw_q = sb("raw_kv", [P, B, TAPS - 1 + CH]), sb("raw_q", [P, B, TAPS - 1 + CH])
    sig_ae = sb("sig_ae", [P, BW])
    keep, eta = sb("keep", [P, B, CH]), sb("eta", [P, B, CH])
    mom = sb("mom", [P, B, CH])
    carry = sb("carry", [P, B, CH])
    theta_pre, theta_log = sb("theta_pre", [P, B, D]), sb("theta_log", [P, B, D])
    theta_sum = sb("theta_sum", [P, B])
    k_sq = sb("k_sq", [P, B, D])
    zeros = sb("zeros", [P, CH])
    ab_start = sb("ab_start", [P, 1])
    KV, Q, QAB = two("KV", [P, B, CH]), two("Q", [P, B, CH]), two("QAB", [P, B, CH])
    P1, M, AB = two("P1", [P, B, CH]), two("M", [P, B, CH]), two("AB", [P, B, CH])
    spare = sb("spare", [P, 1])
    KM, MIX = two("KM", [P, B, 2, D]), two("MIX", [P, B, P])
    GATE, ENDS = two("GATE", [P, B, H]), two("ENDS", [P, B, 2])
    THETA, KNORM = two("THETA", [P, B]), two("KNORM", [P, B])
    x_res = sb("x_res", [P, B, H])
    state, read_w = sb("state", [P, B, 3 * D]), sb("read_w", [P, B, P])
    sig_h, hid, slope = sb("sig_h", [P, B, D]), sb("hid", [P, B, D]), sb("slope", [P, B, D])
    hid_m = sb("hid_m", [P, B, 2, D])
    squares = sb("squares", [P, 3, B, D])
    dpre, grad_w1, grad_w2 = sb("dpre", [P, B, D]), sb("grad_w1", [P, B, 2, D]), sb("grad_w2", [P, B, D])
    nsum = sb("nsum", [P, 3, B])
    n1, n2, n3, n4, n5, factor = (sb(f"n{i}", [P, B]) for i in range(6))
    hid2, hid2_ab, P2 = (sb(n, [P, B, CH]) for n in ("hid2", "hid2_ab", "P2"))
    sig_h2 = hid2
    retrieved = sb("retrieved", [D, B, CH])
    o_sq = squares[:].rearrange("p a b n -> p (a b n)")[:, 0:HALF * H].rearrange("p (b n) -> p b n", n=H)
    o_sum, o_mean, o_rs = sb("o_sum", [P, B]), sb("o_mean", [P, B]), sb("o_rs", [P, B])
    x2T = xT

    consts, folded, started = sem("consts"), sem("folded"), sem("started")
    x_loaded = sem("x_loaded")
    stats_done, moments_done, rstd_done, x_normed = sem("stats_done"), sem("moments_done"), sem("rstd_done"), sem("x_normed")
    var_done, n_clipped, powered = sem("var_done"), sem("n_clipped"), sem("powered")
    x_turned, x_turned_copied = sem("x_turned"), sem("x_turned_copied")
    kv_made, kv_copied, q_made, q_copied = sem("kv_made"), sem("kv_copied"), sem("q_made"), sem("q_copied")
    kv_conv, q_conv, halo_kv, halo_q = sem("kv_conv"), sem("q_conv"), sem("halo_kv"), sem("halo_q")
    ae_made, ae_sig, rates_made, keep_ready, eta_ready = (sem(n) for n in ("ae_made", "ae_sig", "rates_made", "keep_ready", "eta_ready"))
    mom_ready, carry_ready, m_ready, ab_ready, ends_ready = (sem(n) for n in ("mom_ready", "carry_ready", "m_ready", "ab_ready", "ends_ready"))
    qab_ready, mix_ready = sem("qab_ready"), sem("mix_ready")
    gate_made, gate_read = sem("gate_made"), sem("gate_read")
    t_abs, t_exp, t_ln, t_soft, t_sum, theta_ready = (sem(n) for n in ("t_abs", "t_exp", "t_ln", "t_soft", "t_sum", "theta_ready"))
    k_turned, k_squared, km_ready, knorm_ready = (sem(n) for n in ("k_turned", "k_squared", "km_ready", "knorm_ready"))
    qk_made, p1_ready = sem("qk_made"), sem("p1_ready")
    pre_made, sig_ready, hid_ready, tmp_ready, slope_ready = (sem(n) for n in ("pre_made", "sig_ready", "hid_ready", "tmp_ready", "slope_ready"))
    hid_turned, hid_turned_copied, hid_m_ready = sem("hid_turned"), sem("hid_turned_copied"), sem("hid_m_ready")
    res_made, dpre_ready, squared, nsum_ready, small = (sem(n) for n in ("res_made", "dpre_ready", "squared", "nsum_ready", "small"))
    grad_w1_ready, grad_w2_ready = sem("grad_w1_ready"), sem("grad_w2_ready")
    pre2_made, sig2_ready, hid2_ready, hid2_ab_ready = (sem(n) for n in ("pre2_made", "sig2_ready", "hid2_ready", "hid2_ab_ready"))
    hh_made, p2_ready, ret_made, ret_copied = (sem(n) for n in ("hh_made", "p2_ready", "ret_made", "ret_copied"))
    state_made, state_copied, state_turned, w2_copied, gram_made, gram_copied = (
        sem(n) for n in ("state_made", "state_copied", "state_turned", "w2_copied", "gram_made", "gram_copied"))
    o_made, o_squared, o_meaned, o_rs_ready, gated_ready = (sem(n) for n in ("o_made", "o_squared", "o_meaned", "o_rs_ready", "gated_ready"))
    res_loaded, x2_ready, x2_stored, x2_turned, x2_turned_copied = (
        sem(n) for n in ("res_loaded", "x2_ready", "x2_stored", "x2_turned", "x2_turned_copied"))
    lg_made, lg_read = sem("lg_made"), sem("lg_read")

    x_v = x_dram.rearrange("(b c t) h -> c t b h", b=B, t=CH)
    out_v = out_dram.rearrange("(b c t) h -> c t b h", b=B, t=CH)

    def kmajor(a):
        return a.rearrange("(k p) n -> p k n", p=P)

    def step_of(a, c):
        return a[bass.ds(c, 1), :, :, :].rearrange("o t b h -> t (o b) h")

    loads = [(w_kv[:], kmajor(d["w_kv"])), (w_qq[:], kmajor(d["w_qq"])), (w_ae[:], kmajor(d["w_ae"])),
             (w_gt[:], kmajor(d["w_gt"])), (w_o[:], d["w_o"]), (conv_kv[:], d["conv_kv"]), (conv_q[:], d["conv_q"]),
             (b_ae[:], d["b_ae"]), (b_t[:], d["b_t"]), (b_g[:], d["b_g"]), (norm_g[:], d["norm_g"]),
             (mean_a[:], d["mean_a"]), (mean_e[:], d["mean_e"]), (fold[:], d["fold"]), (fold_low[:], d["fold_low"]),
             (state[0:D, :, 0:D], d["w1T"]), (state[0:D, :, D:2 * D], d["w1T"]), (state[0:D, :, 2 * D:3 * D], d["w2T"]),
             (read_w[0:D, :, 0:D], d["w2T"]), (read_w[D:P, :, 0:D], d["minus_i"]), (ab_start[:], d["ab_start"])]

    A, BB, C, DD = (ps[:, 2 * i:2 * i + 2, :] for i in range(4))

    def wide(pair):
        return pair.rearrange("p a (b n) -> p (a b) n", n=CH)

    with nc.Block() as block:

        @block.sync
        def _(sp):
            def load_x(c):
                sp.dma_start(x_norm[:], step_of(x_v, c)).then_inc(x_loaded, 16)

            def load_res(c):
                sp.dma_start(x_res[:], step_of(x_v, c)).then_inc(res_loaded, 16)

            def store(c):
                sp.wait_ge(x2_ready, 2 * c + 2)
                sp.dma_start(step_of(out_v, c), x_res[:]).then_inc(x2_stored, 16)

            load_x(0)
            for dst, src in loads:
                sp.dma_start(dst, src).then_inc(consts, 16)
            load_res(0)
            sp.wait_ge(x_turned, 2)
            load_x(1)
            with sp.Fori(0, NCH - 2) as c:
                sp.wait_ge(x_turned, 2 * c + 4)
                load_x(c + 2)
                store(c)
                sp.wait_ge(x2_stored, 16 * c + 16)
                sp.wait_ge(x2_turned, 2 * c + 2)
                load_res(c + 1)
            store(NCH - 2)
            sp.wait_ge(x2_stored, 16 * (NCH - 1))
            sp.wait_ge(x2_turned, 2 * (NCH - 1))
            load_res(NCH - 1)
            store(NCH - 1)
            sp.wait_ge(x2_stored, 16 * NCH)

        @block.gpsimd
        def _(pool):
            g = nc.gpsimd

            def prep(c, par, first):
                pool.wait_ge(ab_ready, c + 1)
                pool.wait_ge(q_conv, TAPS * c + TAPS)
                if not first:
                    pool.wait_ge(state_made, c - 1)
                g.tensor_tensor(QAB[par][:], Q[par][:], AB[par][:], ALU.mult).then_inc(qab_ready, 1)
                g.tensor_tensor(MIX[par][:, :, 0:D], bc(fold[:].unsqueeze(1), [P, B, D]),
                                bc(AB[par][:, :, CH - 1:CH], [P, B, D]), ALU.mult).then_inc(mix_ready, 1)
                g.tensor_tensor(MIX[par][:, :, D:P], bc(fold_low[:].unsqueeze(1), [P, B, D]),
                                bc(carry[:, :, CH - 1:CH], [P, B, D]), ALU.mult).then_inc(mix_ready, 1)

            def hidden(c, par, first):
                pool.wait_ge(hid_ready, c + 1)
                if not first:
                    pool.wait_ge(state_made, c)
                g.tensor_tensor(hid_m[:], bc(hid[:].unsqueeze(2), [P, B, 2, D]),
                                bc(ENDS[par][:].unsqueeze(3), [P, B, 2, D]), ALU.mult).then_inc(hid_m_ready, 1)

            def norm(c):
                pool.wait_ge(var_done, c + 1)
                g.tensor_tensor(rstd[:], var_eps[:], t["minus_half"][:, 0:B], ALU.pow).then_inc(rstd_done, 1)

            def gradient_norm(c):
                pool.wait_ge(n_clipped, c + 1)
                g.tensor_tensor(n5[:], n4[:], t["minus_half"][:, 0:B], ALU.pow).then_inc(powered, 1)

            def residual(c, par):
                pool.wait_ge(res_loaded, 16 * c + 16)
                for h in range(2):
                    n = slice(h * HALF, (h + 1) * HALF)
                    pool.wait_ge(o_meaned, 2 * c + h + 1)
                    g.tensor_tensor(o_rs[:, n], o_mean[:, n], t["minus_half"][:, n], ALU.pow).then_inc(o_rs_ready, 1)
                    pool.wait_ge(gated_ready, 2 * c + h + 1)
                    g.tensor_tensor(x_res[:, n, :], x_res[:, n, :], GATE[par][:, n, :], ALU.add).then_inc(x2_ready, 1)

            def step(c, par, first, last, norm_too=True):
                pool.wait_ge(ends_ready, c + 1)
                hidden(c, par, first)
                gradient_norm(c)
                if not last:
                    prep(c + 1, 1 - par, first)
                if norm_too:
                    norm(c + 2)
                residual(c, par)

            norm(0)
            prep(0, 0, True)
            norm(1)
            step(0, 0, True, False)
            with pool.Fori(0, NCH // 2 - 2) as i:
                step(i * 2 + 1, 1, False, False)
                step(i * 2 + 2, 0, False, False)
            step(NCH - 3, 1, False, False)
            step(NCH - 2, 0, False, False, norm_too=False)
            step(NCH - 1, 1, False, True, norm_too=False)

        @block.vector
        def _(dve):
            v = nc.vector

            def start():
                dve.wait_ge(consts, 16 * len(loads))
                v.memset(zeros[:], 0.0).then_inc(folded, 1)
                v.memset(raw_kv[:, :, 0:TAPS - 1], 0.0).then_inc(halo_kv, 1)
                v.memset(raw_q[:, :, 0:TAPS - 1], 0.0).then_inc(halo_q, 1)
                v.memset(carry[0:D, :, :], 0.0).then_inc(folded, 1)
                v.memset(state[D:P, :, :], 0.0).then_inc(folded, 1)
                v.tensor_tensor(w_gt[:, :, 0:H], w_gt[:, :, 0:H], bc(norm_g[:].unsqueeze(1), [P, KH, H]),
                                ALU.mult).then_inc(folded, 1)
                v.tensor_tensor(b_g[:], b_g[:], norm_g[:], ALU.mult).then_inc(folded, 1)
                dve.wait_ge(folded, 5)

            def norm(c):
                dve.wait_ge(x_loaded, 16 * c + 16)
                for b in range(B):
                    v.bn_stats(stats[:, b, :], x_norm[:, b, :]).then_inc(stats_done, 1)
                dve.wait_ge(stats_done, B * c + B)
                v.memset(spare[:], 0.0)
                for b in range(B):
                    v.bn_aggr(moments[:, b, :], stats[:, b, :]).then_inc(moments_done, 1)
                dve.wait_ge(moments_done, B * c + B)
                v.tensor_scalar(var_eps[:], moments[:, :, 1], LN_EPS, None, ALU.add).then_inc(var_done, 1)
                dve.wait_ge(rstd_done, c + 1)
                for b in range(B):
                    v.tensor_scalar(x_norm[:, b, :], x_norm[:, b, :], moments[:, b, 0:1], rstd[:, b:b + 1],
                                    ALU.subtract, ALU.mult).then_inc(x_normed, 1)

            def convolve(c, par, first):
                dve.wait_ge(kv_copied, c + 1)
                dve.wait_ge(q_copied, c + 1)
                if not first:
                    dve.wait_ge(state_made, c - 1)
                    dve.wait_ge(qab_ready, c)
                lanes = [(KV[par], raw_kv, conv_kv, kv_conv), (Q[par], raw_q, conv_q, q_conv)]
                for y, x, w, done in lanes:
                    v.tensor_scalar(y[:], x[:, :, TAPS - 1:TAPS - 1 + CH], w[:, TAPS - 1:TAPS], w[:, TAPS:TAPS + 1],
                                    ALU.mult, ALU.add).then_inc(done, 1)
                for n, j in enumerate(range(TAPS - 2, -1, -1)):
                    for y, x, w, done in lanes:
                        dve.wait_ge(done, TAPS * c + n + 1)
                        v.scalar_tensor_tensor(y[:], x[:, :, j:j + CH], w[:, j:j + 1], y[:], ALU.mult,
                                               ALU.add).then_inc(done, 1)
                dve.wait_ge(kv_conv, TAPS * c + TAPS)
                v.tensor_copy(raw_kv[:, :, 0:TAPS - 1], raw_kv[:, :, CH:CH + TAPS - 1]).then_inc(halo_kv, 1)
                dve.wait_ge(q_conv, TAPS * c + TAPS)
                v.tensor_copy(raw_q[:, :, 0:TAPS - 1], raw_q[:, :, CH:CH + TAPS - 1]).then_inc(halo_q, 1)

            def momentum_scans(c, first):
                dve.wait_ge(eta_ready, c + 1)
                for b in range(B):
                    v.tensor_tensor_scan(mom[:, b, :], eta[:, b, :], t["ident"][:], 0.0, ALU.mult,
                                         ALU.add).then_inc(mom_ready, 1)
                if not first:
                    dve.wait_ge(mix_ready, 2 * c)
                for b in range(B):
                    v.tensor_tensor_scan(carry[D:P, b, :], eta[D:P, b, :], zeros[D:P, :], 1.0, ALU.mult,
                                         ALU.add).then_inc(carry_ready, 1)

            def memory_scans(c, par, first):
                dve.wait_ge(keep_ready, c + 1)
                dve.wait_ge(mom_ready, B * c + B)
                for b in range(B):
                    v.tensor_tensor_scan(M[par][:, b, :], keep[:, b, :], mom[:, b, :], 0.0, ALU.mult,
                                         ALU.add).then_inc(m_ready, 1)
                dve.wait_ge(carry_ready, B * c + B)
                for b in range(B):
                    last = v.tensor_tensor_scan(AB[par][:, b, :], keep[:, b, :], carry[:, b, :], ab_start[:, 0:1],
                                                ALU.mult, ALU.add)
                last.then_inc(ab_ready, 1)
                dve.wait_ge(m_ready, B * c + B)
                if not first:
                    dve.wait_ge(hid_m_ready, c - 1)
                v.tensor_copy(ENDS[par][:, :, 0:1], M[par][:, :, CH - 1:CH])
                v.tensor_copy(ENDS[par][:, :, 1:2], mom[:, :, CH - 1:CH]).then_inc(ends_ready, 1)

            def gates(c, par, pairs, first):
                if not first:
                    dve.wait_ge(x2_ready, 2 * c - 2)
                for i in pairs:
                    dve.wait_ge(gate_made, 4 * c + i + 1)
                    src = A if i % 2 else BB
                    v.tensor_tensor(GATE[par][:, 2 * i:2 * i + 2, :], src[:, :, 0:H],
                                    bc(b_g[:].unsqueeze(1), [P, 2, H]), ALU.add)
                    v.tensor_tensor(theta_pre[:, 2 * i:2 * i + 2, :], src[:, :, H:H + D],
                                    bc(b_t[:].unsqueeze(1), [P, 2, D]), ALU.add).then_inc(gate_read, 1)

            def thetas(c, par):
                dve.wait_ge(t_ln, c + 1)
                v.scalar_tensor_tensor(theta_log[:], theta_pre[:], 0.0, theta_log[:], ALU.max,
                                       ALU.add).then_inc(t_soft, 1)
                dve.wait_ge(t_soft, c + 1)
                v.tensor_reduce(theta_sum[:], theta_log[:], AX.X, ALU.add).then_inc(t_sum, 1)
                dve.wait_ge(t_sum, c + 1)
                v.tensor_scalar(THETA[par][:], theta_sum[:], -0.1 * 0.2 / D, None, ALU.mult).then_inc(theta_ready, 1)

            def keys(c, par, first):
                dve.wait_ge(k_turned, c + 1)
                dve.wait_ge(ends_ready, c + 1)
                v.tensor_tensor(KM[par][:], bc(wide(BB)[:, :, 0:D].unsqueeze(2), [P, B, 2, D]),
                                bc(ENDS[par][:].unsqueeze(3), [P, B, 2, D]), ALU.mult).then_inc(km_ready, 1)
                dve.wait_ge(k_squared, c + 1)
                v.tensor_reduce(KNORM[par][:], k_sq[:], AX.X, ALU.add).then_inc(knorm_ready, 1)
                dve.wait_ge(qk_made, c + 1)
                v.tensor_tensor(P1[par][:], wide(A), M[par][:], ALU.mult).then_inc(p1_ready, 1)

            def hidden(c, first):
                dve.wait_ge(sig_ready, c + 1)
                if not first:
                    dve.wait_ge(hid_m_ready, c)
                pre = C[:, 0, :].rearrange("p (b n) -> p b n", n=D)
                v.tensor_tensor(hid[:], pre, sig_h[:], ALU.mult).then_inc(hid_ready, 1)
                dve.wait_ge(hid_ready, c + 1)
                v.scalar_tensor_tensor(slope[:], sig_h[:], 1.0, hid[:], ALU.subtract, ALU.mult).then_inc(tmp_ready, 1)
                dve.wait_ge(tmp_ready, c + 1)
                v.tensor_tensor(slope[:], sig_h[:], slope[:], ALU.subtract).then_inc(slope_ready, 1)

            def gradients(c, par):
                dve.wait_ge(res_made, c + 1)
                dve.wait_ge(slope_ready, c + 1)
                v.tensor_tensor(dpre[:], wide(C)[:, :, D:P], slope[:], ALU.mult).then_inc(dpre_ready, 1)
                dve.wait_ge(squared, 3 * c + 3)
                v.tensor_reduce(nsum[:], squares[:], AX.X, ALU.add).then_inc(nsum_ready, 1)
                dve.wait_ge(nsum_ready, c + 1)
                dve.wait_ge(knorm_ready, c + 1)
                v.tensor_tensor(n1[:], nsum[:, 0, :], nsum[:, 1, :], ALU.mult).then_inc(small, 1)
                v.tensor_tensor(n2[:], nsum[:, 2, :], KNORM[par][:], ALU.mult).then_inc(small, 1)
                dve.wait_ge(small, 4 * c + 2)
                v.tensor_tensor(n3[:], n1[:], n2[:], ALU.add).then_inc(small, 1)
                dve.wait_ge(small, 4 * c + 3)
                v.tensor_scalar(n4[:], n3[:], 0.04, EPS * EPS, ALU.mult, ALU.max).then_inc(n_clipped, 1)
                dve.wait_ge(powered, c + 1)
                dve.wait_ge(theta_ready, c + 1)
                v.scalar_tensor_tensor(factor[:], n5[:], 1.0, THETA[par][:], ALU.min, ALU.mult).then_inc(small, 1)
                dve.wait_ge(small, 4 * c + 4)
                v.tensor_tensor(grad_w1[:], bc(dpre[:].unsqueeze(2), [P, B, 2, D]),
                                bc(factor[:].unsqueeze(2).unsqueeze(3), [P, B, 2, D]),
                                ALU.mult).then_inc(grad_w1_ready, 1)
                v.tensor_tensor(grad_w2[:], wide(C)[:, :, 0:D], bc(factor[:].unsqueeze(2), [P, B, D]),
                                ALU.mult).then_inc(grad_w2_ready, 1)

            def second_hidden(c, par):
                dve.wait_ge(sig2_ready, c + 1)
                v.tensor_tensor(hid2[:], wide(DD), sig_h2[:], ALU.mult).then_inc(hid2_ready, 1)
                dve.wait_ge(hid2_ready, c + 1)
                v.tensor_tensor(hid2_ab[:], hid2[:], AB[par][:], ALU.mult).then_inc(hid2_ab_ready, 1)

            def second_scores(c, par):
                dve.wait_ge(hh_made, c + 1)
                v.tensor_tensor(P2[:], wide(C), M[par][:], ALU.mult).then_inc(p2_ready, 1)

            def gated_output(c, par):
                for h in range(2):
                    n = slice(h * HALF, (h + 1) * HALF)
                    dve.wait_ge(o_squared, B * c + HALF * (h + 1))
                    v.tensor_scalar(o_mean[:, n], o_sum[:, n], 1.0 / H, EPS, ALU.mult, ALU.add).then_inc(o_meaned, 1)
                    dve.wait_ge(o_rs_ready, 2 * c + h + 1)
                    src = (C if h else DD).rearrange("p a (b n) -> p (a b) n", n=H)
                    for b in range(HALF):
                        bb = h * HALF + b
                        last = v.scalar_tensor_tensor(GATE[par][:, bb, :], src[:, b, :], o_rs[:, bb:bb + 1],
                                                      GATE[par][:, bb, :], ALU.mult, ALU.mult)
                    last.then_inc(gated_ready, 1)

            def logits(c):
                dve.wait_ge(lg_made, c + 1)
                v.tensor_copy(t["logits"][:].rearrange("p (b c) e -> p b c e", c=NCH)[:, :, bass.ds(c, 1), :],
                              DD[:, 0, 0:B * E].rearrange("p (b o e) -> p b o e", o=1, e=E)).then_inc(lg_read, 1)

            def step(c, par, first, last, norm_too=True):
                hidden(c, first)
                gradients(c, par)
                if not last:
                    convolve(c + 1, 1 - par, first)
                second_hidden(c, par)
                if not last:
                    momentum_scans(c + 1, False)
                second_scores(c, par)
                if not last:
                    memory_scans(c + 1, 1 - par, first)
                    gates(c + 1, 1 - par, range(4), first)
                    keys(c + 1, 1 - par, False)
                    thetas(c + 1, 1 - par)
                if norm_too:
                    norm(c + 2)
                gated_output(c, par)
                logits(c)

            start()
            norm(0)
            convolve(0, 0, True)
            momentum_scans(0, True)
            memory_scans(0, 0, True)
            gates(0, 0, range(4), True)
            keys(0, 0, True)
            thetas(0, 0)
            norm(1)
            step(0, 0, True, False)
            with dve.Fori(0, NCH // 2 - 2) as i:
                step(i * 2 + 1, 1, False, False)
                step(i * 2 + 2, 0, False, False)
            step(NCH - 3, 1, False, False)
            step(NCH - 2, 0, False, False, norm_too=False)
            step(NCH - 1, 1, False, True, norm_too=False)

        @block.scalar
        def _(act):
            s = nc.scalar

            def turned(c, first):
                if not first:
                    act.wait_ge(gate_made, 4 * c)
                for h, src in enumerate((A, BB)):
                    act.wait_ge(x_turned, 2 * c + h + 1)
                    s.copy(xT[:, :, h * HW:(h + 1) * HW], src).then_inc(x_turned_copied, 1)

            def projections(c):
                act.wait_ge(halo_kv, c + 1)
                act.wait_ge(kv_made, c + 1)
                s.copy(raw_kv[:, :, TAPS - 1:], wide(A)).then_inc(kv_copied, 1)
                act.wait_ge(halo_q, c + 1)
                act.wait_ge(q_made, c + 1)
                s.copy(raw_q[:, :, TAPS - 1:], wide(BB)).then_inc(q_copied, 1)

            def rates(c, first):
                act.wait_ge(ae_made, c + 1)
                if not first:
                    act.wait_ge(rates_made, 2 * c)
                s.activation(sig_ae[:], A.rearrange("p a n -> p (a n)"), ACT.Sigmoid,
                             bias=b_ae[:, 0:1]).then_inc(ae_sig, 1)
                act.wait_ge(rates_made, 2 * c + 1)
                if not first:
                    act.wait_ge(ab_ready, c)
                s.activation(keep[:], wide(BB), ACT.Copy, bias=1.0, scale=-0.1).then_inc(keep_ready, 1)
                act.wait_ge(rates_made, 2 * c + 2)
                s.activation(eta[:], wide(A), ACT.Copy, bias=0.05, scale=0.9).then_inc(eta_ready, 1)

            def thetas(c, first):
                act.wait_ge(gate_read, 4 * c + 4)
                s.activation(theta_log[:], theta_pre[:], ACT.Abs).then_inc(t_abs, 1)
                act.wait_ge(t_abs, c + 1)
                s.activation(theta_log[:], theta_log[:], ACT.Exp, scale=-1.0).then_inc(t_exp, 1)
                act.wait_ge(t_exp, c + 1)
                s.activation(theta_log[:], theta_log[:], ACT.Ln, bias=1.0).then_inc(t_ln, 1)

            def keys(c, first):
                act.wait_ge(km_ready, c + 1)
                if not first:
                    act.wait_ge(knorm_ready, c)
                s.activation(k_sq[:], wide(BB)[:, :, 0:D], ACT.Square).then_inc(k_squared, 1)

            def hidden(c, first):
                act.wait_ge(pre_made, c + 1)
                if not first:
                    act.wait_ge(slope_ready, c)
                s.activation(sig_h[:], C[:, 0, :].rearrange("p (b n) -> p b n", n=D),
                             ACT.Sigmoid).then_inc(sig_ready, 1)

            def hidden_turned(c, par, first):
                act.wait_ge(hid_turned, c + 1)
                s.copy(KV[par][0:D, :, :], wide(DD)[0:D, :, :]).then_inc(hid_turned_copied, 1)
                if not first:
                    act.wait_ge(o_squared, B * c)
                s.activation(squares[:, 0, :, :], hid[:], ACT.Square).then_inc(squared, 1)

            def gradients(c):
                act.wait_ge(dpre_ready, c + 1)
                s.activation(squares[:, 1, :, :], wide(C)[:, :, 0:D], ACT.Square).then_inc(squared, 1)
                s.activation(squares[:, 2, :, :], dpre[:], ACT.Square).then_inc(squared, 1)

            def second_hidden(c):
                act.wait_ge(pre2_made, c + 1)
                s.activation(sig_h2[:], wide(DD), ACT.Sigmoid).then_inc(sig2_ready, 1)

            def retrieve(c):
                act.wait_ge(ret_made, c + 1)
                s.copy(retrieved[:], wide(DD)[0:D, :, :]).then_inc(ret_copied, 1)

            def new_state(c):
                act.wait_ge(state_made, c + 1)
                new = wide(C)
                s.copy(state[:, :, 0:D], new[:, :, 0:D])
                s.copy(state[:, :, D:3 * D], new).then_inc(state_copied, 1)
                s.copy(read_w[0:D, :, 0:D], new[0:D, :, D:P]).then_inc(state_copied, 1)

            def new_read(c):
                act.wait_ge(state_turned, c + 1)
                s.mul(read_w[D:P, :, D:P], wide(DD)[D:P, :, 0:D], -1.0).then_inc(w2_copied, 1)
                act.wait_ge(gram_made, c + 2)
                s.copy(read_w[0:D, :, D:P],
                       C[0:D, 0, :].rearrange("p (b n) -> p b n", n=D)).then_inc(gram_copied, 1)

            def output_norms(c, first):
                for h, src in enumerate((DD, C)):
                    act.wait_ge(o_made, 2 * c + h + 1)
                    if h or not first:
                        act.wait_ge(o_squared, B * c + HALF * h)
                    if not first:
                        act.wait_ge(o_meaned, 2 * c)
                    o = src.rearrange("p a (b n) -> p (a b) n", n=H)
                    for b in range(HALF):
                        bb = h * HALF + b
                        s.activation(o_sq[:, b, :], o[:, b, :], ACT.Square,
                                     accum_out=o_sum[:, bb:bb + 1]).then_inc(o_squared, 1)

            def result_turned(c):
                for h, src in enumerate((DD, C)):
                    act.wait_ge(x2_turned, 2 * c + h + 1)
                    s.copy(x2T[:, :, h * HW:(h + 1) * HW], src).then_inc(x2_turned_copied, 1)

            def step(c, par, first, last):
                hidden(c, first)
                if not last:
                    turned(c + 1, False)
                hidden_turned(c, par, first)
                gradients(c)
                if not last:
                    projections(c + 1)
                    rates(c + 1, False)
                second_hidden(c)
                retrieve(c)
                if not last:
                    keys(c + 1, False)
                    thetas(c + 1, False)
                new_state(c)
                new_read(c)
                output_norms(c, first)
                result_turned(c)

            act.wait_ge(started, 1)
            s.mul(read_w[D:P, :, D:P], wide(DD)[D:P, :, 0:D], -1.0).then_inc(w2_copied, 1)
            act.wait_ge(gram_made, 1)
            s.copy(read_w[0:D, :, D:P], C[0:D, 0, :].rearrange("p (b n) -> p b n", n=D)).then_inc(gram_copied, 1)
            turned(0, True)
            projections(0)
            rates(0, True)
            keys(0, True)
            thetas(0, True)
            step(0, 0, True, False)
            with act.Fori(0, NCH // 2 - 1) as i:
                step(i * 2 + 1, 1, False, False)
                step(i * 2 + 2, 0, False, False)
            step(NCH - 1, 1, False, True)

        @block.tensor
        def _(pe):
            mm = nc.tensor.matmul

            def turn_x(c, first):
                for h, dst in enumerate((A, BB)):
                    pe.wait_ge(x_normed, B * c + HALF * (h + 1))
                    if not first:
                        pe.wait_ge(p1_ready if h == 0 else knorm_ready, c)
                    for b in range(HALF):
                        for k in range(KH):
                            last = nc.tensor.transpose(dst[:, k, b * CH:(b + 1) * CH],
                                                       x_norm[:, h * HALF + b, k * P:(k + 1) * P], t["ident"][:])
                    last.then_inc(x_turned, 1)

            def project(c, dst, w, done):
                for h in range(2):
                    for k in range(KH):
                        last = mm(dst[:, h, :], w[:, k, :], xT[:, k, h * HW:(h + 1) * HW], start=(k == 0),
                                  stop=(k == KH - 1))
                last.then_inc(done, 1)

            def projections(c):
                pe.wait_ge(x_turned_copied, 2 * c + 2)
                project(c, A, w_kv, kv_made)
                project(c, BB, w_qq, q_made)

            def rates(c):
                pe.wait_ge(kv_copied, c + 1)
                project(c, A, w_ae, ae_made)
                pe.wait_ge(ae_sig, c + 1)
                pe.wait_ge(q_copied, c + 1)
                for dst, w in ((BB, mean_a), (A, mean_e)):
                    for h in range(2):
                        last = mm(dst[:, h, :], w[:], sig_ae[:, h * HW:(h + 1) * HW], start=True, stop=True)
                    last.then_inc(rates_made, 1)

            def gates(c, pairs):
                for i in pairs:
                    dst = A if i % 2 else BB
                    if i == 0:
                        pe.wait_ge(keep_ready, c + 1)
                    elif i == 1:
                        pe.wait_ge(eta_ready, c + 1)
                    else:
                        pe.wait_ge(gate_read, 4 * c + i - 1)
                    for j in range(2):
                        b = 2 * i + j
                        for k in range(KH):
                            last = mm(dst[:, j, 0:H + D], xT[:, k, b * CH:(b + 1) * CH], w_gt[:, k, :],
                                      start=(k == 0), stop=(k == KH - 1))
                    last.then_inc(gate_made, 1)

            def keys(c, par):
                pe.wait_ge(kv_conv, TAPS * c + TAPS)
                pe.wait_ge(gate_read, 4 * c + 3)
                for b in range(B):
                    last = nc.tensor.transpose(wide(BB)[:, b, :], KV[par][:, b, :], t["ident"][:])
                last.then_inc(k_turned, 1)
                pe.wait_ge(q_conv, TAPS * c + TAPS)
                pe.wait_ge(gate_read, 4 * c + 4)
                for b in range(B):
                    last = mm(wide(A)[:, b, :], KV[par][0:D, b, :], Q[par][0:D, b, :], start=True, stop=True)
                last.then_inc(qk_made, 1)

            def hidden(c, par, first):
                pe.wait_ge(kv_conv, TAPS * c + TAPS)
                if not first:
                    pe.wait_ge(state_copied, 2 * c)
                    pe.wait_ge(x2_turned_copied, 2 * c)
                for b in range(B):
                    last = mm(C[:, 0, b * D:(b + 1) * D], KV[par][0:D, b, :], state[0:D, b, 0:D], start=True, stop=True)
                last.then_inc(pre_made, 1)

            def hidden_turned(c, first):
                pe.wait_ge(consts, 16 * len(loads))
                pe.wait_ge(hid_ready, c + 1)
                if not first:
                    pe.wait_ge(lg_read, c)
                for b in range(B):
                    last = nc.tensor.transpose(wide(DD)[0:D, b, :], hid[:, b, :], t["ident"][:])
                last.then_inc(hid_turned, 1)

            def residual(c, par):
                pe.wait_ge(hid_turned_copied, c + 1)
                pe.wait_ge(gram_copied, c + 1)
                for b in range(B):
                    last = mm(wide(C)[:, b, :], KV[par][:, b, :], read_w[:, b, :], start=True, stop=True)
                last.then_inc(res_made, 1)

            def second_hidden(c, par):
                pe.wait_ge(grad_w1_ready, c + 1)
                pe.wait_ge(p1_ready, c + 1)
                pe.wait_ge(qab_ready, c + 1)
                for b in range(B):
                    mm(wide(DD)[:, b, :], state[:, b, 0:2 * D], QAB[par][:, b, :], start=True, stop=False)
                    last = mm(wide(DD)[:, b, :], grad_w1[:, b, :, :].rearrange("p a n -> p (a n)"), P1[par][:, b, :],
                              start=False, stop=True)
                last.then_inc(pre2_made, 1)

            def second_scores(c, par):
                pe.wait_ge(hid2_ready, c + 1)
                pe.wait_ge(grad_w2_ready, c + 1)
                for b in range(B):
                    last = mm(wide(C)[:, b, :], KV[par][0:D, b, :], hid2[0:D, b, :], start=True, stop=True)
                last.then_inc(hh_made, 1)

            def retrieve(c):
                pe.wait_ge(hid2_ab_ready, c + 1)
                pe.wait_ge(p2_ready, c + 1)
                for b in range(B):
                    mm(wide(DD)[0:D, b, :], state[:, b, 2 * D:3 * D], hid2_ab[:, b, :], start=True, stop=False)
                    last = mm(wide(DD)[0:D, b, :], grad_w2[:, b, :], P2[:, b, :], start=False, stop=True)
                last.then_inc(ret_made, 1)

            def new_state(c, par):
                pe.wait_ge(mix_ready, 2 * c + 2)
                pe.wait_ge(km_ready, c + 1)
                pe.wait_ge(hid_m_ready, c + 1)
                for b in range(B):
                    dst = wide(C)[:, b, :]
                    mm(dst, MIX[par][:, b, :], state[:, b, D:3 * D], start=True, stop=False, skip_group_check=True)
                    mm(dst[:, 0:D], KM[par][:, b, :, :].rearrange("p a n -> p (a n)"), grad_w1[:, b, 0, :],
                       start=False, stop=False, skip_group_check=True)
                    last = mm(dst[:, D:P], hid_m[:, b, :, :].rearrange("p a n -> p (a n)"), grad_w2[:, b, :],
                              start=False, stop=True, skip_group_check=True)
                last.then_inc(state_made, 1)

            def turn_state(done):
                for b in range(B):
                    last = nc.tensor.transpose(wide(DD)[:, b, :], state[:, b, D:3 * D], t["ident"][:])
                last.then_inc(done, 1)

            def gram(n):
                pe.wait_ge(consts, 16 * len(loads))
                pe.wait_ge(w2_copied, n + 1)
                for b in range(B):
                    w2 = read_w[D:P, b, D:P]
                    last = mm(C[0:D, 0, b * D:(b + 1) * D], w2, w2, start=True, stop=True)
                last.then_inc(gram_made, 1)

            def new_read(c):
                pe.wait_ge(state_copied, 2 * c + 2)
                pe.wait_ge(ret_copied, c + 1)
                turn_state(state_turned)
                gram(c + 1)

            def outputs(c):
                for h, dst in enumerate((DD, C)):
                    if h:
                        pe.wait_ge(gram_copied, c + 2)
                    for b in range(HALF):
                        last = mm(dst[:, b // 2, (b % 2) * H:(b % 2 + 1) * H], retrieved[:, h * HALF + b, :], w_o[:],
                                  start=True, stop=True)
                    last.then_inc(o_made, 1)

            def turn_result(c):
                for h, dst in enumerate((DD, C)):
                    pe.wait_ge(x2_ready, 2 * c + h + 1)
                    for b in range(HALF):
                        for k in range(KH):
                            last = nc.tensor.transpose(dst[:, k, b * CH:(b + 1) * CH],
                                                       x_res[:, h * HALF + b, k * P:(k + 1) * P], t["ident"][:])
                    last.then_inc(x2_turned, 1)

            def logits(c):
                pe.wait_ge(x2_turned_copied, 2 * c + 2)
                for b in range(B):
                    for k in range(KH):
                        last = mm(DD[:, 0, b * E:(b + 1) * E], x2T[:, k, b * CH:(b + 1) * CH], t["gate_c"][:, k, :],
                                  start=(k == 0), stop=(k == KH - 1))
                last.then_inc(lg_made, 1)

            def step(c, par, first, last):
                hidden(c, par, first)
                if not last:
                    turn_x(c + 1, False)
                hidden_turned(c, first)
                if not last:
                    projections(c + 1)
                residual(c, par)
                if not last:
                    rates(c + 1)
                second_hidden(c, par)
                if not last:
                    gates(c + 1, (0, 1))
                second_scores(c, par)
                if not last:
                    gates(c + 1, (2, 3))
                retrieve(c)
                new_state(c, par)
                if not last:
                    keys(c + 1, 1 - par)
                new_read(c)
                outputs(c)
                turn_result(c)
                logits(c)

            pe.wait_ge(consts, 16 * len(loads))
            pe.wait_ge(folded, 5)
            turn_state(started)
            gram(0)
            turn_x(0, True)
            projections(0)
            rates(0)
            gates(0, range(4))
            keys(0, 0)
            step(0, 0, True, False)
            with pe.Fori(0, NCH // 2 - 1) as i:
                step(i * 2 + 1, 1, False, False)
                step(i * 2 + 2, 0, False, False)
            step(NCH - 1, 1, False, True)


def build(nc, d):
    with ExitStack() as sems, ExitStack() as whole:
        def keep(n, shape, dt=F32):
            return whole.enter_context(nc.sbuf_tensor(n, shape, dt))

        ps = whole.enter_context(nc.psum_tensor("ps", [P, 8, 512], F32))
        t = {
            "ident": keep("ident", [P, P]), "iota": keep("iota", [P, P]), "partition": keep("partition", [P, 1]),
            "rank_of_expert": keep("rank_of_expert", [P, E]), "gate_w": keep("gate_w", [P, KH, E]),
            "gate_c": keep("gate_c", [P, KH, E]), "mean_w": keep("mean_w", [P, P]),
            "upper": keep("upper", [P, P], BF16), "ones_bf": keep("ones_bf", [P, P], BF16),
            "ones_row": keep("ones_row", [P, P]), "minus_half": keep("minus_half", [P, B]), "logits": keep("logits", [P, NT, E]),
            "gather_index": keep("gather_index", [P, ST], I32), "scatter_index": keep("scatter_index", [P, ST], I32),
            "w1": d["w1"], "w2": d["w2"],
        }
        for n in ("ident", "iota", "partition", "rank", "gate_w", "upper", "mean_w", "ones"):
            t["d_" + n] = d[n]
        x1 = nc.dram_tensor("x1", (TOK, H), F32, kind="Internal").ap()
        first = Semaphores(nc, sems, "first_")
        moe = Semaphores(nc, sems, "moe_")
        att = Semaphores(nc, sems, "att_")
        with ExitStack() as ctx:
            first_logits(nc, first, ctx, ps[:], t, d["x"], d["xT"], x1)
        with ExitStack() as ctx:
            route(nc, moe, ctx, ps[:], t, "route1")
        with ExitStack() as ctx:
            experts(nc, moe, ctx, ps[:], t, "moe1", d["x"], x1)
        with ExitStack() as ctx:
            memory_attention(nc, att, ctx, ps[:], t, x1, d["out"], d)
        with nc.Block() as block:
            @block.sync
            def _(sp):
                for n, s in moe.items():
                    if not n.startswith("pool_dma"):
                        sp.sem_clear(s)
        with ExitStack() as ctx:
            route(nc, moe, ctx, ps[:], t, "route2")
        with ExitStack() as ctx:
            experts(nc, moe, ctx, ps[:], t, "moe2", d["out"], d["out"])


def kernel(**inputs):
    import numpy as np
    import concourse.bacc as bacc
    from concourse.bass_utils import run_bass_kernel_spmd

    a = {k.replace("L0_attn_", ""): np.asarray(v) for k, v in inputs.items()}
    x = a["hidden"].reshape(TOK, H)
    f = np.float32
    eye = np.eye(P, dtype=f)

    def over_partitions(row):
        return np.broadcast_to(row[None, :], (P, row.shape[0]))

    low = np.arange(P) >= D
    arrays = {
        "x": x, "xT": x.T,
        "gate_w": a["L0_ffn_gate_w"], "w1": a["L0_ffn_w1"], "w2": a["L0_ffn_w2"],
        "w_kv": np.concatenate([a["Wk"].T, a["Wv"].T], 1), "w_qq": np.concatenate([a["Wq"].T, a["Wq"].T], 1),
        "w_ae": np.concatenate([a["aW"].T, a["eW"].T], 1), "w_gt": np.concatenate([a["gW"].T, a["tW"].T], 1),
        "w_o": a["Wo"].T,
        "conv_kv": np.concatenate([np.concatenate([a["ckw"], a["ckb"][:, None]], 1),
                                   np.concatenate([a["cvw"], a["cvb"][:, None]], 1)], 0),
        "conv_q": np.concatenate([np.concatenate([a["cqw"], a["cqb"][:, None]], 1)] * 2, 0),
        "b_ae": np.concatenate([a["ab"], a["eb"]])[:, None],
        "b_t": over_partitions(a["tb"]), "b_g": over_partitions(a["gb"]), "norm_g": over_partitions(a["norm_g"]),
        "w1T": np.broadcast_to(a["mW1"].T[:, None, :], (D, B, D)),
        "w2T": np.broadcast_to(a["mW2"].T[:, None, :], (D, B, D)),
        "ident": eye, "iota": np.broadcast_to(np.arange(P, dtype=f)[None, :], (P, P)),
        "partition": np.arange(P, dtype=f)[:, None],
        "rank": np.broadcast_to((E - np.arange(E)).astype(f)[None, :], (P, E)),
        "upper": np.triu(np.ones((P, P), f)), "ones": np.ones((P, P), f), "mean_w": np.full((P, P), 1.0 / H, f),
        "mean_a": np.where(low, 0.0, 1.0 / D).astype(f)[:, None] * np.ones((1, P), f),
        "mean_e": np.where(low, 1.0 / D, 0.0).astype(f)[:, None] * np.ones((1, P), f),
        "fold": np.concatenate([eye[:D, :D]] * 2, 0), "fold_low": np.concatenate([0 * eye[:D, :D], eye[:D, :D]], 0),
        "minus_i": np.broadcast_to(-eye[:D, None, :D], (D, B, D)),
        "ab_start": np.where(low, 0.0, 1.0).astype(f)[:, None],
    }
    arrays = {k: np.ascontiguousarray(v) for k, v in arrays.items()}
    nc = bacc.Bacc("TRN2", target_bir_lowering=False, num_devices=1)
    d = {k: nc.dram_tensor("in_" + k, v.shape, F32, kind="ExternalInput").ap() for k, v in arrays.items()}
    d["out"] = nc.dram_tensor("out_x", (TOK, H), F32, kind="ExternalOutput").ap()
    build(nc, d)
    r = run_bass_kernel_spmd(nc, [{"in_" + k: v for k, v in arrays.items()}], core_ids=[0])
    return r.results[0]["out_x"].reshape(B, S, H)
```

```python
from contextlib import ExitStack

import concourse.bass as bass
from concourse import mybir

F32 = mybir.dt.float32
BF16 = mybir.dt.bfloat16
I32 = mybir.dt.int32
ALU = mybir.AluOpType
ACT = mybir.ActivationFunctionType
AX = mybir.AxisListType

P = 128
B, S, H = 8, 1024, 256
D = 64
CH = 128
NCH = S // CH
TOK = B * S
NT = TOK // P
KH = H // P
E, F, CAP = 8, 1024, 320
SLOTS = E * CAP
ST = SLOTS // P
PAIRS = E // 2
PT = ST // PAIRS
KF = F // P
LN_EPS = 1e-5
EPS = 1e-6
BIG = 16384.0
TAPS = 4
BW = B * CH


class Semaphores(dict):

    def __init__(self, nc, ctx, prefix):
        self.nc, self.ctx, self.prefix = nc, ctx, prefix

    def __missing__(self, name):
        self[name] = self.ctx.enter_context(self.nc.semaphore(self.prefix + name))
        return self[name]


def bc(ap, shape):
    return ap.broadcast_to(shape)


def route(nc, sems, ctx, ps, t, name):

    def sem(n):
        return sems[n]

    def sb(n, shape, dt):
        return ctx.enter_context(nc.sbuf_tensor(f"{name}_{n}", shape, dt))

    logits, ones_row = t["logits"], t["ones_row"]
    top = sb("top", [P, NT], F32)
    hit = sb("hit", [P, NT, E], F32)
    rank = sb("rank", [P, NT], F32)
    onehot = sb("onehot", [P, NT, E], BF16)
    total = sb("total", [P, NT, E], F32)
    running = sb("running", [P, NT, E], F32)
    place = sb("place", [P, NT, E], F32)
    pos = sb("pos", [P, NT], F32)
    over = sb("over", [P, NT], F32)
    slot = sb("slot", [P, NT], F32)
    slot_i = sb("slot_i", [P, NT], I32)
    row_i = sb("row_i", [P, NT], I32)
    col_i = sb("col_i", [P, NT], I32)
    row = sb("row", [P, NT], F32)
    col = sb("col", [P, NT], F32)
    row_hot = sb("row_hot", [P, NT, P], BF16)
    col_hot = sb("col_hot", [P, NT, 3, ST], BF16)
    found = sb("found", [P, 3, ST], F32)
    token = sb("token", [P, ST], F32)
    empty = sb("empty", [P, ST], F32)
    sc_f = sb("sc_f", [P, ST], F32)
    cum_ps = ps[:, 0, :].rearrange("p (n e) -> p n e", e=E)
    tot_ps = ps[:, 1, :].rearrange("p (n e) -> p n e", e=E)
    tab_ps = ps[:, 2, 0:3 * ST]
    QUARTER = NT // 4

    chain = sem("dve_done")
    onehot_ready = sem("onehot_ready")
    counts_ready = sem("counts_ready")
    col_hot_ready = sem("col_hot_ready")
    row_hot_ready = sem("row_hot_ready")
    table_ready = sem("table_ready")
    with nc.Block() as block:

        @block.vector
        def _(dve):
            v = nc.vector
            v.tensor_reduce(top[:], logits[:], AX.X, ALU.max).then_inc(chain, 1)
            dve.wait_ge(chain, 1)
            v.tensor_tensor(hit[:], logits[:], bc(top[:].unsqueeze(2), [P, NT, E]), ALU.is_equal).then_inc(chain, 1)
            dve.wait_ge(chain, 2)
            v.tensor_tensor(hit[:], hit[:], bc(t["rank_of_expert"][:].unsqueeze(1), [P, NT, E]),
                            ALU.mult).then_inc(chain, 1)
            dve.wait_ge(chain, 3)
            v.tensor_reduce(rank[:], hit[:], AX.X, ALU.max).then_inc(chain, 1)
            dve.wait_ge(chain, 4)
            v.tensor_tensor(onehot[:], hit[:], bc(rank[:].unsqueeze(2), [P, NT, E]),
                            ALU.is_equal).then_inc(onehot_ready, 1)
            dve.wait_ge(counts_ready, 1)
            v.tensor_copy(total[:], tot_ps).then_inc(chain, 1)
            dve.wait_ge(chain, 5)
            for e in range(E):
                last = v.tensor_tensor_scan(running[:, :, e], ones_row[:, 0:NT], total[:, :, e], 0.0,
                                            ALU.mult, ALU.add)
            last.then_inc(chain, 1)
            dve.wait_ge(chain, 6)
            v.tensor_tensor(running[:], running[:], total[:], ALU.subtract).then_inc(chain, 1)
            dve.wait_ge(chain, 7)
            v.tensor_tensor(place[:], cum_ps, running[:], ALU.add).then_inc(chain, 1)
            dve.wait_ge(chain, 8)
            v.tensor_tensor(place[:], place[:], onehot[:], ALU.mult).then_inc(chain, 1)
            dve.wait_ge(chain, 9)
            v.tensor_reduce(pos[:], place[:], AX.X, ALU.add).then_inc(chain, 1)
            dve.wait_ge(chain, 10)
            v.tensor_scalar(over[:], pos[:], float(CAP), BIG, ALU.is_gt, ALU.mult).then_inc(chain, 1)
            v.tensor_scalar(slot[:], rank[:], -float(CAP), float(E * CAP) - 1.0, ALU.mult, ALU.add).then_inc(chain, 1)
            dve.wait_ge(chain, 12)
            v.tensor_tensor(slot[:], slot[:], pos[:], ALU.add).then_inc(chain, 1)
            dve.wait_ge(chain, 13)
            v.tensor_tensor(slot_i[:], slot[:], over[:], ALU.add).then_inc(chain, 1)
            dve.wait_ge(chain, 14)
            v.tensor_scalar(row_i[:], slot_i[:], P - 1, None, ALU.bitwise_and).then_inc(chain, 1)
            v.tensor_scalar(col_i[:], slot_i[:], 7, None, ALU.logical_shift_right).then_inc(chain, 1)
            dve.wait_ge(chain, 16)
            v.tensor_copy(row[:], row_i[:]).then_inc(chain, 1)
            v.tensor_copy(col[:], col_i[:]).then_inc(chain, 1)
            dve.wait_ge(chain, 18)
            v.tensor_tensor(col_hot[:, :, 0, :], bc(col[:].unsqueeze(2), [P, NT, ST]),
                            bc(t["iota"][:, 0:ST].unsqueeze(1), [P, NT, ST]), ALU.is_equal).then_inc(chain, 1)
            dve.wait_ge(chain, 19)
            v.tensor_tensor(col_hot[:, :, 1, :], col_hot[:, :, 0, :],
                            bc(t["iota"][:, 0:NT].unsqueeze(2), [P, NT, ST]), ALU.mult)
            v.tensor_scalar(col_hot[:, :, 2, :], col_hot[:, :, 0, :], t["partition"][:, 0:1], None,
                            ALU.mult).then_inc(col_hot_ready, 1)
            for i in range(4):
                n = slice(i * QUARTER, (i + 1) * QUARTER)
                v.tensor_tensor(row_hot[:, n, :], bc(row[:, n].unsqueeze(2), [P, QUARTER, P]),
                                bc(t["iota"][:].unsqueeze(1), [P, QUARTER, P]),
                                ALU.is_equal).then_inc(row_hot_ready, 1)
            dve.wait_ge(table_ready, 1)
            v.tensor_copy(found[:], tab_ps.rearrange("p (a s) -> p a s", a=3)).then_inc(chain, 1)
            dve.wait_ge(chain, 20)
            v.scalar_tensor_tensor(token[:], found[:, 1, :], float(P), found[:, 2, :], ALU.mult,
                                   ALU.add).then_inc(chain, 1)
            v.tensor_scalar(empty[:], found[:, 0, :], -BIG, BIG, ALU.mult, ALU.add).then_inc(chain, 1)
            dve.wait_ge(chain, 22)
            v.tensor_copy(t["gather_index"][:], token[:]).then_inc(chain, 1)
            v.tensor_tensor(t["scatter_index"][:], token[:], empty[:], ALU.add).then_inc(chain, 1)

        @block.tensor
        def _(pe):
            pe.wait_ge(onehot_ready, 1)
            nc.tensor.matmul(ps[:, 0, :], t["upper"][:], onehot[:].rearrange("p n e -> p (n e)"), start=True, stop=True)
            nc.tensor.matmul(ps[:, 1, :], t["ones_bf"][:], onehot[:].rearrange("p n e -> p (n e)"), start=True,
                             stop=True).then_inc(counts_ready, 1)
            pe.wait_ge(col_hot_ready, 1)
            for n in range(NT):
                if n % QUARTER == 0:
                    pe.wait_ge(row_hot_ready, n // QUARTER + 1)
                last = nc.tensor.matmul(tab_ps, row_hot[:, n, :], col_hot[:, n, :, :].rearrange("p a s -> p (a s)"),
                                        start=(n == 0), stop=(n == NT - 1))
            last.then_inc(table_ready, 1)


def experts(nc, sems, ctx, ps, t, name, rows_dram, result_dram):

    def sem(n):
        return sems[n]

    def sb(n, shape, dt=F32):
        return ctx.enter_context(nc.sbuf_tensor(f"{name}_{n}", shape, dt))

    rows = sb("rows", [P, ST, H])
    stats = sb("stats", [P, PT, 6])
    moments = sb("moments", [P, PT, 2])
    rstd = sb("rstd", [P, PT])
    var_eps = sb("var_eps", [P, PT])
    spare = sb("spare", [P, 1])
    normed = sb("normed", [P, PT, H])
    normedT = sb("normedT", [P, KH, PT * P])
    lg = sb("lg", [P, PT, E])
    lmax = sb("lmax", [P, PT])
    ex = sb("ex", [P, PT, E])
    den = sb("den", [P, PT])
    prob = sb("prob", [P, PT])
    w1 = [sb(f"w1_{i}", [P, KH, F]) for i in range(2)]
    w2 = [sb(f"w2_{i}", [P, KF, H]) for i in range(2)]
    hidden = [sb(f"hidden{i}", [P, KF, CAP]) for i in range(2)]

    gathered = sem("pool_dma_gathered_" + name)
    w1_loaded = [sem(f"w1_loaded{i}") for i in range(2)]
    w2_loaded = [sem(f"w2_loaded{i}") for i in range(2)]
    stats_done = sem("stats_done")
    moments_done = sem("moments_done")
    rstd_done = sem("rstd_done")
    var_done = sem("var_done")
    normed_ready = sem("normed_ready")
    turned = sem("turned")
    turned_copied = sem("turned_copied")
    logits_done = sem("logits_done")
    lg_copied = sem("lg_copied")
    lmax_done = sem("lmax_done")
    lg_shifted = sem("lg_shifted")
    exp_done = sem("exp_done")
    den_done = sem("den_done")
    inv_done = sem("inv_done")
    prob_ready = sem("prob_ready")
    up_done = [sem(f"up_done{i}") for i in range(2)]
    relu_done = sem("relu_done")
    y_done = [sem(f"y_done{i}") for i in range(2)]
    y_read = sem("y_read")
    scattered = sem("pool_dma_scattered_" + name)

    YS = [[(0, 0, P, 0), (1, 0, P, P), (2, 0, D, 2 * P)], [(2, D, D, 0), (3, 0, P, D), (4, 0, P, D + P)]]
    NY = len(YS[0])

    with nc.Block() as block:

        @block.sync
        def _(sp):
            def load_up(g, i):
                sp.dma_start(w1[i][:], t["w1"][bass.ds(g * 2 + i, 1), :, :].rearrange("o (k p) f -> p (o k) f", p=P)
                             ).then_inc(w1_loaded[i], 16)

            def load_down(g, i):
                sp.dma_start(w2[i][:], t["w2"][bass.ds(g * 2 + i, 1), :, :].rearrange("o (k p) h -> p (o k) h", p=P)
                             ).then_inc(w2_loaded[i], 16)

            for i in range(2):
                load_up(0, i)
                load_down(0, i)
            with sp.Fori(1, PAIRS) as g:
                for i in range(2):
                    sp.wait_ge(up_done[i], g * KF)
                    load_up(g, i)
                for i in range(2):
                    sp.wait_ge(y_done[i], g * NY)
                    load_down(g, i)

        @block.gpsimd
        def _(pool):
            def gather(g):
                for j in range(g * PT, (g + 1) * PT):
                    nc.gpsimd.indirect_dma_start(rows[:, j, :], None, rows_dram,
                                                 bass.IndirectOffsetOnAxis(t["gather_index"][:, j:j + 1], 0),
                                                 bounds_check=TOK - 1, oob_is_err=False).then_inc(gathered, 16)

            def power(g):
                pool.wait_ge(var_done, g + 1)
                nc.gpsimd.tensor_tensor(rstd[:], var_eps[:], t["minus_half"][:, 0:PT], ALU.pow).then_inc(rstd_done, 1)

            def scatter(g):
                for i in range(PT):
                    j = g * PT + i
                    pool.wait_ge(y_read, 2 * NY * g + (i + 1 if i < 2 else i + 2))
                    nc.gpsimd.indirect_dma_start(result_dram,
                                                 bass.IndirectOffsetOnAxis(t["scatter_index"][:, j:j + 1], 0),
                                                 rows[:, j, :], None,
                                                 bounds_check=TOK - 1, oob_is_err=False).then_inc(scattered, 16)

            for g in range(PAIRS):
                gather(g)
                if g == 1:
                    power(0)
                pool.wait_ge(gathered, 16 * PT * (g + 1))
            for g in range(PAIRS):
                if g + 1 < PAIRS:
                    power(g + 1)
                scatter(g)
            pool.wait_ge(scattered, 16 * ST)

        @block.vector
        def _(dve):
            v = nc.vector

            def norm(g):
                dve.wait_ge(gathered, 16 * PT * (g + 1))
                for i in range(PT):
                    v.bn_stats(stats[:, i, :], rows[:, bass.ds(g * PT + i, 1), :].rearrange("p o h -> p (o h)")
                               ).then_inc(stats_done, 1)
                dve.wait_ge(stats_done, PT * (g + 1))
                v.memset(spare[:], 0.0)
                for i in range(PT):
                    v.bn_aggr(moments[:, i, :], stats[:, i, :]).then_inc(moments_done, 1)
                dve.wait_ge(moments_done, PT * (g + 1))
                v.tensor_scalar(var_eps[:], moments[:, :, 1], LN_EPS, None, ALU.add).then_inc(var_done, 1)
                dve.wait_ge(rstd_done, g + 1)
                for i in range(PT):
                    v.tensor_scalar(normed[:, i, :], rows[:, bass.ds(g * PT + i, 1), :].rearrange("p o h -> p (o h)"),
                                    moments[:, i, 0:1], rstd[:, i:i + 1], ALU.subtract,
                                    ALU.mult).then_inc(normed_ready, 1)

            def probability(g):
                dve.wait_ge(logits_done, g + 1)
                v.tensor_copy(lg[:], ps[:, 5, 0:PT * E].rearrange("p (i e) -> p i e", e=E)).then_inc(lg_copied, 1)
                dve.wait_ge(lg_copied, g + 1)
                v.tensor_reduce(lmax[:], lg[:], AX.X, ALU.max).then_inc(lmax_done, 1)
                dve.wait_ge(lmax_done, g + 1)
                v.tensor_tensor(lg[:], lg[:], bc(lmax[:].unsqueeze(2), [P, PT, E]),
                                ALU.subtract).then_inc(lg_shifted, 1)
                dve.wait_ge(exp_done, g + 1)
                v.tensor_reduce(den[:], ex[:], AX.X, ALU.add).then_inc(den_done, 1)
                dve.wait_ge(den_done, g + 1)
                v.reciprocal(prob[:], den[:]).then_inc(inv_done, 1)
                dve.wait_ge(inv_done, g + 1)
                v.tensor_scalar(prob[:], prob[:], 0.5, None, ALU.mult).then_inc(prob_ready, 1)
                dve.wait_ge(prob_ready, g + 1)

            def finish(g):
                for i in range(2):
                    for j, (tile, p0, n, _) in enumerate(YS[i]):
                        dve.wait_ge(y_done[i], NY * g + j + 1)
                        r = rows[p0:p0 + n, bass.ds(g * PT + tile, 1), :].rearrange("p o h -> p (o h)")
                        v.scalar_tensor_tensor(r, ps[p0:p0 + n, 6 + (NY * i + j) % 2, 0:H],
                                               prob[p0:p0 + n, tile:tile + 1], r, ALU.mult,
                                               ALU.add).then_inc(y_read, 1)

            norm(0)
            with dve.Fori(0, PAIRS - 1) as g:
                probability(g)
                dve.wait_ge(turned, PT * (g + 1))
                norm(g + 1)
                finish(g)
            probability(PAIRS - 1)
            finish(PAIRS - 1)

        @block.scalar
        def _(act):
            s = nc.scalar

            def turn(g, first):
                if not first:
                    act.wait_ge(up_done[1], KF * g)
                for i in range(PT):
                    act.wait_ge(turned, PT * g + i + 1)
                    s.copy(normedT[:, :, i * P:(i + 1) * P],
                           ps[:, i % 2, 0:H].rearrange("p (k c) -> p k c", k=KH)).then_inc(turned_copied, 1)
                act.wait_ge(lg_shifted, g + 1)
                s.activation(ex[:], lg[:], ACT.Exp).then_inc(exp_done, 1)
                for i in range(2):
                    if not first:
                        act.wait_ge(y_done[i], NY * g)
                    for f in range(KF):
                        act.wait_ge(up_done[i], KF * g + f + 1)
                        s.activation(hidden[i][:, f, :], ps[:, 2 + (KF * i + f) % 3, 0:CAP], ACT.Relu).then_inc(relu_done, 1)

            turn(0, True)
            with act.Fori(1, PAIRS) as g:
                turn(g, False)

        @block.tensor
        def _(pe):
            def logits(g, i):
                pe.wait_ge(turned_copied, PT * g + i + 1)
                for k in range(KH):
                    last = nc.tensor.matmul(ps[:, 5, i * E:(i + 1) * E], normedT[:, k, i * P:(i + 1) * P],
                                            t["gate_w"][:, k, :], start=(k == 0), stop=(k == KH - 1))
                return last

            def turn(g, first):
                for i in range(PT):
                    pe.wait_ge(normed_ready, PT * g + i + 1)
                    if not first or i >= 2:
                        pe.wait_ge(turned_copied, PT * g + i - 1)
                    if i == 0 and not first:
                        pe.wait_ge(lg_copied, g)
                    for k in range(KH):
                        last = nc.tensor.transpose(ps[:, i % 2, k * P:(k + 1) * P], normed[:, i, k * P:(k + 1) * P],
                                                   t["ident"][:])
                    last.then_inc(turned, 1)
                    if i:
                        logits(g, i - 1)
                logits(g, PT - 1).then_inc(logits_done, 1)
                for i in range(2):
                    pe.wait_ge(w1_loaded[i], 16 * g + 16)
                    for f in range(KF):
                        if KF * i + f >= 3:
                            pe.wait_ge(relu_done, 2 * KF * g + KF * i + f - 2)
                        for k in range(KH):
                            last = nc.tensor.matmul(ps[:, 2 + (KF * i + f) % 3, 0:CAP], w1[i][:, k, f * P:(f + 1) * P],
                                                    normedT[:, k, i * CAP:(i + 1) * CAP], start=(k == 0),
                                                    stop=(k == KH - 1))
                        last.then_inc(up_done[i], 1)
                for i in range(2):
                    pe.wait_ge(w2_loaded[i], 16 * g + 16)
                    pe.wait_ge(relu_done, 2 * KF * g + KF * (i + 1))
                    for j, (_, p0, n, c0) in enumerate(YS[i]):
                        if not first or NY * i + j >= 2:
                            pe.wait_ge(y_read, 2 * NY * g + NY * i + j - 1)
                        for f in range(KF):
                            last = nc.tensor.matmul(ps[p0:p0 + n, 6 + (NY * i + j) % 2, 0:H],
                                                    hidden[i][:, f, c0:c0 + n], w2[i][:, f, :],
                                                    start=(f == 0), stop=(f == KF - 1))
                        last.then_inc(y_done[i], 1)

            turn(0, True)
            with pe.Fori(1, PAIRS) as g:
                turn(g, False)


def first_logits(nc, sems, ctx, ps, t, x_dram, xT_dram, x1_dram):

    def sem(n):
        return sems[n]

    GROUP = 1024
    PER = GROUP // P
    xt = [ctx.enter_context(nc.sbuf_tensor(f"xt{i}", [P, KH, GROUP], F32)) for i in range(2)]
    mean = ctx.enter_context(nc.sbuf_tensor("gate_mean", [P, E], F32))
    stage = ctx.enter_context(nc.sbuf_tensor("stage", [P, 2, P], F32))
    consts = sem("consts")
    x_copied = sem("x_copied")
    loaded = [sem(f"loaded{i}") for i in range(2)]
    mean_done = sem("mean_done")
    mean_copied = sem("mean_copied")
    centred = sem("centred")
    made = sem("made")
    read = sem("read")
    cast = sem("cast")
    loads = [(t["ident"][:], t["d_ident"]), (t["iota"][:], t["d_iota"]), (t["partition"][:], t["d_partition"]),
             (t["rank_of_expert"][:], t["d_rank"]), (t["gate_w"][:], t["d_gate_w"].rearrange("(k p) e -> p k e", p=P)),
             (stage[:, 0, :], t["d_upper"]), (t["mean_w"][:], t["d_mean_w"]), (stage[:, 1, :], t["d_ones"])]

    with nc.Block() as block:

        @block.sync
        def _(sp):
            def load(n, i):
                sp.dma_start(xt[i][:], xT_dram[:, bass.ds(n * GROUP, GROUP)].rearrange("(k p) n -> p k n", p=P)
                             ).then_inc(loaded[i], 16)

            for dst, src in loads:
                sp.dma_start(dst, src).then_inc(consts, 16)
            load(0, 0)
            load(1, 1)
            with sp.Fori(1, TOK // GROUP // 2) as n:
                for i in range(2):
                    sp.wait_ge(made, n * 2 + i - 1)
                    load(n * 2 + i, i)

        @block.gpsimd
        def _(pool):
            pool.dma_start(x1_dram.rearrange("(a b) h -> a (b h)", a=P), x_dram.rearrange("(a b) h -> a (b h)", a=P)
                           ).then_inc(x_copied, 16)
            pool.wait_ge(x_copied, 16)

        @block.vector
        def _(dve):
            v = nc.vector
            dve.wait_ge(consts, 16 * len(loads))
            v.tensor_copy(t["upper"][:], stage[:, 0, :]).then_inc(cast, 1)
            v.tensor_copy(t["ones_bf"][:], stage[:, 1, :]).then_inc(cast, 1)
            v.memset(t["ones_row"][:], 1.0).then_inc(cast, 1)
            v.memset(t["minus_half"][:], -0.5).then_inc(cast, 1)
            dve.wait_ge(mean_done, 1)
            v.tensor_copy(mean[:], ps[:, 2, 0:E]).then_inc(mean_copied, 1)
            dve.wait_ge(mean_copied, 1)
            v.tensor_tensor(t["gate_c"][:], t["gate_w"][:], bc(mean[:].unsqueeze(1), [P, KH, E]),
                            ALU.subtract).then_inc(centred, 1)
            with dve.Fori(0, TOK // GROUP // 2) as n:
                for i in range(2):
                    dve.wait_ge(made, n * 2 + i + 1)
                    v.tensor_copy(t["logits"][:, bass.ds(n * (2 * PER) + i * PER, PER), :],
                                  ps[:, i, 0:PER * E].rearrange("p (n e) -> p n e", e=E)).then_inc(read, 1)

        @block.tensor
        def _(pe):
            pe.wait_ge(consts, 16 * len(loads))
            for k in range(KH):
                last = nc.tensor.matmul(ps[:, 2, 0:E], t["mean_w"][:], t["gate_w"][:, k, :], start=(k == 0),
                                        stop=(k == KH - 1))
            last.then_inc(mean_done, 1)
            pe.wait_ge(centred, 1)

            def group(n, i, first):
                pe.wait_ge(loaded[i], n * 16 + 16)
                if not first:
                    pe.wait_ge(read, n * 2 + i - 1)
                for j in range(PER):
                    for k in range(KH):
                        last = nc.tensor.matmul(ps[:, i, j * E:(j + 1) * E], xt[i][:, k, j * P:(j + 1) * P],
                                                t["gate_c"][:, k, :], start=(k == 0), stop=(k == KH - 1))
                last.then_inc(made, 1)

            for i in range(2):
                group(0, i, True)
            with pe.Fori(1, TOK // GROUP // 2) as n:
                for i in range(2):
                    group(n, i, False)


def memory_attention(nc, sems, ctx, ps, t, x_dram, out_dram, d):

    def sem(n):
        return sems[n]

    def sb(n, shape, dt=F32):
        return ctx.enter_context(nc.sbuf_tensor(f"att_{n}", shape, dt))

    def two(n, shape):
        return [sb(f"{n}{i}", shape) for i in range(2)]

    HALF = B // 2
    HW = HALF * CH
    w_kv, w_qq, w_ae = sb("w_kv", [P, KH, P]), sb("w_qq", [P, KH, P]), sb("w_ae", [P, KH, P])
    w_gt = sb("w_gt", [P, KH, H + D])
    w_o = sb("w_o", [D, H])
    conv_kv, conv_q = sb("conv_kv", [P, TAPS + 1]), sb("conv_q", [P, TAPS + 1])
    b_ae, b_t, b_g, norm_g = sb("b_ae", [P, 1]), sb("b_t", [P, D]), sb("b_g", [P, H]), sb("norm_g", [P, H])
    mean_a, mean_e = sb("mean_a", [P, P]), sb("mean_e", [P, P])
    fold, fold_low = sb("fold", [P, D]), sb("fold_low", [P, D])
    x_norm = sb("x_norm", [P, B, H])
    stats, moments, var_eps, rstd = sb("stats", [P, B, 6]), sb("moments", [P, B, 2]), sb("var_eps", [P, B]), sb("rstd", [P, B])
    xT = sb("xT", [P, KH, BW])
    raw_kv, raw_q = sb("raw_kv", [P, B, TAPS - 1 + CH]), sb("raw_q", [P, B, TAPS - 1 + CH])
    keep, eta = sb("keep", [P, B, CH]), sb("eta", [P, B, CH])
    mom = sb("mom", [P, B, CH])
    sig_ae = mom[:].rearrange("p b n -> p (b n)")
    carry = sb("carry", [P, B, CH])
    theta_pre, theta_log = sb("theta_pre", [P, B, D]), sb("theta_log", [P, B, D])
    theta_sum = sb("theta_sum", [P, B])
    k_sq = sb("k_sq", [P, B, D])
    zeros = sb("zeros", [P, CH])
    ab_start = sb("ab_start", [P, 1])
    Q = sb("Q", [P, B, CH])
    KV, QAB = two("KV", [P, B, CH]), two("QAB", [P, B, CH])
    P1, M, AB = two("P1", [P, B, CH]), two("M", [P, B, CH]), two("AB", [P, B, CH])
    spare = sb("spare", [P, 1])
    KM, MIX = two("KM", [P, B, 2, D]), two("MIX", [P, B, P])
    GATE, ENDS = two("GATE", [P, B, H]), two("ENDS", [P, B, 2])
    THETA, KNORM = two("THETA", [P, B]), two("KNORM", [P, B])
    x_res = sb("x_res", [P, B, H])
    state, read_w = two("state", [P, B, 3 * D]), sb("read_w", [P, B, P])
    sig_h, hid, slope = sb("sig_h", [P, B, D]), sb("hid", [P, B, D]), sb("slope", [P, B, D])
    hid_m = sb("hid_m", [P, B, 2, D])
    squares = sb("squares", [P, 3, B, D])
    dpre, grad_w1, grad_w2 = sb("dpre", [P, B, D]), sb("grad_w1", [P, B, 2, D]), sb("grad_w2", [P, B, D])
    nsum = sb("nsum", [P, 3, B])
    n1, n2, n3, n4, n5, factor = (sb(f"n{i}", [P, B]) for i in range(6))
    hid2, hid2_ab = (sb(n, [P, B, CH]) for n in ("hid2", "hid2_ab"))
    sig_h2 = P2 = hid2
    retrieved = sb("retrieved", [D, B, CH])
    o_sq = squares[:].rearrange("p a b n -> p (a b n)")[:, 0:HALF * H].rearrange("p (b n) -> p b n", n=H)
    o_sum, o_mean, o_rs = sb("o_sum", [P, B]), sb("o_mean", [P, B]), sb("o_rs", [P, B])
    x2T = sb("x2T", [P, KH, BW])

    consts, folded = sem("consts"), sem("folded")
    x_loaded = sem("x_loaded")
    stats_done, moments_done, rstd_done, x_normed = sem("stats_done"), sem("moments_done"), sem("rstd_done"), sem("x_normed")
    var_done, n_clipped, powered = sem("var_done"), sem("n_clipped"), sem("powered")
    x_turned, x_turned_copied = sem("x_turned"), sem("x_turned_copied")
    kv_made, kv_copied, q_made, q_copied = sem("kv_made"), sem("kv_copied"), sem("q_made"), sem("q_copied")
    kv_conv, q_conv, halo_kv, halo_q = sem("kv_conv"), sem("q_conv"), sem("halo_kv"), sem("halo_q")
    ae_made, ae_sig, rates_made, keep_ready, eta_ready = (sem(n) for n in ("ae_made", "ae_sig", "rates_made", "keep_ready", "eta_ready"))
    mom_ready, carry_ready, m_ready, ab_ready, ends_ready = (sem(n) for n in ("mom_ready", "carry_ready", "m_ready", "ab_ready", "ends_ready"))
    qab_ready, mix_ready = sem("qab_ready"), sem("mix_ready")
    gate_made, gate_read = sem("gate_made"), sem("gate_read")
    t_abs, t_exp, t_ln, t_soft, t_sum, theta_ready = (sem(n) for n in ("t_abs", "t_exp", "t_ln", "t_soft", "t_sum", "theta_ready"))
    k_turned, k_squared, km_ready, knorm_ready = (sem(n) for n in ("k_turned", "k_squared", "km_ready", "knorm_ready"))
    qk_made, p1_ready = sem("qk_made"), sem("p1_ready")
    pre_made, sig_ready, hid_ready, tmp_ready, slope_ready = (sem(n) for n in ("pre_made", "sig_ready", "hid_ready", "tmp_ready", "slope_ready"))
    hid_turned, hid_turned_copied, hid_m_ready = sem("hid_turned"), sem("hid_turned_copied"), sem("hid_m_ready")
    res_made, dpre_ready, squared, nsum_ready, small = (sem(n) for n in ("res_made", "dpre_ready", "squared", "nsum_ready", "small"))
    grad_w1_ready, grad_w2_ready = sem("grad_w1_ready"), sem("grad_w2_ready")
    pre2_made, sig2_ready, hid2_ready, hid2_ab_ready = (sem(n) for n in ("pre2_made", "sig2_ready", "hid2_ready", "hid2_ab_ready"))
    hh_made, p2_ready, ret_made, ret_copied = (sem(n) for n in ("hh_made", "p2_ready", "ret_made", "ret_copied"))
    state_made, state_copied, state_turned, w2_copied, gram_made, gram_copied = (
        sem(n) for n in ("state_made", "state_copied", "state_turned", "w2_copied", "gram_made", "gram_copied"))
    o_made, o_squared, o_meaned, o_rs_ready, gated_ready = (sem(n) for n in ("o_made", "o_squared", "o_meaned", "o_rs_ready", "gated_ready"))
    res_loaded, x2_ready, x2_stored, x2_turned, x2_turned_copied = (
        sem(n) for n in ("res_loaded", "x2_ready", "x2_stored", "x2_turned", "x2_turned_copied"))
    lg_made, lg_read = sem("lg_made"), sem("lg_read")

    x_v = x_dram.rearrange("(b c t) h -> c t b h", b=B, t=CH)
    out_v = out_dram.rearrange("(b c t) h -> c t b h", b=B, t=CH)

    def kmajor(a):
        return a.rearrange("(k p) n -> p k n", p=P)

    def step_of(a, c):
        return a[bass.ds(c, 1), :, :, :].rearrange("o t b h -> t (o b) h")

    loads = [(w_kv[:], kmajor(d["w_kv"])), (w_qq[:], kmajor(d["w_qq"])), (w_ae[:], kmajor(d["w_ae"])),
             (w_gt[:], kmajor(d["w_gt"])), (w_o[:], d["w_o"]), (conv_kv[:], d["conv_kv"]), (conv_q[:], d["conv_q"]),
             (b_ae[:], d["b_ae"]), (b_t[:], d["b_t"]), (b_g[:], d["b_g"]), (norm_g[:], d["norm_g"]),
             (mean_a[:], d["mean_a"]), (mean_e[:], d["mean_e"]), (fold[:], d["fold"]), (fold_low[:], d["fold_low"]),
             (state[0][0:D, :, 0:D], d["w1T"]), (state[0][0:D, :, D:2 * D], d["w1T"]),
             (state[0][0:D, :, 2 * D:3 * D], d["w2T"]),
             (read_w[0:D, :, 0:D], d["w2T"]), (read_w[D:P, :, 0:D], d["minus_i"]), (ab_start[:], d["ab_start"])]

    A, BB, C, DD = (ps[:, 2 * i:2 * i + 2, :] for i in range(4))

    def wide(pair):
        return pair.rearrange("p a (b n) -> p (a b) n", n=CH)

    with nc.Block() as block:

        @block.sync
        def _(sp):
            def load_x(c):
                sp.dma_start(x_norm[:], step_of(x_v, c)).then_inc(x_loaded, 16)

            def load_res(c):
                sp.dma_start(x_res[:], step_of(x_v, c)).then_inc(res_loaded, 16)

            def store(c):
                sp.wait_ge(x2_ready, 2 * c + 2)
                sp.dma_start(step_of(out_v, c), x_res[:]).then_inc(x2_stored, 16)

            load_x(0)
            for dst, src in loads:
                sp.dma_start(dst, src).then_inc(consts, 16)
            load_res(0)
            with sp.Fori(0, NCH - 1) as c:
                store(c)
                sp.wait_ge(x2_stored, 16 * c + 16)
                sp.wait_ge(x2_turned, 2 * c + 2)
                load_res(c + 1)
            store(NCH - 1)
            sp.wait_ge(x2_stored, 16 * NCH)

        @block.gpsimd
        def _(pool):
            g = nc.gpsimd

            def prep(c, par, first):
                pool.wait_ge(ab_ready, c + 1)
                pool.wait_ge(q_conv, TAPS * c + TAPS)
                if not first:
                    pool.wait_ge(state_made, c - 1)
                g.tensor_tensor(QAB[par][:], Q[:], AB[par][:], ALU.mult).then_inc(qab_ready, 1)
                g.tensor_tensor(MIX[par][:, :, 0:D], bc(fold[:].unsqueeze(1), [P, B, D]),
                                bc(AB[par][:, :, CH - 1:CH], [P, B, D]), ALU.mult).then_inc(mix_ready, 1)
                g.tensor_tensor(MIX[par][:, :, D:P], bc(fold_low[:].unsqueeze(1), [P, B, D]),
                                bc(carry[:, :, CH - 1:CH], [P, B, D]), ALU.mult).then_inc(mix_ready, 1)

            def hidden(c, par, first):
                pool.wait_ge(hid_ready, c + 1)
                if not first:
                    pool.wait_ge(state_made, c)
                g.tensor_tensor(hid_m[:], bc(hid[:].unsqueeze(2), [P, B, 2, D]),
                                bc(ENDS[par][:].unsqueeze(3), [P, B, 2, D]), ALU.mult).then_inc(hid_m_ready, 1)

            def norm(c):
                pool.wait_ge(var_done, c + 1)
                g.tensor_tensor(rstd[:], var_eps[:], t["minus_half"][:, 0:B], ALU.pow).then_inc(rstd_done, 1)

            def gradient_norm(c):
                pool.wait_ge(n_clipped, c + 1)
                g.tensor_tensor(n5[:], n4[:], t["minus_half"][:, 0:B], ALU.pow).then_inc(powered, 1)

            def residual(c, par):
                pool.wait_ge(res_loaded, 16 * c + 16)
                for h in range(2):
                    n = slice(h * HALF, (h + 1) * HALF)
                    pool.wait_ge(o_meaned, 2 * c + h + 1)
                    g.tensor_tensor(o_rs[:, n], o_mean[:, n], t["minus_half"][:, n], ALU.pow).then_inc(o_rs_ready, 1)
                    pool.wait_ge(gated_ready, 2 * c + h + 1)
                    g.tensor_tensor(x_res[:, n, :], x_res[:, n, :], GATE[par][:, n, :], ALU.add).then_inc(x2_ready, 1)

            def step(c, par, first, last, norm_too=True):
                pool.wait_ge(ends_ready, c + 1)
                hidden(c, par, first)
                if norm_too:
                    norm(c + 2)
                gradient_norm(c)
                if not last:
                    prep(c + 1, 1 - par, first)
                residual(c, par)

            norm(0)
            prep(0, 0, True)
            norm(1)
            step(0, 0, True, False)
            with pool.Fori(0, NCH // 2 - 2) as i:
                step(i * 2 + 1, 1, False, False)
                step(i * 2 + 2, 0, False, False)
            step(NCH - 3, 1, False, False)
            step(NCH - 2, 0, False, False, norm_too=False)
            step(NCH - 1, 1, False, True, norm_too=False)

        @block.vector
        def _(dve):
            v = nc.vector

            def start():
                dve.wait_ge(consts, 16 * len(loads))
                v.memset(zeros[:], 0.0).then_inc(folded, 1)
                v.memset(spare[:], 0.0).then_inc(lg_read, 1)
                v.memset(raw_kv[:, :, 0:TAPS - 1], 0.0).then_inc(halo_kv, 1)
                v.memset(raw_q[:, :, 0:TAPS - 1], 0.0).then_inc(halo_q, 1)
                v.memset(carry[0:D, :, :], 0.0).then_inc(folded, 1)
                v.memset(state[0][D:P, :, :], 0.0).then_inc(folded, 1)
                v.tensor_tensor(w_gt[:, :, 0:H], w_gt[:, :, 0:H], bc(norm_g[:].unsqueeze(1), [P, KH, H]),
                                ALU.mult).then_inc(folded, 1)
                v.tensor_tensor(b_g[:], b_g[:], norm_g[:], ALU.mult).then_inc(folded, 1)
                dve.wait_ge(folded, 5)

            def moments_of(c):
                dve.wait_ge(x_loaded, 16 * c + 16)
                for b in range(B):
                    v.bn_stats(stats[:, b, :], x_norm[:, b, :]).then_inc(stats_done, 1)
                dve.wait_ge(stats_done, B * c + B)
                v.memset(spare[:], 0.0)
                for b in range(B):
                    v.bn_aggr(moments[:, b, :], stats[:, b, :]).then_inc(moments_done, 1)
                dve.wait_ge(moments_done, B * c + B)
                v.tensor_scalar(var_eps[:], moments[:, :, 1], LN_EPS, None, ALU.add).then_inc(var_done, 1)

            def normalise(c):
                dve.wait_ge(rstd_done, c + 1)
                for b in range(B):
                    v.tensor_scalar(x_norm[:, b, :], x_norm[:, b, :], moments[:, b, 0:1], rstd[:, b:b + 1],
                                    ALU.subtract, ALU.mult).then_inc(x_normed, 1)

            def convolve(c, par, first, very_first=False):
                dve.wait_ge(kv_copied, c + 1)
                dve.wait_ge(q_copied, c + 1)
                if not first:
                    dve.wait_ge(state_made, c - 1)
                    dve.wait_ge(hh_made, c - 1)
                if not very_first:
                    dve.wait_ge(qab_ready, c)
                    dve.wait_ge(qk_made, c)
                lanes = [(KV[par], raw_kv, conv_kv, kv_conv), (Q, raw_q, conv_q, q_conv)]
                for y, x, w, done in lanes:
                    v.tensor_scalar(y[:], x[:, :, TAPS - 1:TAPS - 1 + CH], w[:, TAPS - 1:TAPS], w[:, TAPS:TAPS + 1],
                                    ALU.mult, ALU.add).then_inc(done, 1)
                for n, j in enumerate(range(TAPS - 2, -1, -1)):
                    for y, x, w, done in lanes:
                        dve.wait_ge(done, TAPS * c + n + 1)
                        v.scalar_tensor_tensor(y[:], x[:, :, j:j + CH], w[:, j:j + 1], y[:], ALU.mult,
                                               ALU.add).then_inc(done, 1)
                dve.wait_ge(kv_conv, TAPS * c + TAPS)
                v.tensor_copy(raw_kv[:, :, 0:TAPS - 1], raw_kv[:, :, CH:CH + TAPS - 1]).then_inc(halo_kv, 1)
                dve.wait_ge(q_conv, TAPS * c + TAPS)
                v.tensor_copy(raw_q[:, :, 0:TAPS - 1], raw_q[:, :, CH:CH + TAPS - 1]).then_inc(halo_q, 1)

            def momentum_scans(c, first):
                dve.wait_ge(eta_ready, c + 1)
                for b in range(B):
                    v.tensor_tensor_scan(mom[:, b, :], eta[:, b, :], t["ident"][:], 0.0, ALU.mult,
                                         ALU.add).then_inc(mom_ready, 1)
                if not first:
                    dve.wait_ge(mix_ready, 2 * c)
                for b in range(B):
                    v.tensor_tensor_scan(carry[D:P, b, :], eta[D:P, b, :], zeros[D:P, :], 1.0, ALU.mult,
                                         ALU.add).then_inc(carry_ready, 1)

            def memory_scans(c, par, first):
                dve.wait_ge(keep_ready, c + 1)
                dve.wait_ge(mom_ready, B * c + B)
                for b in range(B):
                    v.tensor_tensor_scan(M[par][:, b, :], keep[:, b, :], mom[:, b, :], 0.0, ALU.mult,
                                         ALU.add).then_inc(m_ready, 1)
                dve.wait_ge(carry_ready, B * c + B)
                for b in range(B):
                    last = v.tensor_tensor_scan(AB[par][:, b, :], keep[:, b, :], carry[:, b, :], ab_start[:, 0:1],
                                                ALU.mult, ALU.add)
                last.then_inc(ab_ready, 1)
                dve.wait_ge(m_ready, B * c + B)
                if not first:
                    dve.wait_ge(hid_m_ready, c - 1)
                v.tensor_copy(ENDS[par][:, :, 0:1], M[par][:, :, CH - 1:CH])
                v.tensor_copy(ENDS[par][:, :, 1:2], mom[:, :, CH - 1:CH]).then_inc(ends_ready, 1)

            def gates(c, par, pairs, first):
                if not first:
                    dve.wait_ge(x2_ready, 2 * c - 2)
                for i in pairs:
                    dve.wait_ge(gate_made, 4 * c + i + 1)
                    src = A if i % 2 else BB
                    v.tensor_tensor(GATE[par][:, 2 * i:2 * i + 2, :], src[:, :, 0:H],
                                    bc(b_g[:].unsqueeze(1), [P, 2, H]), ALU.add)
                    v.tensor_tensor(theta_pre[:, 2 * i:2 * i + 2, :], src[:, :, H:H + D],
                                    bc(b_t[:].unsqueeze(1), [P, 2, D]), ALU.add).then_inc(gate_read, 1)

            def thetas(c, par):
                dve.wait_ge(t_ln, c + 1)
                v.scalar_tensor_tensor(theta_log[:], theta_pre[:], 0.0, theta_log[:], ALU.max,
                                       ALU.add).then_inc(t_soft, 1)
                dve.wait_ge(t_soft, c + 1)
                v.tensor_reduce(theta_sum[:], theta_log[:], AX.X, ALU.add).then_inc(t_sum, 1)
                dve.wait_ge(t_sum, c + 1)
                v.tensor_scalar(THETA[par][:], theta_sum[:], -0.1 * 0.2 / D, None, ALU.mult).then_inc(theta_ready, 1)

            def keys(c, par, first):
                dve.wait_ge(k_turned, c + 1)
                dve.wait_ge(ends_ready, c + 1)
                v.tensor_tensor(KM[par][:], bc(wide(BB)[:, :, 0:D].unsqueeze(2), [P, B, 2, D]),
                                bc(ENDS[par][:].unsqueeze(3), [P, B, 2, D]), ALU.mult).then_inc(km_ready, 1)
                dve.wait_ge(k_squared, c + 1)
                v.tensor_reduce(KNORM[par][:], k_sq[:], AX.X, ALU.add).then_inc(knorm_ready, 1)
                dve.wait_ge(qk_made, c + 1)
                v.tensor_tensor(P1[par][:], wide(A), M[par][:], ALU.mult).then_inc(p1_ready, 1)

            def hidden(c, first):
                dve.wait_ge(sig_ready, c + 1)
                if not first:
                    dve.wait_ge(hid_m_ready, c)
                pre = C[:, 0, :].rearrange("p (b n) -> p b n", n=D)
                v.tensor_tensor(hid[:], pre, sig_h[:], ALU.mult).then_inc(hid_ready, 1)
                dve.wait_ge(hid_ready, c + 1)
                v.scalar_tensor_tensor(slope[:], sig_h[:], 1.0, hid[:], ALU.subtract, ALU.mult).then_inc(tmp_ready, 1)
                dve.wait_ge(tmp_ready, c + 1)
                v.tensor_tensor(slope[:], sig_h[:], slope[:], ALU.subtract).then_inc(slope_ready, 1)

            def gradient_norms(c, par):
                dve.wait_ge(res_made, c + 1)
                dve.wait_ge(slope_ready, c + 1)
                v.tensor_tensor(dpre[:], wide(C)[:, :, D:P], slope[:], ALU.mult).then_inc(dpre_ready, 1)
                dve.wait_ge(squared, 3 * c + 3)
                v.tensor_reduce(nsum[:], squares[:], AX.X, ALU.add).then_inc(nsum_ready, 1)
                dve.wait_ge(nsum_ready, c + 1)
                dve.wait_ge(knorm_ready, c + 1)
                v.tensor_tensor(n1[:], nsum[:, 0, :], nsum[:, 1, :], ALU.mult).then_inc(small, 1)
                v.tensor_tensor(n2[:], nsum[:, 2, :], KNORM[par][:], ALU.mult).then_inc(small, 1)
                dve.wait_ge(small, 4 * c + 2)
                v.tensor_tensor(n3[:], n1[:], n2[:], ALU.add).then_inc(small, 1)
                dve.wait_ge(small, 4 * c + 3)
                v.tensor_scalar(n4[:], n3[:], 0.04, EPS * EPS, ALU.mult, ALU.max).then_inc(n_clipped, 1)

            def gradients(c, par):
                dve.wait_ge(powered, c + 1)
                dve.wait_ge(theta_ready, c + 1)
                v.scalar_tensor_tensor(factor[:], n5[:], 1.0, THETA[par][:], ALU.min, ALU.mult).then_inc(small, 1)
                dve.wait_ge(small, 4 * c + 4)
                v.tensor_tensor(grad_w1[:], bc(dpre[:].unsqueeze(2), [P, B, 2, D]),
                                bc(factor[:].unsqueeze(2).unsqueeze(3), [P, B, 2, D]),
                                ALU.mult).then_inc(grad_w1_ready, 1)
                v.tensor_tensor(grad_w2[:], wide(C)[:, :, 0:D], bc(factor[:].unsqueeze(2), [P, B, D]),
                                ALU.mult).then_inc(grad_w2_ready, 1)

            def second_hidden(c, par):
                dve.wait_ge(sig2_ready, c + 1)
                v.tensor_tensor(hid2[:], wide(DD), sig_h2[:], ALU.mult).then_inc(hid2_ready, 1)
                dve.wait_ge(hid2_ready, c + 1)
                v.tensor_tensor(hid2_ab[:], hid2[:], AB[par][:], ALU.mult).then_inc(hid2_ab_ready, 1)

            def second_scores(c, par):
                dve.wait_ge(hh_made, c + 1)
                dve.wait_ge(hid2_ab_ready, c + 1)
                v.tensor_tensor(P2[:], wide(DD), M[par][:], ALU.mult).then_inc(p2_ready, 1)

            def gated_output(c, par, h):
                n = slice(h * HALF, (h + 1) * HALF)
                dve.wait_ge(o_squared, B * c + HALF * (h + 1))
                v.tensor_scalar(o_mean[:, n], o_sum[:, n], 1.0 / H, EPS, ALU.mult, ALU.add).then_inc(o_meaned, 1)
                dve.wait_ge(o_rs_ready, 2 * c + h + 1)
                src = (BB if h else DD).rearrange("p a (b n) -> p (a b) n", n=H)
                for b in range(HALF):
                    bb = h * HALF + b
                    last = v.scalar_tensor_tensor(GATE[par][:, bb, :], src[:, b, :], o_rs[:, bb:bb + 1],
                                                  GATE[par][:, bb, :], ALU.mult, ALU.mult)
                last.then_inc(gated_ready, 1)

            def logits(c):
                dve.wait_ge(lg_made, c + 1)
                v.tensor_copy(t["logits"][:].rearrange("p (b c) e -> p b c e", c=NCH)[:, :, bass.ds(c, 1), :],
                              C[:, 0, 0:B * E].rearrange("p (b o e) -> p b o e", o=1, e=E)).then_inc(lg_read, 1)

            def step(c, par, first, last, norm_too=True):
                hidden(c, first)
                if norm_too:
                    moments_of(c + 2)
                gradient_norms(c, par)
                if norm_too:
                    normalise(c + 2)
                gradients(c, par)
                if not last:
                    convolve(c + 1, 1 - par, first)
                second_hidden(c, par)
                if not last:
                    momentum_scans(c + 1, False)
                second_scores(c, par)
                if not last:
                    memory_scans(c + 1, 1 - par, first)
                    gates(c + 1, 1 - par, range(4), first)
                if not first:
                    logits(c - 1)
                if not last:
                    keys(c + 1, 1 - par, False)
                    thetas(c + 1, 1 - par)
                gated_output(c, par, 0)
                gated_output(c, par, 1)

            start()
            moments_of(0)
            normalise(0)
            convolve(0, 0, True, True)
            momentum_scans(0, True)
            memory_scans(0, 0, True)
            gates(0, 0, range(4), True)
            keys(0, 0, True)
            thetas(0, 0)
            moments_of(1)
            normalise(1)
            step(0, 0, True, False)
            with dve.Fori(0, NCH // 2 - 2) as i:
                step(i * 2 + 1, 1, False, False)
                step(i * 2 + 2, 0, False, False)
            step(NCH - 3, 1, False, False)
            step(NCH - 2, 0, False, False, norm_too=False)
            step(NCH - 1, 1, False, True, norm_too=False)
            logits(NCH - 1)

        @block.scalar
        def _(act):
            s = nc.scalar

            def turned(c, first, load=True):
                if not first:
                    act.wait_ge(gate_made, 4 * c)
                for h, src in enumerate((A, BB)):
                    act.wait_ge(x_turned, 2 * c + h + 1)
                    if h and load:
                        act.dma_start(x_norm[:], step_of(x_v, c + 1)).then_inc(x_loaded, 16)
                    s.copy(xT[:, :, h * HW:(h + 1) * HW], src).then_inc(x_turned_copied, 1)

            def kv_projection(c):
                act.wait_ge(halo_kv, c + 1)
                act.wait_ge(kv_made, c + 1)
                s.copy(raw_kv[:, :, TAPS - 1:], wide(A)).then_inc(kv_copied, 1)

            def q_projection(c):
                act.wait_ge(halo_q, c + 1)
                act.wait_ge(q_made, c + 1)
                s.copy(raw_q[:, :, TAPS - 1:], wide(BB)).then_inc(q_copied, 1)

            def sigmoids(c, first):
                act.wait_ge(ae_made, c + 1)
                if not first:
                    act.wait_ge(ends_ready, c)
                s.activation(sig_ae, A.rearrange("p a n -> p (a n)"), ACT.Sigmoid,
                             bias=b_ae[:, 0:1]).then_inc(ae_sig, 1)

            def rates(c, first):
                act.wait_ge(rates_made, 2 * c + 1)
                if not first:
                    act.wait_ge(ab_ready, c)
                s.activation(keep[:], wide(BB), ACT.Copy, bias=1.0, scale=-0.1).then_inc(keep_ready, 1)
                act.wait_ge(rates_made, 2 * c + 2)
                s.activation(eta[:], wide(A), ACT.Copy, bias=0.05, scale=0.9).then_inc(eta_ready, 1)

            def thetas(c, first):
                act.wait_ge(gate_read, 4 * c + 4)
                s.activation(theta_log[:], theta_pre[:], ACT.Abs).then_inc(t_abs, 1)
                act.wait_ge(t_abs, c + 1)
                s.activation(theta_log[:], theta_log[:], ACT.Exp, scale=-1.0).then_inc(t_exp, 1)
                act.wait_ge(t_exp, c + 1)
                s.activation(theta_log[:], theta_log[:], ACT.Ln, bias=1.0).then_inc(t_ln, 1)

            def keys(c, first):
                act.wait_ge(km_ready, c + 1)
                if not first:
                    act.wait_ge(knorm_ready, c)
                s.activation(k_sq[:], wide(BB)[:, :, 0:D], ACT.Square).then_inc(k_squared, 1)

            def hidden(c, first):
                act.wait_ge(pre_made, c + 1)
                if not first:
                    act.wait_ge(slope_ready, c)
                s.activation(sig_h[:], C[:, 0, :].rearrange("p (b n) -> p b n", n=D),
                             ACT.Sigmoid).then_inc(sig_ready, 1)

            def hidden_turned(c, par, first):
                act.wait_ge(hid_turned, c + 1)
                s.copy(KV[par][0:D, :, :], wide(C)[0:D, :, :]).then_inc(hid_turned_copied, 1)
                if not first:
                    act.wait_ge(o_squared, B * c)
                s.activation(squares[:, 0, :, :], hid[:], ACT.Square).then_inc(squared, 1)

            def gradients(c):
                act.wait_ge(dpre_ready, c + 1)
                s.activation(squares[:, 1, :, :], wide(C)[:, :, 0:D], ACT.Square).then_inc(squared, 1)
                s.activation(squares[:, 2, :, :], dpre[:], ACT.Square).then_inc(squared, 1)

            def second_hidden(c):
                act.wait_ge(pre2_made, c + 1)
                s.activation(sig_h2[:], wide(DD), ACT.Sigmoid).then_inc(sig2_ready, 1)

            def retrieve(c):
                act.wait_ge(ret_made, c + 1)
                s.copy(retrieved[:], wide(DD)[0:D, :, :]).then_inc(ret_copied, 1)

            def new_state(c, par):
                act.wait_ge(state_made, c + 1)
                new = wide(C)
                s.copy(state[1 - par][:, :, 0:D], new[:, :, 0:D])
                s.copy(state[1 - par][:, :, D:3 * D], new).then_inc(state_copied, 1)
                s.copy(read_w[0:D, :, 0:D], new[0:D, :, D:P]).then_inc(state_copied, 1)

            def new_turned(n):
                act.wait_ge(state_turned, n + 1)
                s.mul(read_w[D:P, :, D:P], wide(C)[D:P, :, 0:D], -1.0).then_inc(w2_copied, 1)

            def new_gram(n):
                act.wait_ge(gram_made, n + 1)
                s.copy(read_w[0:D, :, D:P],
                       C[0:D, 0, :].rearrange("p (b n) -> p b n", n=D)).then_inc(gram_copied, 1)

            def output_norms(c, first, h):
                act.wait_ge(o_made, 2 * c + h + 1)
                if h or not first:
                    act.wait_ge(o_squared, B * c + HALF * h)
                if not first:
                    act.wait_ge(o_meaned, 2 * c)
                o = (BB if h else DD).rearrange("p a (b n) -> p (a b) n", n=H)
                for b in range(HALF):
                    bb = h * HALF + b
                    s.activation(o_sq[:, b, :], o[:, b, :], ACT.Square,
                                 accum_out=o_sum[:, bb:bb + 1]).then_inc(o_squared, 1)

            def result_turned(c, h):
                act.wait_ge(x2_turned, 2 * c + h + 1)
                s.copy(x2T[:, :, h * HW:(h + 1) * HW], DD).then_inc(x2_turned_copied, 1)

            def step(c, par, first, last, load=True):
                hidden(c, first)
                if not last:
                    turned(c + 1, False, load)
                hidden_turned(c, par, first)
                if not last:
                    kv_projection(c + 1)
                gradients(c)
                if not first:
                    result_turned(c - 1, 0)
                if not last:
                    q_projection(c + 1)
                if not first:
                    result_turned(c - 1, 1)
                if not last:
                    sigmoids(c + 1, False)
                new_state(c, par)
                second_hidden(c)
                new_turned(c + 1)
                if not last:
                    rates(c + 1, False)
                new_gram(c + 1)
                retrieve(c)
                if not last:
                    thetas(c + 1, False)
                    keys(c + 1, False)
                output_norms(c, first, 0)
                output_norms(c, first, 1)

            new_turned(0)
            new_gram(0)
            turned(0, True)
            kv_projection(0)
            q_projection(0)
            sigmoids(0, True)
            rates(0, True)
            keys(0, True)
            thetas(0, True)
            step(0, 0, True, False)
            with act.Fori(0, NCH // 2 - 2) as i:
                step(i * 2 + 1, 1, False, False)
                step(i * 2 + 2, 0, False, False)
            step(NCH - 3, 1, False, False)
            step(NCH - 2, 0, False, False, load=False)
            step(NCH - 1, 1, False, True)
            result_turned(NCH - 1, 0)
            result_turned(NCH - 1, 1)

        @block.tensor
        def _(pe):
            mm = nc.tensor.matmul

            def turn_x(c, first, out_before=True):
                for h, dst in enumerate((A, BB)):
                    pe.wait_ge(x_normed, B * c + HALF * (h + 1))
                    if not first:
                        pe.wait_ge(p1_ready if h == 0 else knorm_ready, c)
                    if h == 1 and not first and out_before:
                        pe.wait_ge(gated_ready, 2 * c - 2)
                    for b in range(HALF):
                        for k in range(KH):
                            last = nc.tensor.transpose(dst[:, k, b * CH:(b + 1) * CH],
                                                       x_norm[:, h * HALF + b, k * P:(k + 1) * P], t["ident"][:])
                    last.then_inc(x_turned, 1)

            def project(c, dst, w, done):
                for h in range(2):
                    for k in range(KH):
                        last = mm(dst[:, h, :], w[:, k, :], xT[:, k, h * HW:(h + 1) * HW], start=(k == 0),
                                  stop=(k == KH - 1))
                last.then_inc(done, 1)

            def kv_projection(c):
                pe.wait_ge(x_turned_copied, 2 * c + 2)
                project(c, A, w_kv, kv_made)

            def q_projection(c):
                project(c, BB, w_qq, q_made)

            def ae_projection(c):
                pe.wait_ge(kv_copied, c + 1)
                project(c, A, w_ae, ae_made)

            def rates(c):
                pe.wait_ge(ae_sig, c + 1)
                pe.wait_ge(q_copied, c + 1)
                for dst, w in ((BB, mean_a), (A, mean_e)):
                    for h in range(2):
                        last = mm(dst[:, h, :], w[:], sig_ae[:, h * HW:(h + 1) * HW], start=True, stop=True)
                    last.then_inc(rates_made, 1)

            def gates(c, pairs):
                for i in pairs:
                    dst = A if i % 2 else BB
                    if i == 0:
                        pe.wait_ge(keep_ready, c + 1)
                    elif i == 1:
                        pe.wait_ge(eta_ready, c + 1)
                    else:
                        pe.wait_ge(gate_read, 4 * c + i - 1)
                    for j in range(2):
                        b = 2 * i + j
                        for k in range(KH):
                            last = mm(dst[:, j, 0:H + D], xT[:, k, b * CH:(b + 1) * CH], w_gt[:, k, :],
                                      start=(k == 0), stop=(k == KH - 1))
                    last.then_inc(gate_made, 1)

            def keys(c, par):
                pe.wait_ge(kv_conv, TAPS * c + TAPS)
                pe.wait_ge(gate_read, 4 * c + 3)
                for b in range(B):
                    last = nc.tensor.transpose(wide(BB)[:, b, :], KV[par][:, b, :], t["ident"][:])
                last.then_inc(k_turned, 1)
                pe.wait_ge(q_conv, TAPS * c + TAPS)
                pe.wait_ge(gate_read, 4 * c + 4)
                for b in range(B):
                    last = mm(wide(A)[:, b, :], KV[par][0:D, b, :], Q[0:D, b, :], start=True, stop=True)
                last.then_inc(qk_made, 1)

            def hidden(c, par, first):
                pe.wait_ge(kv_conv, TAPS * c + TAPS)
                pe.wait_ge(gram_copied, c + 1)
                if not first:
                    pe.wait_ge(state_copied, 2 * c)
                    pe.wait_ge(lg_read, c)
                for b in range(B):
                    last = mm(C[:, 0, b * D:(b + 1) * D], KV[par][0:D, b, :], state[par][0:D, b, 0:D], start=True, stop=True)
                last.then_inc(pre_made, 1)

            def hidden_turned(c):
                pe.wait_ge(consts, 16 * len(loads))
                pe.wait_ge(hid_ready, c + 1)
                for b in range(B):
                    last = nc.tensor.transpose(wide(C)[0:D, b, :], hid[:, b, :], t["ident"][:])
                last.then_inc(hid_turned, 1)

            def residual(c, par):
                pe.wait_ge(hid_turned_copied, c + 1)
                pe.wait_ge(gram_copied, c + 1)
                for b in range(B):
                    last = mm(wide(C)[:, b, :], KV[par][:, b, :], read_w[:, b, :], start=True, stop=True)
                last.then_inc(res_made, 1)

            def second_hidden(c, par, first):
                pe.wait_ge(grad_w1_ready, c + 1)
                pe.wait_ge(p1_ready, c + 1)
                pe.wait_ge(qab_ready, c + 1)
                if not first:
                    pe.wait_ge(x2_turned_copied, 2 * c)
                for b in range(B):
                    mm(wide(DD)[:, b, :], state[par][:, b, 0:2 * D], QAB[par][:, b, :], start=True, stop=False)
                    last = mm(wide(DD)[:, b, :], grad_w1[:, b, :, :].rearrange("p a n -> p (a n)"), P1[par][:, b, :],
                              start=False, stop=True)
                last.then_inc(pre2_made, 1)

            def second_scores(c, par):
                pe.wait_ge(hid2_ready, c + 1)
                for b in range(B):
                    last = mm(wide(DD)[:, b, :], KV[par][0:D, b, :], hid2[0:D, b, :], start=True, stop=True)
                last.then_inc(hh_made, 1)

            def retrieve(c, par):
                pe.wait_ge(hid2_ab_ready, c + 1)
                pe.wait_ge(p2_ready, c + 1)
                for b in range(B):
                    mm(wide(DD)[0:D, b, :], state[par][:, b, 2 * D:3 * D], hid2_ab[:, b, :], start=True, stop=False)
                    last = mm(wide(DD)[0:D, b, :], grad_w2[:, b, :], P2[:, b, :], start=False, stop=True)
                last.then_inc(ret_made, 1)

            def new_state(c, par):
                pe.wait_ge(mix_ready, 2 * c + 2)
                pe.wait_ge(km_ready, c + 1)
                pe.wait_ge(hid_m_ready, c + 1)
                pe.wait_ge(grad_w2_ready, c + 1)
                for b in range(B):
                    dst = wide(C)[:, b, :]
                    mm(dst, MIX[par][:, b, :], state[par][:, b, D:3 * D], start=True, stop=False, skip_group_check=True)
                    mm(dst[:, 0:D], KM[par][:, b, :, :].rearrange("p a n -> p (a n)"), grad_w1[:, b, 0, :],
                       start=False, stop=False, skip_group_check=True)
                    last = mm(dst[:, D:P], hid_m[:, b, :, :].rearrange("p a n -> p (a n)"), grad_w2[:, b, :],
                              start=False, stop=True, skip_group_check=True)
                last.then_inc(state_made, 1)

            def turn_state(st):
                for b in range(B):
                    last = nc.tensor.transpose(wide(C)[:, b, :], st[:, b, D:3 * D], t["ident"][:])
                last.then_inc(state_turned, 1)

            def gram(n):
                pe.wait_ge(consts, 16 * len(loads))
                pe.wait_ge(w2_copied, n + 1)
                for b in range(B):
                    w2 = read_w[D:P, b, D:P]
                    last = mm(C[0:D, 0, b * D:(b + 1) * D], w2, w2, start=True, stop=True)
                last.then_inc(gram_made, 1)

            def outputs(c, h, next_prep):
                if h == 0:
                    pe.wait_ge(ret_copied, c + 1)
                elif next_prep:
                    pe.wait_ge(knorm_ready, c + 2)
                dst = BB if h else DD
                for b in range(HALF):
                    last = mm(dst[:, b // 2, (b % 2) * H:(b % 2 + 1) * H], retrieved[:, h * HALF + b, :], w_o[:],
                              start=True, stop=True)
                last.then_inc(o_made, 1)

            def turn_result(c, h):
                pe.wait_ge(x2_ready, 2 * c + h + 1)
                if h:
                    pe.wait_ge(x2_turned_copied, 2 * c + 1)
                for b in range(HALF):
                    for k in range(KH):
                        last = nc.tensor.transpose(DD[:, k, b * CH:(b + 1) * CH],
                                                   x_res[:, h * HALF + b, k * P:(k + 1) * P], t["ident"][:])
                last.then_inc(x2_turned, 1)

            def logits(c, grams):
                pe.wait_ge(x2_turned_copied, 2 * c + 2)
                pe.wait_ge(gram_copied, grams)
                for b in range(B):
                    for k in range(KH):
                        last = mm(C[:, 0, b * E:(b + 1) * E], x2T[:, k, b * CH:(b + 1) * CH], t["gate_c"][:, k, :],
                                  start=(k == 0), stop=(k == KH - 1))
                last.then_inc(lg_made, 1)

            def step(c, par, first, last):
                hidden(c, par, first)
                if not last:
                    turn_x(c + 1, False, not first)
                hidden_turned(c)
                if not last:
                    kv_projection(c + 1)
                residual(c, par)
                if not first:
                    turn_result(c - 1, 0)
                if not last:
                    q_projection(c + 1)
                if not first:
                    turn_result(c - 1, 1)
                if not last:
                    ae_projection(c + 1)
                new_state(c, par)
                second_hidden(c, par, first)
                pe.wait_ge(state_copied, 2 * c + 2)
                turn_state(state[1 - par])
                if not last:
                    rates(c + 1)
                gram(c + 1)
                second_scores(c, par)
                if not last:
                    gates(c + 1, (0, 1))
                retrieve(c, par)
                if not last:
                    gates(c + 1, (2, 3))
                    keys(c + 1, 1 - par)
                if not first:
                    logits(c - 1, c + 2)
                outputs(c, 0, not last)
                outputs(c, 1, not last)

            pe.wait_ge(consts, 16 * len(loads))
            pe.wait_ge(folded, 5)
            turn_state(state[0])
            gram(0)
            turn_x(0, True)
            kv_projection(0)
            q_projection(0)
            ae_projection(0)
            rates(0)
            gates(0, range(4))
            keys(0, 0)
            step(0, 0, True, False)
            with pe.Fori(0, NCH // 2 - 1) as i:
                step(i * 2 + 1, 1, False, False)
                step(i * 2 + 2, 0, False, False)
            step(NCH - 1, 1, False, True)
            turn_result(NCH - 1, 0)
            turn_result(NCH - 1, 1)
            pe.wait_ge(lg_read, NCH)
            logits(NCH - 1, NCH + 1)


def build(nc, d):
    with ExitStack() as sems, ExitStack() as whole:
        def keep(n, shape, dt=F32):
            return whole.enter_context(nc.sbuf_tensor(n, shape, dt))

        ps = whole.enter_context(nc.psum_tensor("ps", [P, 8, 512], F32))
        t = {
            "ident": keep("ident", [P, P]), "iota": keep("iota", [P, P]), "partition": keep("partition", [P, 1]),
            "rank_of_expert": keep("rank_of_expert", [P, E]), "gate_w": keep("gate_w", [P, KH, E]),
            "gate_c": keep("gate_c", [P, KH, E]), "mean_w": keep("mean_w", [P, P]),
            "upper": keep("upper", [P, P], BF16), "ones_bf": keep("ones_bf", [P, P], BF16),
            "ones_row": keep("ones_row", [P, P]), "minus_half": keep("minus_half", [P, B]), "logits": keep("logits", [P, NT, E]),
            "gather_index": keep("gather_index", [P, ST], I32), "scatter_index": keep("scatter_index", [P, ST], I32),
            "w1": d["w1"], "w2": d["w2"],
        }
        for n in ("ident", "iota", "partition", "rank", "gate_w", "upper", "mean_w", "ones"):
            t["d_" + n] = d[n]
        x1 = nc.dram_tensor("x1", (TOK, H), F32, kind="Internal").ap()
        first = Semaphores(nc, sems, "first_")
        moe = Semaphores(nc, sems, "moe_")
        att = Semaphores(nc, sems, "att_")
        with ExitStack() as ctx:
            first_logits(nc, first, ctx, ps[:], t, d["x"], d["xT"], x1)
        with ExitStack() as ctx:
            route(nc, moe, ctx, ps[:], t, "route1")
        with ExitStack() as ctx:
            experts(nc, moe, ctx, ps[:], t, "moe1", d["x"], x1)
        with ExitStack() as ctx:
            memory_attention(nc, att, ctx, ps[:], t, x1, d["out"], d)
        with nc.Block() as block:
            @block.sync
            def _(sp):
                for n, s in moe.items():
                    if not n.startswith("pool_dma"):
                        sp.sem_clear(s)
        with ExitStack() as ctx:
            route(nc, moe, ctx, ps[:], t, "route2")
        with ExitStack() as ctx:
            experts(nc, moe, ctx, ps[:], t, "moe2", d["out"], d["out"])


def kernel(**inputs):
    import numpy as np
    import concourse.bacc as bacc
    from concourse.bass_utils import run_bass_kernel_spmd

    a = {k.replace("L0_attn_", ""): np.asarray(v) for k, v in inputs.items()}
    x = a["hidden"].reshape(TOK, H)
    f = np.float32
    eye = np.eye(P, dtype=f)

    def over_partitions(row):
        return np.broadcast_to(row[None, :], (P, row.shape[0]))

    low = np.arange(P) >= D
    arrays = {
        "x": x, "xT": x.T,
        "gate_w": a["L0_ffn_gate_w"], "w1": a["L0_ffn_w1"], "w2": a["L0_ffn_w2"],
        "w_kv": np.concatenate([a["Wk"].T, a["Wv"].T], 1), "w_qq": np.concatenate([a["Wq"].T, a["Wq"].T], 1),
        "w_ae": np.concatenate([a["aW"].T, a["eW"].T], 1), "w_gt": np.concatenate([a["gW"].T, a["tW"].T], 1),
        "w_o": a["Wo"].T,
        "conv_kv": np.concatenate([np.concatenate([a["ckw"], a["ckb"][:, None]], 1),
                                   np.concatenate([a["cvw"], a["cvb"][:, None]], 1)], 0),
        "conv_q": np.concatenate([np.concatenate([a["cqw"], a["cqb"][:, None]], 1)] * 2, 0),
        "b_ae": np.concatenate([a["ab"], a["eb"]])[:, None],
        "b_t": over_partitions(a["tb"]), "b_g": over_partitions(a["gb"]), "norm_g": over_partitions(a["norm_g"]),
        "w1T": np.broadcast_to(a["mW1"].T[:, None, :], (D, B, D)),
        "w2T": np.broadcast_to(a["mW2"].T[:, None, :], (D, B, D)),
        "ident": eye, "iota": np.broadcast_to(np.arange(P, dtype=f)[None, :], (P, P)),
        "partition": np.arange(P, dtype=f)[:, None],
        "rank": np.broadcast_to((E - np.arange(E)).astype(f)[None, :], (P, E)),
        "upper": np.triu(np.ones((P, P), f)), "ones": np.ones((P, P), f), "mean_w": np.full((P, P), 1.0 / H, f),
        "mean_a": np.where(low, 0.0, 1.0 / D).astype(f)[:, None] * np.ones((1, P), f),
        "mean_e": np.where(low, 1.0 / D, 0.0).astype(f)[:, None] * np.ones((1, P), f),
        "fold": np.concatenate([eye[:D, :D]] * 2, 0), "fold_low": np.concatenate([0 * eye[:D, :D], eye[:D, :D]], 0),
        "minus_i": np.broadcast_to(-eye[:D, None, :D], (D, B, D)),
        "ab_start": np.where(low, 0.0, 1.0).astype(f)[:, None],
    }
    arrays = {k: np.ascontiguousarray(v) for k, v in arrays.items()}
    nc = bacc.Bacc("TRN2", target_bir_lowering=False, num_devices=1)
    d = {k: nc.dram_tensor("in_" + k, v.shape, F32, kind="ExternalInput").ap() for k, v in arrays.items()}
    d["out"] = nc.dram_tensor("out_x", (TOK, H), F32, kind="ExternalOutput").ap()
    build(nc, d)
    r = run_bass_kernel_spmd(nc, [{"in_" + k: v for k, v in arrays.items()}], core_ids=[0])
    return r.results[0]["out_x"].reshape(B, S, H)
```

```python
from contextlib import ExitStack

import concourse.bass as bass
from concourse import mybir

F32 = mybir.dt.float32
F32R = mybir.dt.float32r
BF16 = mybir.dt.bfloat16
I32 = mybir.dt.int32
ALU = mybir.AluOpType
ACT = mybir.ActivationFunctionType
AX = mybir.AxisListType

P = 128
B, S, H = 8, 1024, 256
D = 64
CH = 128
NCH = S // CH
TOK = B * S
NT = TOK // P
KH = H // P
E, F, CAP = 8, 1024, 320
SLOTS = E * CAP
ST = SLOTS // P
PAIRS = E // 2
PT = ST // PAIRS
TURNS = (PT + 1) // 2
KF = F // P
LN_EPS = 1e-5
EPS = 1e-6
BIG = 16384.0
TAPS = 4
BW = B * CH


class Semaphores(dict):

    def __init__(self, nc, ctx, prefix):
        self.nc, self.ctx, self.prefix = nc, ctx, prefix

    def __missing__(self, name):
        self[name] = self.ctx.enter_context(self.nc.semaphore(self.prefix + name))
        return self[name]


def bc(ap, shape):
    return ap.broadcast_to(shape)


def route(nc, sems, ctx, ps, t, name, weights):

    def sem(n):
        return sems[n]

    def sb(n, shape, dt):
        return ctx.enter_context(nc.sbuf_tensor(f"{name}_{n}", shape, dt))

    logits, ones_row = t["logits"], t["ones_row"]
    top = sb("top", [P, NT], F32)
    hit = sb("hit", [P, NT, E], F32)
    rank = sb("rank", [P, NT], F32)
    onehot = sb("onehot", [P, NT, E], BF16)
    total = sb("total", [P, NT, E], F32)
    running = sb("running", [P, NT, E], F32)
    place = sb("place", [P, NT, E], F32)
    pos = sb("pos", [P, NT], F32)
    over = sb("over", [P, NT], F32)
    slot = sb("slot", [P, NT], F32)
    slot_i = sb("slot_i", [P, NT], I32)
    row_i = sb("row_i", [P, NT], I32)
    col_i = sb("col_i", [P, NT], I32)
    row = sb("row", [P, NT], F32)
    col = sb("col", [P, NT], F32)
    row_hot = sb("row_hot", [P, NT, P], BF16)
    col_hot = sb("col_hot", [P, NT, 3, ST], BF16)
    found = sb("found", [P, 3, ST], F32)
    token = sb("token", [P, ST], F32)
    empty = sb("empty", [P, ST], F32)
    sc_f = sb("sc_f", [P, ST], F32)
    cum_ps = ps[:, 0, :].rearrange("p (n e) -> p n e", e=E)
    tot_ps = ps[:, 1, :].rearrange("p (n e) -> p n e", e=E)
    tab_ps = ps[:, 2, 0:3 * ST]
    QUARTER = NT // 4

    chain = sem("dve_done")
    onehot_ready = sem("onehot_ready")
    counts_ready = sem("counts_ready")
    col_hot_ready = sem("col_hot_ready")
    row_hot_ready = sem("row_hot_ready")
    table_ready = sem("table_ready")
    with nc.Block() as block:

        @block.sync
        def _(sp):
            for u in Weights.UNITS:
                weights.load(sp, 0, u)

        @block.vector
        def _(dve):
            v = nc.vector
            v.tensor_reduce(top[:], logits[:], AX.X, ALU.max).then_inc(chain, 1)
            dve.wait_ge(chain, 1)
            v.tensor_tensor(hit[:], logits[:], bc(top[:].unsqueeze(2), [P, NT, E]), ALU.is_equal).then_inc(chain, 1)
            dve.wait_ge(chain, 2)
            v.tensor_tensor(hit[:], hit[:], bc(t["rank_of_expert"][:].unsqueeze(1), [P, NT, E]),
                            ALU.mult).then_inc(chain, 1)
            dve.wait_ge(chain, 3)
            v.tensor_reduce(rank[:], hit[:], AX.X, ALU.max).then_inc(chain, 1)
            dve.wait_ge(chain, 4)
            v.tensor_tensor(onehot[:], hit[:], bc(rank[:].unsqueeze(2), [P, NT, E]),
                            ALU.is_equal).then_inc(onehot_ready, 1)
            dve.wait_ge(counts_ready, 1)
            v.tensor_copy(total[:], tot_ps).then_inc(chain, 1)
            dve.wait_ge(chain, 5)
            for e in range(E):
                last = v.tensor_tensor_scan(running[:, :, e], ones_row[:, 0:NT], total[:, :, e], 0.0,
                                            ALU.mult, ALU.add)
            last.then_inc(chain, 1)
            dve.wait_ge(chain, 6)
            v.tensor_tensor(running[:], running[:], total[:], ALU.subtract).then_inc(chain, 1)
            dve.wait_ge(chain, 7)
            v.tensor_tensor(place[:], cum_ps, running[:], ALU.add).then_inc(chain, 1)
            dve.wait_ge(chain, 8)
            v.tensor_tensor(place[:], place[:], onehot[:], ALU.mult).then_inc(chain, 1)
            dve.wait_ge(chain, 9)
            v.tensor_reduce(pos[:], place[:], AX.X, ALU.add).then_inc(chain, 1)
            dve.wait_ge(chain, 10)
            v.tensor_scalar(over[:], pos[:], float(CAP), BIG, ALU.is_gt, ALU.mult).then_inc(chain, 1)
            v.tensor_scalar(slot[:], rank[:], -float(CAP), float(E * CAP) - 1.0, ALU.mult, ALU.add).then_inc(chain, 1)
            dve.wait_ge(chain, 12)
            v.tensor_tensor(slot[:], slot[:], pos[:], ALU.add).then_inc(chain, 1)
            dve.wait_ge(chain, 13)
            v.tensor_tensor(slot_i[:], slot[:], over[:], ALU.add).then_inc(chain, 1)
            dve.wait_ge(chain, 14)
            v.tensor_scalar(row_i[:], slot_i[:], P - 1, None, ALU.bitwise_and).then_inc(chain, 1)
            v.tensor_scalar(col_i[:], slot_i[:], 7, None, ALU.logical_shift_right).then_inc(chain, 1)
            dve.wait_ge(chain, 16)
            v.tensor_copy(row[:], row_i[:]).then_inc(chain, 1)
            v.tensor_copy(col[:], col_i[:]).then_inc(chain, 1)
            dve.wait_ge(chain, 18)
            v.tensor_tensor(col_hot[:, :, 0, :], bc(col[:].unsqueeze(2), [P, NT, ST]),
                            bc(t["iota"][:, 0:ST].unsqueeze(1), [P, NT, ST]), ALU.is_equal).then_inc(chain, 1)
            dve.wait_ge(chain, 19)
            v.tensor_tensor(col_hot[:, :, 1, :], col_hot[:, :, 0, :],
                            bc(t["iota"][:, 0:NT].unsqueeze(2), [P, NT, ST]), ALU.mult)
            v.tensor_scalar(col_hot[:, :, 2, :], col_hot[:, :, 0, :], t["partition"][:, 0:1], None,
                            ALU.mult).then_inc(col_hot_ready, 1)
            for i in range(4):
                n = slice(i * QUARTER, (i + 1) * QUARTER)
                v.tensor_tensor(row_hot[:, n, :], bc(row[:, n].unsqueeze(2), [P, QUARTER, P]),
                                bc(t["iota"][:].unsqueeze(1), [P, QUARTER, P]),
                                ALU.is_equal).then_inc(row_hot_ready, 1)
            dve.wait_ge(table_ready, 1)
            v.tensor_copy(found[:], tab_ps.rearrange("p (a s) -> p a s", a=3)).then_inc(chain, 1)
            dve.wait_ge(chain, 20)
            v.scalar_tensor_tensor(token[:], found[:, 1, :], float(P), found[:, 2, :], ALU.mult,
                                   ALU.add).then_inc(chain, 1)
            v.tensor_scalar(empty[:], found[:, 0, :], -BIG, BIG, ALU.mult, ALU.add).then_inc(chain, 1)
            dve.wait_ge(chain, 22)
            v.tensor_copy(t["gather_index"][:], token[:]).then_inc(chain, 1)
            v.tensor_tensor(t["scatter_index"][:], token[:], empty[:], ALU.add).then_inc(chain, 1)

        @block.tensor
        def _(pe):
            pe.wait_ge(onehot_ready, 1)
            nc.tensor.matmul(ps[:, 0, :], t["upper"][:], onehot[:].rearrange("p n e -> p (n e)"), start=True, stop=True)
            nc.tensor.matmul(ps[:, 1, :], t["ones_bf"][:], onehot[:].rearrange("p n e -> p (n e)"), start=True,
                             stop=True).then_inc(counts_ready, 1)
            pe.wait_ge(col_hot_ready, 1)
            for n in range(NT):
                if n % QUARTER == 0:
                    pe.wait_ge(row_hot_ready, n // QUARTER + 1)
                last = nc.tensor.matmul(tab_ps, row_hot[:, n, :], col_hot[:, n, :, :].rearrange("p a s -> p (a s)"),
                                        start=(n == 0), stop=(n == NT - 1))
            last.then_inc(table_ready, 1)


class Weights:

    UNITS = ("up", 0), ("up", 1), ("down", 0), ("down", 1)

    def __init__(self, nc, ctx, sems, t, name):
        def sb(n, unit, dt):
            shape = [P, KH, F] if unit[0] == "up" else [P, KF, H]
            return ctx.enter_context(nc.sbuf_tensor(f"{name}_{n}_{unit[0]}{unit[1]}", shape, dt))

        self.nc, self.t = nc, t
        self.raw = {u: sb("raw", u, F32) for u in self.UNITS}
        self.high = {u: sb("high", u, F32R) for u in self.UNITS}
        self.low = {u: sb("low", u, F32R) for u in self.UNITS}
        self.loaded = {u: sems[f"loaded_{u[0]}{u[1]}"] for u in self.UNITS}
        self.high_done = {u: sems[f"high_done_{u[0]}{u[1]}"] for u in self.UNITS}
        self.low_done = {u: sems[f"low_done_{u[0]}{u[1]}"] for u in self.UNITS}

    def load(self, sp, g, u):
        dram = self.t["w1" if u[0] == "up" else "w2"]
        sp.dma_start(self.raw[u][:], dram[bass.ds(g * 2 + u[1], 1), :, :].rearrange("o (k p) n -> p (o k) n", p=P)
                     ).then_inc(self.loaded[u], 16)

    def piece(self, w, u, f):
        return w[u][:, :, f * P:(f + 1) * P] if u[0] == "up" else w[u][:, f:f + 1, :]


def experts(nc, sems, ctx, ps, t, name, weights, rows_dram, result_dram, result_ready=None, later=None):

    def sem(n):
        return sems[n]

    def sb(n, shape, dt=F32):
        return ctx.enter_context(nc.sbuf_tensor(f"{name}_{n}", shape, dt))

    UP, DOWN = Weights.UNITS[0:2], Weights.UNITS[2:4]
    rows = sb("rows", [P, ST, H])
    stats = sb("stats", [P, PT, 6])
    moments = sb("moments", [P, PT, 2])
    rstd = sb("rstd", [P, PT])
    var_eps = sb("var_eps", [P, PT])
    spare = sb("spare", [P, 1])
    normed = sb("normed", [P, PT, H])
    normedT = sb("normedT", [P, KH, PT * P])
    normedT_high, normedT_low = sb("normedT_high", [P, KH, PT * P], F32R), sb("normedT_low", [P, KH, PT * P], F32R)
    lg = sb("lg", [P, PT, E])
    lmax = sb("lmax", [P, PT])
    ex = sb("ex", [P, PT, E])
    den = sb("den", [P, PT])
    prob = sb("prob", [P, PT])
    hidden_high = [sb(f"hidden_high{i}", [P, KF, i * D + CAP], F32R) for i in range(2)]
    hidden_low = [sb(f"hidden_low{i}", [P, KF, i * D + CAP], F32R) for i in range(2)]

    gathered = sem("pool_dma_gathered_" + name)
    stats_done = sem("stats_done")
    moments_done = sem("moments_done")
    rstd_done = sem("rstd_done")
    var_done = sem("var_done")
    normed_ready = sem("normed_ready")
    turned = sem("turned")
    turned_copied = sem("turned_copied")
    turned_split = sem("turned_split")
    logits_done = sem("logits_done")
    lg_copied = sem("lg_copied")
    lmax_done = sem("lmax_done")
    lg_shifted = sem("lg_shifted")
    exp_done = sem("exp_done")
    den_done = sem("den_done")
    inv_done = sem("inv_done")
    prob_ready = sem("prob_ready")
    up_done = [sem(f"up_done{i}") for i in range(2)]
    relu_done = sem("relu_done")
    relu_split = sem("relu_split")
    y_done = [sem(f"y_done{i}") for i in range(2)]
    y_read = sem("y_read")
    padded = sem("padded")
    scattered = sem("pool_dma_scattered_" + name)

    YS = [[(0, 0, P, 0), (1, 0, P, P), (2, 0, D, 2 * P)], [(2, D, D, 0), (3, 0, P, P), (4, 0, P, 2 * P)]]
    NY = len(YS[0])

    with nc.Block() as block:

        @block.sync
        def _(sp):
            sp.wait_ge(gathered, 16 * PT)
            for dst, src in later.loads if later else ():
                sp.dma_start(dst, src).then_inc(later.loaded, 16)
            with sp.Fori(1, PAIRS) as g:
                for u in Weights.UNITS:
                    sp.wait_ge(weights.low_done[u], g * KF)
                    weights.load(sp, g, u)

        @block.gpsimd
        def _(pool):
            def gather(g):
                for j in range(g * PT, (g + 1) * PT):
                    nc.gpsimd.indirect_dma_start(rows[:, j, :], None, rows_dram,
                                                 bass.IndirectOffsetOnAxis(t["gather_index"][:, j:j + 1], 0),
                                                 bounds_check=TOK - 1, oob_is_err=False).then_inc(gathered, 16)

            def power(g):
                pool.wait_ge(var_done, g + 1)
                nc.gpsimd.tensor_tensor(rstd[:], var_eps[:], t["minus_half"][:, 0:PT], ALU.pow).then_inc(rstd_done, 1)

            def scatter(g):
                for i in range(PT):
                    j = g * PT + i
                    pool.wait_ge(y_read, 2 * NY * g + (i + 1 if i < 2 else i + 2))
                    nc.gpsimd.indirect_dma_start(result_dram,
                                                 bass.IndirectOffsetOnAxis(t["scatter_index"][:, j:j + 1], 0),
                                                 rows[:, j, :], None,
                                                 bounds_check=TOK - 1, oob_is_err=False).then_inc(scattered, 16)

            for g in range(PAIRS):
                gather(g)
                if g == 0:
                    power(0)
                pool.wait_ge(gathered, 16 * PT * (g + 1))
            if result_ready is not None:
                pool.wait_ge(result_ready, 16)
            for g in range(PAIRS):
                if g + 1 < PAIRS:
                    power(g + 1)
                scatter(g)
            pool.wait_ge(scattered, 16 * ST)

        @block.vector
        def _(dve):
            v = nc.vector

            def norm(g):
                dve.wait_ge(gathered, 16 * PT * (g + 1))
                for i in range(PT):
                    v.bn_stats(stats[:, i, :], rows[:, bass.ds(g * PT + i, 1), :].rearrange("p o h -> p (o h)")
                               ).then_inc(stats_done, 1)
                dve.wait_ge(stats_done, PT * (g + 1))
                v.memset(spare[:], 0.0)
                for i in range(PT):
                    v.bn_aggr(moments[:, i, :], stats[:, i, :]).then_inc(moments_done, 1)
                dve.wait_ge(moments_done, PT * (g + 1))
                v.tensor_scalar(var_eps[:], moments[:, :, 1], LN_EPS, None, ALU.add).then_inc(var_done, 1)

            def normalise(g, first):
                if not first:
                    dve.wait_ge(turned, TURNS * g)
                dve.wait_ge(rstd_done, g + 1)
                for i in range(PT):
                    v.tensor_scalar(normed[:, i, :], rows[:, bass.ds(g * PT + i, 1), :].rearrange("p o h -> p (o h)"),
                                    moments[:, i, 0:1], rstd[:, i:i + 1], ALU.subtract,
                                    ALU.mult).then_inc(normed_ready, 1)

            def split_turned(g, i):
                dve.wait_ge(turned_copied, TURNS * g + i + 1)
                n = slice(2 * i * P, min(2 * i + 2, PT) * P)
                v.tensor_tensor(normedT_low[:, :, n], normedT[:, :, n], normedT_high[:, :, n].bitcast(F32),
                                ALU.subtract).then_inc(turned_split, 1)

            def shifted_logits(g):
                dve.wait_ge(logits_done, g + 1)
                v.tensor_copy(lg[:], ps[:, 5, 0:PT * E].rearrange("p (i e) -> p i e", e=E)).then_inc(lg_copied, 1)
                dve.wait_ge(lg_copied, g + 1)
                v.tensor_reduce(lmax[:], lg[:], AX.X, ALU.max).then_inc(lmax_done, 1)
                dve.wait_ge(lmax_done, g + 1)
                v.tensor_tensor(lg[:], lg[:], bc(lmax[:].unsqueeze(2), [P, PT, E]),
                                ALU.subtract).then_inc(lg_shifted, 1)

            def probability(g, first):
                dve.wait_ge(exp_done, g + 1)
                v.tensor_reduce(den[:], ex[:], AX.X, ALU.add).then_inc(den_done, 1)
                dve.wait_ge(den_done, g + 1)
                if not first:
                    dve.wait_ge(y_read, 2 * NY * g)
                v.reciprocal(prob[:], den[:]).then_inc(inv_done, 1)
                dve.wait_ge(inv_done, g + 1)
                v.tensor_scalar(prob[:], prob[:], 0.5, None, ALU.mult).then_inc(prob_ready, 1)
                dve.wait_ge(prob_ready, g + 1)

            def low_piece(g, u, f):
                dve.wait_ge(weights.high_done[u], KF * g + f + 1)
                v.tensor_tensor(weights.piece(weights.low, u, f), weights.piece(weights.raw, u, f),
                                weights.piece(weights.high, u, f).bitcast(F32),
                                ALU.subtract).then_inc(weights.low_done[u], 1)

            def low_hidden(g, i, f):
                dve.wait_ge(relu_done, 2 * KF * g + KF * i + f + 1)
                v.scalar_tensor_tensor(hidden_low[i][:, f, i * D:], ps[:, 2 + (KF * i + f) % 3, 0:CAP], 0.0,
                                       hidden_high[i][:, f, i * D:].bitcast(F32), ALU.max,
                                       ALU.subtract).then_inc(relu_split, 1)

            def finish(g, i, j):
                tile, p0, n, _ = YS[i][j]
                dve.wait_ge(y_done[i], NY * g + j + 1)
                r = rows[p0:p0 + n, bass.ds(g * PT + tile, 1), :].rearrange("p o h -> p (o h)")
                v.scalar_tensor_tensor(r, ps[p0:p0 + n, 6 + (NY * i + j) % 2, 0:H],
                                       prob[p0:p0 + n, tile:tile + 1], r, ALU.mult,
                                       ALU.add).then_inc(y_read, 1)

            def pair(g, first, last):
                for f in range(KF):
                    low_hidden(g, 0, f)
                    if f == 0:
                        shifted_logits(g)
                    elif f == 3:
                        probability(g, first)
                    low_piece(g, DOWN[1], f)
                for f in range(KF):
                    low_hidden(g, 1, f)
                    if not last:
                        low_piece(g + 1, UP[0], f)
                if not last:
                    norm(g + 1)
                finish(g, 0, 0)
                if not last:
                    normalise(g + 1, False)
                finish(g, 0, 1)
                if not last:
                    for f in range(KF):
                        low_piece(g + 1, UP[1], f)
                finish(g, 0, 2)
                if last:
                    for j in range(NY):
                        finish(g, 1, j)
                    return
                for f in range(KF // 2):
                    low_piece(g + 1, DOWN[0], f)
                for j in range(NY):
                    finish(g, 1, j)
                    split_turned(g + 1, j)
                    if j == 0:
                        for f in range(KF // 2, KF):
                            low_piece(g + 1, DOWN[0], f)

            for u in (UP[0], UP[1]):
                for f in range(KF):
                    low_piece(0, u, f)
            norm(0)
            normalise(0, True)
            v.memset(hidden_high[1][:, :, 0:D].bitcast(F32), 0.0).then_inc(padded, 1)
            for i in range(TURNS):
                split_turned(0, i)
            v.memset(hidden_low[1][:, :, 0:D].bitcast(F32), 0.0).then_inc(padded, 1)
            for f in range(KF):
                low_piece(0, DOWN[0], f)
            pair(0, True, False)
            with dve.Fori(1, PAIRS - 1) as g:
                pair(g, False, False)
            pair(PAIRS - 1, False, True)

        @block.scalar
        def _(act):
            s = nc.scalar

            def high_piece(g, u, f, first):
                if f == 0:
                    act.wait_ge(weights.loaded[u], 16 * g + 16)
                if not first:
                    if u[0] == "up":
                        act.wait_ge(up_done[u[1]], KF * (g - 1) + f + 1)
                    elif f == 0:
                        act.wait_ge(y_done[u[1]], NY * g)
                s.copy(weights.piece(weights.high, u, f), weights.piece(weights.raw, u, f)
                       ).then_inc(weights.high_done[u], 1)

            def turned_tiles(g, i, first):
                if i == 0 and not first:
                    act.wait_ge(up_done[1], KF * g)
                act.wait_ge(turned, TURNS * g + i + 1)
                n = slice(2 * i * P, min(2 * i + 2, PT) * P)
                src = ps[:, i % 2, 0:KH * (n.stop - n.start)].rearrange("p (k c) -> p k c", k=KH)
                s.copy(normedT[:, :, n], src)
                s.copy(normedT_high[:, :, n], src).then_inc(turned_copied, 1)

            def exponentials(g):
                act.wait_ge(lg_shifted, g + 1)
                s.activation(ex[:], lg[:], ACT.Exp).then_inc(exp_done, 1)

            def relu(g, i, f, first):
                if f == 0 and not first:
                    act.wait_ge(y_done[i], NY * g)
                act.wait_ge(up_done[i], KF * g + f + 1)
                s.activation(hidden_high[i][:, f, i * D:], ps[:, 2 + (KF * i + f) % 3, 0:CAP],
                             ACT.Relu).then_inc(relu_done, 1)

            def pair(g, first, last):
                for f in range(KF):
                    relu(g, 0, f, first)
                    if f == 2:
                        exponentials(g)
                    high_piece(g, DOWN[1], f, first)
                for f in range(KF):
                    relu(g, 1, f, first)
                    if not last:
                        high_piece(g + 1, UP[0], f, False)
                if not last:
                    for f in range(KF):
                        high_piece(g + 1, UP[1], f, False)
                    for f in range(KF):
                        high_piece(g + 1, DOWN[0], f, False)
                    for i in range(TURNS):
                        turned_tiles(g + 1, i, False)

            for u in (UP[0], UP[1]):
                for f in range(KF):
                    high_piece(0, u, f, True)
            for i in range(TURNS):
                turned_tiles(0, i, True)
            for f in range(KF):
                high_piece(0, DOWN[0], f, True)
            pair(0, True, False)
            with act.Fori(1, PAIRS - 1) as g:
                pair(g, False, False)
            pair(PAIRS - 1, False, True)

        @block.tensor
        def _(pe):
            mm = nc.tensor.matmul

            def passes(dst, high_l, low_l, high_r, low_r, start, stop):
                mm(dst, high_l, high_r, start=start, stop=False)
                mm(dst, high_l, low_r, start=False, stop=False)
                return mm(dst, low_l, high_r, start=False, stop=stop)

            def logits(g, i, first):
                pe.wait_ge(turned_copied, TURNS * g + i + 1)
                if i == 0 and not first:
                    pe.wait_ge(lg_copied, g)
                for j in range(2 * i, min(2 * i + 2, PT)):
                    for k in range(KH):
                        last = mm(ps[:, 5, j * E:(j + 1) * E], normedT[:, k, j * P:(j + 1) * P], t["gate_w"][:, k, :],
                                  start=(k == 0), stop=(k == KH - 1))
                return last

            def turn(g, i, first):
                tiles = range(2 * i, min(2 * i + 2, PT))
                if i == 2 or i == 0 and not first:
                    pe.wait_ge(turned_copied, TURNS * g + i // 2)
                for j in tiles:
                    pe.wait_ge(normed_ready, PT * g + j + 1)
                    for k in range(KH):
                        at = (k * len(tiles) + j - 2 * i) * P
                        last = nc.tensor.transpose(ps[:, i % 2, at:at + P], normed[:, j, k * P:(k + 1) * P],
                                                   t["ident"][:])
                last.then_inc(turned, 1)

            def up(g, i, first):
                pe.wait_ge(turned_split, TURNS * g + TURNS - 1 + i)
                for f in range(KF):
                    pe.wait_ge(weights.low_done[UP[i]], KF * g + f + 1)
                    if KF * i + f >= 3 or not first:
                        pe.wait_ge(relu_split, 2 * KF * g + KF * i + f - 2)
                    for k in range(KH):
                        m, n = slice(f * P, (f + 1) * P), slice(i * CAP, (i + 1) * CAP)
                        last = passes(ps[:, 2 + (KF * i + f) % 3, 0:CAP], weights.high[UP[i]][:, k, m],
                                      weights.low[UP[i]][:, k, m], normedT_high[:, k, n], normedT_low[:, k, n],
                                      k == 0, k == KH - 1)
                    last.then_inc(up_done[i], 1)

            def down(g, i, j, first):
                if j == 0:
                    pe.wait_ge(weights.low_done[DOWN[i]], KF * g + KF)
                    pe.wait_ge(relu_split, 2 * KF * g + KF * (i + 1))
                if i == 1 and j == 0 and first:
                    pe.wait_ge(padded, 2)
                if not first or NY * i + j >= 2:
                    pe.wait_ge(y_read, 2 * NY * g + NY * i + j - 1)
                _, p0, n, c0 = YS[i][j]
                c = slice(c0, c0 + p0 + n)
                for f in range(KF):
                    last = passes(ps[0:p0 + n, 6 + (NY * i + j) % 2, 0:H], hidden_high[i][:, f, c],
                                  hidden_low[i][:, f, c], weights.high[DOWN[i]][:, f, :],
                                  weights.low[DOWN[i]][:, f, :], f == 0, f == KF - 1)
                last.then_inc(y_done[i], 1)

            def pair(g, first, last):
                up(g, 0, first)
                up(g, 1, first)
                for j in range(NY):
                    down(g, 0, j, first)
                for j in range(NY):
                    down(g, 1, j, first)
                    if not last:
                        turn(g + 1, j, False)
                        if j:
                            logits(g + 1, j - 1, False)
                if not last:
                    logits(g + 1, TURNS - 1, False).then_inc(logits_done, 1)

            for i in range(TURNS):
                turn(0, i, True)
                last = logits(0, i, True)
            last.then_inc(logits_done, 1)
            pair(0, True, False)
            with pe.Fori(1, PAIRS - 1) as g:
                pair(g, False, False)
            pair(PAIRS - 1, False, True)


def first_logits(nc, sems, ctx, ps, t, x_dram, xT_dram, x1_dram):

    def sem(n):
        return sems[n]

    GROUP = 1024
    PER = GROUP // P
    xt = [ctx.enter_context(nc.sbuf_tensor(f"xt{i}", [P, KH, GROUP], F32)) for i in range(2)]
    mean = ctx.enter_context(nc.sbuf_tensor("gate_mean", [P, E], F32))
    along = [ctx.enter_context(nc.sbuf_tensor(f"along{i}", [E, GROUP], F32)) for i in range(2)]
    stage = ctx.enter_context(nc.sbuf_tensor("stage", [P, 2, P], F32))
    consts = sem("consts")
    x_copied = sem("x_copied")
    loaded = [sem(f"loaded{i}") for i in range(2)]
    mean_done = sem("mean_done")
    mean_copied = sem("mean_copied")
    centred = sem("centred")
    made = sem("made")
    copied = sem("copied")
    placed = sem("placed")
    read = sem("read")
    cast = sem("cast")
    loads = [(t["ident"][:], t["d_ident"]), (t["iota"][:], t["d_iota"]), (t["partition"][:], t["d_partition"]),
             (t["rank_of_expert"][:], t["d_rank"]), (t["gate_w"][:], t["d_gate_w"].rearrange("(k p) e -> p k e", p=P)),
             (stage[:, 0, :], t["d_upper"]), (t["mean_w"][:], t["d_mean_w"]), (stage[:, 1, :], t["d_ones"])]

    with nc.Block() as block:

        @block.sync
        def _(sp):
            def load(n, i):
                sp.dma_start(xt[i][:], xT_dram[:, bass.ds(n * GROUP, GROUP)].rearrange("(k p) n -> p k n", p=P)
                             ).then_inc(loaded[i], 16)

            for dst, src in loads:
                sp.dma_start(dst, src).then_inc(consts, 16)
            load(0, 0)
            load(1, 1)
            with sp.Fori(1, TOK // GROUP // 2) as n:
                for i in range(2):
                    sp.wait_ge(made, n * 2 + i - 1)
                    load(n * 2 + i, i)
            sp.dma_start(x1_dram.rearrange("(a b) h -> a (b h)", a=P), x_dram.rearrange("(a b) h -> a (b h)", a=P)
                         ).then_inc(x_copied, 16)

        @block.vector
        def _(dve):
            v = nc.vector
            dve.wait_ge(consts, 16 * len(loads))
            v.tensor_copy(t["upper"][:], stage[:, 0, :]).then_inc(cast, 1)
            v.tensor_copy(t["ones_bf"][:], stage[:, 1, :]).then_inc(cast, 1)
            v.memset(t["ones_row"][:], 1.0).then_inc(cast, 1)
            v.memset(t["minus_half"][:], -0.5).then_inc(cast, 1)
            dve.wait_ge(mean_done, 1)
            v.tensor_copy(mean[:], ps[:, 6, 0:E]).then_inc(mean_copied, 1)
            dve.wait_ge(mean_copied, 1)
            v.tensor_tensor(t["gate_c"][:], t["gate_w"][:], bc(mean[:].unsqueeze(1), [P, KH, E]),
                            ALU.subtract).then_inc(centred, 1)
            with dve.Fori(0, TOK // GROUP // 2) as n:
                for i in range(2):
                    dve.wait_ge(placed, n * 2 + i + 1)
                    v.tensor_copy(t["logits"][:, bass.ds(n * (2 * PER) + i * PER, PER), :],
                                  ps[:, 4 + i, 0:PER * E].rearrange("p (n e) -> p n e", e=E)).then_inc(read, 1)

        @block.scalar
        def _(act):
            def copy(n, i, first):
                act.wait_ge(made, n * 2 + i + 1)
                if not first:
                    act.wait_ge(placed, n * 2 + i - 1)
                nc.scalar.copy(along[i][:].rearrange("e (h n) -> e h n", h=2), ps[0:E, 2 * i:2 * i + 2, :]
                               ).then_inc(copied, 1)

            for i in range(2):
                copy(0, i, True)
            with act.Fori(1, TOK // GROUP // 2) as n:
                for i in range(2):
                    copy(n, i, False)

        @block.tensor
        def _(pe):
            pe.wait_ge(consts, 16 * len(loads))
            for k in range(KH):
                last = nc.tensor.matmul(ps[:, 6, 0:E], t["mean_w"][:], t["gate_w"][:, k, :], start=(k == 0),
                                        stop=(k == KH - 1))
            last.then_inc(mean_done, 1)
            pe.wait_ge(centred, 1)

            def products(n, i, first):
                pe.wait_ge(loaded[i], n * 16 + 16)
                if not first:
                    pe.wait_ge(copied, n * 2 + i - 1)
                for h in range(2):
                    for k in range(KH):
                        last = nc.tensor.matmul(ps[0:E, 2 * i + h, :], t["gate_c"][:, k, :],
                                                xt[i][:, k, h * (GROUP // 2):(h + 1) * (GROUP // 2)],
                                                start=(k == 0), stop=(k == KH - 1))
                last.then_inc(made, 1)

            def place(n, i, first):
                pe.wait_ge(copied, n * 2 + i + 1)
                if not first:
                    pe.wait_ge(read, n * 2 + i)
                nc.tensor.matmul(ps[:, 6, 0:E], t["mean_w"][:], t["gate_w"][:, 0, :], start=True, stop=True)
                for j in range(PER):
                    last = nc.tensor.transpose(ps[:, 4 + i, j * E:(j + 1) * E], along[i][:, j * P:(j + 1) * P],
                                               t["ident"][0:E, 0:E])
                last.then_inc(placed, 1)

            products(0, 0, True)
            products(0, 1, True)
            place(0, 0, True)
            with pe.Fori(1, TOK // GROUP // 2) as n:
                products(n, 0, False)
                place(n - 1, 1, False)
                products(n, 1, False)
                place(n, 0, False)
            place(TOK // GROUP // 2 - 1, 1, False)


class AttentionInputs:

    def __init__(self, nc, ctx, sems, d):
        def sb(n, shape):
            return ctx.enter_context(nc.sbuf_tensor(f"att_{n}", shape, F32))

        self.conv_kv, self.conv_q = sb("conv_kv", [P, TAPS + 1]), sb("conv_q", [P, TAPS + 1])
        self.b_ae, self.b_t, self.b_g, self.norm_g = (
            sb("b_ae", [P, 1]), sb("b_t", [P, D]), sb("b_g", [P, H]), sb("norm_g", [P, H]))
        self.fold, self.fold_low = sb("fold", [P, D]), sb("fold_low", [P, D])
        self.ab_start = sb("ab_start", [P, 1])
        self.state, self.read_w = sb("state0", [P, B, 3 * D]), sb("read_w", [P, B, P])
        self.gate = sb("GATE1", [P, B, H])
        stage, cols = self.gate[:].rearrange("p b n -> p (b n)"), KH * (3 * P + H + D)
        self.w = stage[:, 0:cols].rearrange("p (k n) -> p k n", k=KH)
        self.w_o = stage[0:D, cols:cols + H]
        self.means = [stage[:, cols + H + i * P:cols + H + (i + 1) * P] for i in range(2)]
        self.loaded = sems["consts"]
        self.loads = [
            (self.w, d["w_x"].rearrange("(k p) n -> p k n", p=P)), (self.w_o, d["w_o"]),
            (self.conv_kv[:], d["conv_kv"]), (self.conv_q[:], d["conv_q"]),
            (self.b_ae[:], d["b_ae"]), (self.b_t[:], d["b_t"]), (self.b_g[:], d["b_g"]), (self.norm_g[:], d["norm_g"]),
            (self.means[0], d["mean_a"]), (self.means[1], d["mean_e"]), (self.fold[:], d["fold"]),
            (self.fold_low[:], d["fold_low"]), (self.state[0:D, :, 0:D], d["w1T"]),
            (self.state[0:D, :, D:2 * D], d["w1T"]), (self.state[0:D, :, 2 * D:3 * D], d["w2T"]),
            (self.read_w[0:D, :, 0:D], d["w2T"]), (self.read_w[D:P, :, 0:D], d["minus_i"]),
            (self.ab_start[:], d["ab_start"])]


def memory_attention(nc, sems, ctx, ps, t, x_dram, out_dram, given):

    def sem(n):
        return sems[n]

    def sb(n, shape, dt=F32):
        return ctx.enter_context(nc.sbuf_tensor(f"att_{n}", shape, dt))

    def two(n, shape):
        return [sb(f"{n}{i}", shape) for i in range(2)]

    HALF = B // 2
    HW = HALF * CH
    w_high, w_low = sb("w_high", [P, KH, 3 * P + H + D], F32R), sb("w_low", [P, KH, 3 * P + H + D], F32R)
    KV_COLS, QQ_COLS, AE_COLS, GT_COLS = slice(0, P), slice(P, 2 * P), slice(2 * P, 3 * P), slice(3 * P, 3 * P + H + D)
    w_o_high, w_o_low = sb("w_o_high", [D, H], F32R), sb("w_o_low", [D, H], F32R)
    conv_kv, conv_q, b_ae, b_t = given.conv_kv, given.conv_q, given.b_ae, given.b_t
    b_g, norm_g, fold, fold_low, ab_start = given.b_g, given.norm_g, given.fold, given.fold_low, given.ab_start
    mean_a, mean_e = sb("mean_a", [P, P], F32R), sb("mean_e", [P, P], F32R)
    x_norm = sb("x_norm", [P, B, H])
    stats, moments, var_eps, rstd = sb("stats", [P, B, 6]), sb("moments", [P, B, 2]), sb("var_eps", [P, B]), sb("rstd", [P, B])
    xT_high, xT_low = sb("xT_high", [P, KH, BW], F32R), sb("xT_low", [P, KH, BW], F32R)
    raw_kv, raw_q = sb("raw_kv", [P, B, TAPS - 1 + CH]), sb("raw_q", [P, B, TAPS - 1 + CH])
    keep, eta = sb("keep", [P, B, CH]), sb("eta", [P, B, CH])
    mom = sb("mom", [P, B, CH])
    sig_ae = mom[:].rearrange("p b n -> p (b n)")
    sig_high, sig_low = sb("sig_high", [P, BW], F32R), sb("sig_low", [P, BW], F32R)
    carry = sb("carry", [P, B, CH])
    theta_pre, theta_log = sb("theta_pre", [P, B, D]), sb("theta_log", [P, B, D])
    theta_sum = sb("theta_sum", [P, B])
    zeros = sb("zeros", [P, CH])
    Q, QAB = sb("Q", [P, B, CH]), sb("QAB", [P, B, CH])
    KV = two("KV", [P, B, CH])
    P1, M, AB = sb("P1", [P, B, CH]), sb("M", [P, B, CH]), sb("AB", [P, B, CH])
    spare = sb("spare", [P, 1])
    KM, MIX = sb("KM", [P, B, 2, D]), sb("MIX", [P, B, P])
    GATE, ENDS = [sb("GATE0", [P, B, H]), given.gate], two("ENDS", [P, B, 2])
    THETA, KNORM = two("THETA", [P, B]), two("KNORM", [P, B])
    x_res = sb("x_res", [P, B, H])
    state, read_w = [given.state, sb("state1", [P, B, 3 * D])], given.read_w
    sig_h, hid, slope = sb("sig_h", [P, B, D]), sb("hid", [P, B, D]), sb("slope", [P, B, D])
    hid_m = sb("hid_m", [P, B, 2, D])
    squares = sb("squares", [P, 3, B, D])
    dpre, grad_w1, grad_w2 = sb("dpre", [P, B, D]), sb("grad_w1", [P, B, 2, D]), sb("grad_w2", [P, B, D])
    k_sq = dpre
    nsum = sb("nsum", [P, 3, B])
    n1, n2, n3, n4, n5, factor = (sb(f"n{i}", [P, B]) for i in range(6))
    hid2, hid2_ab = (sb(n, [P, B, CH]) for n in ("hid2", "hid2_ab"))
    sig_h2 = P2 = hid2
    retrieved_high, retrieved_low = sb("retrieved_high", [D, B, CH], F32R), sb("retrieved_low", [D, B, CH], F32R)
    o_sq = squares[:].rearrange("p a b n -> p (a b n)")[:, 0:HALF * H].rearrange("p (b n) -> p b n", n=H)
    o_sum, o_mean, o_rs = sb("o_sum", [P, B]), sb("o_mean", [P, B]), sb("o_rs", [P, B])
    x2T = sb("x2T", [P, KH, BW])

    consts, folded, rounded = sem("consts"), sem("folded"), sem("rounded")
    x_loaded = sem("x_loaded")
    stats_done, moments_done, rstd_done, x_normed = sem("stats_done"), sem("moments_done"), sem("rstd_done"), sem("x_normed")
    var_done, n_clipped, powered = sem("var_done"), sem("n_clipped"), sem("powered")
    x_turned, x_turned_copied, x_turned_split = sem("x_turned"), sem("x_turned_copied"), sem("x_turned_split")
    ae_copied, ae_split, ret_split = sem("ae_copied"), sem("ae_split"), sem("ret_split")
    kv_made, kv_copied, q_made, q_copied = sem("kv_made"), sem("kv_copied"), sem("q_made"), sem("q_copied")
    kv_conv, q_conv, halo_kv, halo_q = sem("kv_conv"), sem("q_conv"), sem("halo_kv"), sem("halo_q")
    ae_made, ae_sig, rates_made, keep_ready, eta_ready = (sem(n) for n in ("ae_made", "ae_sig", "rates_made", "keep_ready", "eta_ready"))
    mom_ready, carry_ready, m_ready, ab_ready, ends_ready = (sem(n) for n in ("mom_ready", "carry_ready", "m_ready", "ab_ready", "ends_ready"))
    qab_ready, mix_ready = sem("qab_ready"), sem("mix_ready")
    gate_made, gate_read = sem("gate_made"), sem("gate_read")
    t_abs, t_exp, t_ln, t_soft, t_sum, theta_ready = (sem(n) for n in ("t_abs", "t_exp", "t_ln", "t_soft", "t_sum", "theta_ready"))
    k_turned, k_squared, km_ready, knorm_ready = (sem(n) for n in ("k_turned", "k_squared", "km_ready", "knorm_ready"))
    qk_made, p1_ready = sem("qk_made"), sem("p1_ready")
    pre_made, sig_ready, hid_ready, tmp_ready, slope_ready = (sem(n) for n in ("pre_made", "sig_ready", "hid_ready", "tmp_ready", "slope_ready"))
    hid_turned, hid_turned_copied, hid_m_ready = sem("hid_turned"), sem("hid_turned_copied"), sem("hid_m_ready")
    res_made, dpre_ready, squared, nsum_ready, small = (sem(n) for n in ("res_made", "dpre_ready", "squared", "nsum_ready", "small"))
    grad_w1_ready, grad_w2_ready = sem("grad_w1_ready"), sem("grad_w2_ready")
    pre2_made, sig2_ready, hid2_ready, hid2_ab_ready = (sem(n) for n in ("pre2_made", "sig2_ready", "hid2_ready", "hid2_ab_ready"))
    hh_made, p2_ready, ret_made, ret_copied = (sem(n) for n in ("hh_made", "p2_ready", "ret_made", "ret_copied"))
    state_made, state_copied, state_turned, w2_copied, gram_made, gram_copied = (
        sem(n) for n in ("state_made", "state_copied", "state_turned", "w2_copied", "gram_made", "gram_copied"))
    o_made, o_squared, o_meaned, o_rs_ready, gated_ready = (sem(n) for n in ("o_made", "o_squared", "o_meaned", "o_rs_ready", "gated_ready"))
    res_loaded, x2_ready, x2_stored, x2_turned, x2_turned_copied = (
        sem(n) for n in ("res_loaded", "x2_ready", "x2_stored", "x2_turned", "x2_turned_copied"))
    lg_made, lg_read = sem("lg_made"), sem("lg_read")

    x_v = x_dram.rearrange("(b c t) h -> c t b h", b=B, t=CH)
    out_v = out_dram.rearrange("(b c t) h -> c t b h", b=B, t=CH)

    def step_of(a, c):
        return a[bass.ds(c, 1), :, :, :].rearrange("o t b h -> t (o b) h")

    w_whole, w_o_whole, mean_whole, loads = given.w, given.w_o, given.means, given.loads

    A, BB, C, DD = (ps[:, 2 * i:2 * i + 2, :] for i in range(4))

    def wide(pair):
        return pair.rearrange("p a (b n) -> p (a b) n", n=CH)

    with nc.Block() as block:

        @block.sync
        def _(sp):
            def load_x(c):
                sp.dma_start(x_norm[:], step_of(x_v, c)).then_inc(x_loaded, 16)

            def load_res(c):
                sp.dma_start(x_res[:], step_of(x_v, c)).then_inc(res_loaded, 16)

            def store(c):
                sp.wait_ge(x2_ready, 2 * c + 2)
                sp.dma_start(step_of(out_v, c), x_res[:]).then_inc(x2_stored, 16)

            load_x(0)
            load_res(0)
            with sp.Fori(0, NCH - 1) as c:
                store(c)
                sp.wait_ge(x2_stored, 16 * c + 16)
                sp.wait_ge(x2_turned, 2 * c + 2)
                load_res(c + 1)
            store(NCH - 1)
            sp.wait_ge(x2_stored, 16 * NCH)

        @block.gpsimd
        def _(pool):
            g = nc.gpsimd

            def prep(c, very_first):
                pool.wait_ge(ab_ready, c + 1)
                pool.wait_ge(q_conv, TAPS * c + TAPS)
                if not very_first:
                    pool.wait_ge(pre2_made, c)
                g.tensor_tensor(QAB[:], Q[:], AB[:], ALU.mult).then_inc(qab_ready, 1)
                g.tensor_tensor(MIX[:, :, 0:D], bc(fold[:].unsqueeze(1), [P, B, D]),
                                bc(AB[:, :, CH - 1:CH], [P, B, D]), ALU.mult).then_inc(mix_ready, 1)
                g.tensor_tensor(MIX[:, :, D:P], bc(fold_low[:].unsqueeze(1), [P, B, D]),
                                bc(carry[:, :, CH - 1:CH], [P, B, D]), ALU.mult).then_inc(mix_ready, 1)

            def hidden(c, par, first):
                pool.wait_ge(ends_ready, c + 1)
                pool.wait_ge(hid_ready, c + 1)
                if not first:
                    pool.wait_ge(state_made, c)
                g.tensor_tensor(hid_m[:], bc(hid[:].unsqueeze(2), [P, B, 2, D]),
                                bc(ENDS[par][:].unsqueeze(3), [P, B, 2, D]), ALU.mult).then_inc(hid_m_ready, 1)

            def norm(c):
                pool.wait_ge(var_done, c + 1)
                g.tensor_tensor(rstd[:], var_eps[:], t["minus_half"][:, 0:B], ALU.pow).then_inc(rstd_done, 1)

            def gradient_norm(c):
                pool.wait_ge(n_clipped, c + 1)
                g.tensor_tensor(n5[:], n4[:], t["minus_half"][:, 0:B], ALU.pow).then_inc(powered, 1)

            def output_power(c, h):
                n = slice(h * HALF, (h + 1) * HALF)
                pool.wait_ge(o_meaned, 2 * c + h + 1)
                g.tensor_tensor(o_rs[:, n], o_mean[:, n], t["minus_half"][:, n], ALU.pow).then_inc(o_rs_ready, 1)

            def residual(c, par, h):
                n = slice(h * HALF, (h + 1) * HALF)
                if h == 0:
                    pool.wait_ge(res_loaded, 16 * c + 16)
                pool.wait_ge(gated_ready, 2 * c + h + 1)
                g.tensor_tensor(x_res[:, n, :], x_res[:, n, :], GATE[par][:, n, :], ALU.add).then_inc(x2_ready, 1)

            def step(c, par, first, last, norm_too=True):
                gradient_norm(c)
                if norm_too:
                    norm(c + 2)
                if not last:
                    prep(c + 1, False)
                output_power(c, 0)
                residual(c, par, 0)
                output_power(c, 1)
                if not last:
                    hidden(c + 1, 1 - par, False)
                residual(c, par, 1)

            norm(0)
            norm(1)
            prep(0, True)
            hidden(0, 0, True)
            step(0, 0, True, False)
            with pool.Fori(0, NCH // 2 - 2) as i:
                step(i * 2 + 1, 1, False, False)
                step(i * 2 + 2, 0, False, False)
            step(NCH - 3, 1, False, False)
            step(NCH - 2, 0, False, False, norm_too=False)
            step(NCH - 1, 1, False, True, norm_too=False)

        @block.vector
        def _(dve):
            v = nc.vector

            def start():
                dve.wait_ge(consts, 16 * len(loads))
                v.memset(zeros[:], 0.0).then_inc(folded, 1)
                v.memset(spare[:], 0.0).then_inc(lg_read, 1)
                v.memset(raw_kv[:, :, 0:TAPS - 1], 0.0).then_inc(halo_kv, 1)
                v.memset(raw_q[:, :, 0:TAPS - 1], 0.0).then_inc(halo_q, 1)
                v.memset(carry[0:D, :, :], 0.0).then_inc(folded, 1)
                v.memset(state[0][D:P, :, :], 0.0).then_inc(folded, 1)
                w_gate = w_whole[:, :, GT_COLS.start:GT_COLS.start + H]
                v.tensor_tensor(w_gate, w_gate, bc(norm_g[:].unsqueeze(1), [P, KH, H]),
                                ALU.mult).then_inc(folded, 1)
                v.tensor_tensor(b_g[:], b_g[:], norm_g[:], ALU.mult).then_inc(folded, 1)
                dve.wait_ge(folded, 5)
                for high, low, whole in ((w_high, w_low, w_whole), (w_o_high, w_o_low, w_o_whole)):
                    v.tensor_copy(high[:], whole).then_inc(rounded, 1)
                for m, whole in ((mean_a, mean_whole[0]), (mean_e, mean_whole[1])):
                    v.tensor_copy(m[:], whole).then_inc(rounded, 1)
                dve.wait_ge(rounded, 4)
                for high, low, whole in ((w_high, w_low, w_whole), (w_o_high, w_o_low, w_o_whole)):
                    v.tensor_tensor(low[:], whole, high[:].bitcast(F32), ALU.subtract).then_inc(rounded, 1)

            def stats_of(c, batches, very_first=False):
                if batches[0] == 0:
                    dve.wait_ge(x_loaded, 16 * c + 16)
                    if not very_first:
                        dve.wait_ge(x_normed, B * c)
                for b in batches:
                    v.bn_stats(stats[:, b, :], x_norm[:, b, :]).then_inc(stats_done, 1)

            def moments_of(c):
                dve.wait_ge(stats_done, B * c + B)
                v.memset(spare[:], 0.0)
                for b in range(B):
                    v.bn_aggr(moments[:, b, :], stats[:, b, :]).then_inc(moments_done, 1)
                dve.wait_ge(moments_done, B * c + B)
                v.tensor_scalar(var_eps[:], moments[:, :, 1], LN_EPS, None, ALU.add).then_inc(var_done, 1)

            def normalise(c):
                dve.wait_ge(rstd_done, c + 1)
                for b in range(B):
                    v.tensor_scalar(x_norm[:, b, :], x_norm[:, b, :], moments[:, b, 0:1], rstd[:, b:b + 1],
                                    ALU.subtract, ALU.mult).then_inc(x_normed, 1)

            def split_turned(c):
                for h, src in enumerate((A, BB)):
                    dve.wait_ge(x_turned_copied, 2 * c + h + 1)
                    n = slice(h * HW, (h + 1) * HW)
                    v.tensor_tensor(xT_low[:, :, n], src, xT_high[:, :, n].bitcast(F32),
                                    ALU.subtract).then_inc(x_turned_split, 1)

            def split_sigmoids(c):
                dve.wait_ge(ae_copied, c + 1)
                v.tensor_tensor(sig_low[:], sig_ae, sig_high[:].bitcast(F32), ALU.subtract).then_inc(ae_split, 1)

            def split_retrieved(c):
                dve.wait_ge(ret_copied, c + 1)
                v.tensor_tensor(retrieved_low[:], wide(DD)[0:D, :, :], retrieved_high[:].bitcast(F32),
                                ALU.subtract).then_inc(ret_split, 1)

            def tap(c, lane, n):
                y, x, w, done = lane
                j = TAPS - 1 - n
                dve.wait_ge(done, TAPS * c + n)
                v.scalar_tensor_tensor(y[:], x[:, :, j:j + CH], w[:, j:j + 1], y[:], ALU.mult,
                                       ALU.add).then_inc(done, 1)

            def convolve(c, par):
                lanes = [(KV[par], raw_kv, conv_kv, kv_conv), (Q, raw_q, conv_q, q_conv)]
                for n in range(1, TAPS - 1):
                    for lane in lanes:
                        tap(c, lane, n)
                tap(c, lanes[0], TAPS - 1)
                dve.wait_ge(kv_conv, TAPS * c + TAPS)
                v.tensor_copy(raw_kv[:, :, 0:TAPS - 1], raw_kv[:, :, CH:CH + TAPS - 1]).then_inc(halo_kv, 1)

            def convolve_rest(c):
                tap(c, (Q, raw_q, conv_q, q_conv), TAPS - 1)
                dve.wait_ge(q_conv, TAPS * c + TAPS)
                v.tensor_copy(raw_q[:, :, 0:TAPS - 1], raw_q[:, :, CH:CH + TAPS - 1]).then_inc(halo_q, 1)

            def momentum_scans(c):
                dve.wait_ge(eta_ready, c + 1)
                for b in range(B):
                    v.tensor_tensor_scan(mom[:, b, :], eta[:, b, :], t["ident"][:], 0.0, ALU.mult,
                                         ALU.add).then_inc(mom_ready, 1)

            def carry_scans(c, first):
                if not first:
                    dve.wait_ge(mix_ready, 2 * c)
                for b in range(B):
                    v.tensor_tensor_scan(carry[D:P, b, :], eta[D:P, b, :], zeros[D:P, :], 1.0, ALU.mult,
                                         ALU.add).then_inc(carry_ready, 1)

            def memory_scans(c, very_first):
                dve.wait_ge(keep_ready, c + 1)
                dve.wait_ge(mom_ready, B * c + B)
                if not very_first:
                    dve.wait_ge(p2_ready, c)
                    dve.wait_ge(p1_ready, c)
                    dve.wait_ge(hid2_ab_ready, c)
                    dve.wait_ge(mix_ready, 2 * c)
                for b in range(B):
                    v.tensor_tensor_scan(M[:, b, :], keep[:, b, :], mom[:, b, :], 0.0, ALU.mult,
                                         ALU.add).then_inc(m_ready, 1)

            def decay_scans(c, par, first):
                dve.wait_ge(carry_ready, B * c + B)
                for b in range(B):
                    last = v.tensor_tensor_scan(AB[:, b, :], keep[:, b, :], carry[:, b, :], ab_start[:, 0:1],
                                                ALU.mult, ALU.add)
                last.then_inc(ab_ready, 1)
                dve.wait_ge(m_ready, B * c + B)
                if not first:
                    dve.wait_ge(hid_m_ready, c - 1)
                v.tensor_copy(ENDS[par][:, :, 0:1], M[:, :, CH - 1:CH])
                v.tensor_copy(ENDS[par][:, :, 1:2], mom[:, :, CH - 1:CH]).then_inc(ends_ready, 1)

            def gates(c, par, pairs, first):
                if not first:
                    dve.wait_ge(x2_ready, 2 * c - 2)
                for i in pairs:
                    dve.wait_ge(gate_made, 4 * c + i + 1)
                    src = A if i % 2 else BB
                    v.tensor_tensor(GATE[par][:, 2 * i:2 * i + 2, :], src[:, :, 0:H],
                                    bc(b_g[:].unsqueeze(1), [P, 2, H]), ALU.add)
                    v.tensor_tensor(theta_pre[:, 2 * i:2 * i + 2, :], src[:, :, H:H + D],
                                    bc(b_t[:].unsqueeze(1), [P, 2, D]), ALU.add).then_inc(gate_read, 1)

            def thetas(c, par):
                dve.wait_ge(t_ln, c + 1)
                v.scalar_tensor_tensor(theta_log[:], theta_pre[:], 0.0, theta_log[:], ALU.max,
                                       ALU.add).then_inc(t_soft, 1)
                dve.wait_ge(t_soft, c + 1)
                v.tensor_reduce(theta_sum[:], theta_log[:], AX.X, ALU.add).then_inc(t_sum, 1)
                dve.wait_ge(t_sum, c + 1)
                v.tensor_scalar(THETA[par][:], theta_sum[:], -0.1 * 0.2 / D, None, ALU.mult).then_inc(theta_ready, 1)

            def keys(c, par, first):
                dve.wait_ge(k_turned, c + 1)
                dve.wait_ge(ends_ready, c + 1)
                if not first:
                    dve.wait_ge(state_made, c)
                v.tensor_tensor(KM[:], bc(wide(BB)[:, :, 0:D].unsqueeze(2), [P, B, 2, D]),
                                bc(ENDS[par][:].unsqueeze(3), [P, B, 2, D]), ALU.mult).then_inc(km_ready, 1)

            def key_norms(c, par):
                dve.wait_ge(k_squared, c + 1)
                v.tensor_reduce(KNORM[par][:], k_sq[:], AX.X, ALU.add).then_inc(knorm_ready, 1)

            def scores(c):
                dve.wait_ge(qk_made, c + 1)
                v.tensor_tensor(P1[:], wide(A), M[:], ALU.mult).then_inc(p1_ready, 1)

            def hidden(c, first):
                dve.wait_ge(sig_ready, c + 1)
                if not first:
                    dve.wait_ge(hid_m_ready, c)
                v.tensor_tensor(hid[:], wide(C)[:, :, 0:D], sig_h[:], ALU.mult).then_inc(hid_ready, 1)

            def slope_of(c):
                dve.wait_ge(hid_ready, c + 1)
                v.scalar_tensor_tensor(slope[:], sig_h[:], 1.0, hid[:], ALU.subtract, ALU.mult).then_inc(tmp_ready, 1)
                dve.wait_ge(tmp_ready, c + 1)
                v.tensor_tensor(slope[:], sig_h[:], slope[:], ALU.subtract).then_inc(slope_ready, 1)

            def residual(c):
                dve.wait_ge(res_made, c + 1)
                dve.wait_ge(slope_ready, c + 1)
                v.tensor_tensor(dpre[:], wide(C)[:, :, D:P], slope[:], ALU.mult).then_inc(dpre_ready, 1)

            def gradient_norms(c, par):
                dve.wait_ge(squared, 3 * c + 3)
                v.tensor_reduce(nsum[:], squares[:], AX.X, ALU.add).then_inc(nsum_ready, 1)
                dve.wait_ge(nsum_ready, c + 1)
                dve.wait_ge(knorm_ready, c + 1)
                v.tensor_tensor(n1[:], nsum[:, 0, :], nsum[:, 1, :], ALU.mult).then_inc(small, 1)
                v.tensor_tensor(n2[:], nsum[:, 2, :], KNORM[par][:], ALU.mult).then_inc(small, 1)
                dve.wait_ge(small, 4 * c + 2)
                v.tensor_tensor(n3[:], n1[:], n2[:], ALU.add).then_inc(small, 1)
                dve.wait_ge(small, 4 * c + 3)
                v.tensor_scalar(n4[:], n3[:], 0.04, EPS * EPS, ALU.mult, ALU.max).then_inc(n_clipped, 1)

            def gradients(c, par):
                dve.wait_ge(powered, c + 1)
                dve.wait_ge(theta_ready, c + 1)
                v.scalar_tensor_tensor(factor[:], n5[:], 1.0, THETA[par][:], ALU.min, ALU.mult).then_inc(small, 1)
                dve.wait_ge(small, 4 * c + 4)
                v.tensor_tensor(grad_w1[:], bc(dpre[:].unsqueeze(2), [P, B, 2, D]),
                                bc(factor[:].unsqueeze(2).unsqueeze(3), [P, B, 2, D]),
                                ALU.mult).then_inc(grad_w1_ready, 1)
                v.tensor_tensor(grad_w2[:], wide(C)[:, :, 0:D], bc(factor[:].unsqueeze(2), [P, B, D]),
                                ALU.mult).then_inc(grad_w2_ready, 1)

            def second_hidden(c, par):
                dve.wait_ge(sig2_ready, c + 1)
                v.tensor_tensor(hid2[:], wide(DD), sig_h2[:], ALU.mult).then_inc(hid2_ready, 1)

            def decayed_hidden(c):
                dve.wait_ge(hid2_ready, c + 1)
                v.tensor_tensor(hid2_ab[:], hid2[:], AB[:], ALU.mult).then_inc(hid2_ab_ready, 1)

            def second_scores(c, par):
                dve.wait_ge(hh_made, c + 1)
                dve.wait_ge(hid2_ab_ready, c + 1)
                v.tensor_tensor(P2[:], wide(DD), M[:], ALU.mult).then_inc(p2_ready, 1)

            def output_mean(c, h):
                n = slice(h * HALF, (h + 1) * HALF)
                dve.wait_ge(o_squared, B * c + HALF * (h + 1))
                v.tensor_scalar(o_mean[:, n], o_sum[:, n], 1.0 / H, EPS, ALU.mult, ALU.add).then_inc(o_meaned, 1)

            def gated_output(c, par, h):
                dve.wait_ge(o_rs_ready, 2 * c + h + 1)
                src = DD.rearrange("p a (b n) -> p (a b) n", n=H)
                for b in range(HALF):
                    bb = h * HALF + b
                    last = v.scalar_tensor_tensor(GATE[par][:, bb, :], src[:, b, :], o_rs[:, bb:bb + 1],
                                                  GATE[par][:, bb, :], ALU.mult, ALU.mult)
                last.then_inc(gated_ready, 1)

            def logits(c):
                dve.wait_ge(lg_made, c + 1)
                v.tensor_copy(t["logits"][:].rearrange("p (b c) e -> p b c e", c=NCH)[:, :, bass.ds(c, 1), :],
                              C[:, 0, 0:B * E].rearrange("p (b o e) -> p b o e", o=1, e=E)).then_inc(lg_read, 1)

            def step(c, par, first, last, norm_too=True):
                if not last:
                    split_turned(c + 1)
                slope_of(c)
                if not first:
                    output_mean(c - 1, 1)
                residual(c)
                if not first:
                    gated_output(c - 1, 1 - par, 1)
                gradient_norms(c, par)
                thetas(c, par)
                gradients(c, par)
                if norm_too:
                    stats_of(c + 2, range(B))
                    moments_of(c + 2)
                if not last:
                    split_sigmoids(c + 1)
                    convolve(c + 1, 1 - par)
                second_hidden(c, par)
                if not last:
                    convolve_rest(c + 1)
                decayed_hidden(c)
                if not last:
                    momentum_scans(c + 1)
                second_scores(c, par)
                if not last:
                    carry_scans(c + 1, False)
                    memory_scans(c + 1, False)
                    gates(c + 1, 1 - par, (0, 1), first)
                    decay_scans(c + 1, 1 - par, first)
                split_retrieved(c)
                if not last:
                    gates(c + 1, 1 - par, (2, 3), first)
                if not first:
                    logits(c - 1)
                if norm_too:
                    normalise(c + 2)
                if not last:
                    keys(c + 1, 1 - par, False)
                output_mean(c, 0)
                if not last:
                    scores(c + 1)
                    key_norms(c + 1, 1 - par)
                    hidden(c + 1, False)
                gated_output(c, par, 0)
                if last:
                    output_mean(c, 1)
                    gated_output(c, par, 1)

            start()
            stats_of(0, range(B), True)
            moments_of(0)
            normalise(0)
            split_turned(0)
            stats_of(1, range(B))
            moments_of(1)
            normalise(1)
            split_sigmoids(0)
            convolve(0, 0)
            convolve_rest(0)
            momentum_scans(0)
            carry_scans(0, True)
            gates(0, 0, (0, 1), True)
            memory_scans(0, True)
            decay_scans(0, 0, True)
            gates(0, 0, (2, 3), True)
            keys(0, 0, True)
            key_norms(0, 0)
            scores(0)
            hidden(0, True)
            step(0, 0, True, False)
            with dve.Fori(0, NCH // 2 - 2) as i:
                step(i * 2 + 1, 1, False, False)
                step(i * 2 + 2, 0, False, False)
            step(NCH - 3, 1, False, False)
            step(NCH - 2, 0, False, False, norm_too=False)
            step(NCH - 1, 1, False, True, norm_too=False)
            logits(NCH - 1)

        @block.scalar
        def _(act):
            s = nc.scalar

            def turned(c, first, load=True):
                if not first:
                    act.wait_ge(gate_made, 4 * c)
                for h, src in enumerate((A, BB)):
                    act.wait_ge(x_turned, 2 * c + h + 1)
                    if h and load:
                        act.dma_start(x_norm[:], step_of(x_v, c + 1)).then_inc(x_loaded, 16)
                    s.copy(xT_high[:, :, h * HW:(h + 1) * HW], src).then_inc(x_turned_copied, 1)

            def kv_projection(c):
                act.wait_ge(halo_kv, c + 1)
                act.wait_ge(kv_made, c + 1)
                s.copy(raw_kv[:, :, TAPS - 1:], wide(A)).then_inc(kv_copied, 1)

            def last_tap(c, par, first):
                if not first:
                    act.wait_ge(hh_made, c - 1)
                act.wait_ge(kv_copied, c + 1)
                s.activation(KV[par][:], raw_kv[:, :, TAPS - 1:], ACT.Identity, bias=conv_kv[:, TAPS:TAPS + 1],
                             scale=conv_kv[:, TAPS - 1:TAPS]).then_inc(kv_conv, 1)

            def q_projection(c, very_first):
                act.wait_ge(halo_q, c + 1)
                act.wait_ge(q_made, c + 1)
                s.copy(raw_q[:, :, TAPS - 1:], wide(BB)).then_inc(q_copied, 1)
                if not very_first:
                    act.wait_ge(qab_ready, c)
                    act.wait_ge(qk_made, c)
                act.wait_ge(q_copied, c + 1)
                s.activation(Q[:], raw_q[:, :, TAPS - 1:], ACT.Identity, bias=conv_q[:, TAPS:TAPS + 1],
                             scale=conv_q[:, TAPS - 1:TAPS]).then_inc(q_conv, 1)

            def sigmoids(c, first):
                act.wait_ge(ae_made, c + 1)
                if not first:
                    act.wait_ge(ends_ready, c)
                s.activation(sig_ae, A.rearrange("p a n -> p (a n)"), ACT.Sigmoid,
                             bias=b_ae[:, 0:1]).then_inc(ae_sig, 1)
                act.wait_ge(ae_sig, c + 1)
                s.copy(sig_high[:], sig_ae).then_inc(ae_copied, 1)

            def rates(c, first):
                act.wait_ge(rates_made, 2 * c + 1)
                if not first:
                    act.wait_ge(ab_ready, c)
                s.activation(keep[:], wide(BB), ACT.Copy, bias=1.0, scale=-0.1).then_inc(keep_ready, 1)
                act.wait_ge(rates_made, 2 * c + 2)
                s.activation(eta[:], wide(A), ACT.Copy, bias=0.05, scale=0.9).then_inc(eta_ready, 1)

            def thetas(c, first):
                act.wait_ge(gate_read, 4 * c + 4)
                if not first:
                    act.wait_ge(t_sum, c)
                s.activation(theta_log[:], theta_pre[:], ACT.Abs).then_inc(t_abs, 1)
                act.wait_ge(t_abs, c + 1)
                s.activation(theta_log[:], theta_log[:], ACT.Exp, scale=-1.0).then_inc(t_exp, 1)

            def theta_logs(c):
                act.wait_ge(t_exp, c + 1)
                s.activation(theta_log[:], theta_log[:], ACT.Ln, bias=1.0).then_inc(t_ln, 1)

            def keys(c, first):
                act.wait_ge(km_ready, c + 1)
                if not first:
                    act.wait_ge(grad_w1_ready, c)
                s.activation(k_sq[:], wide(BB)[:, :, 0:D], ACT.Square).then_inc(k_squared, 1)

            def hidden(c, first):
                act.wait_ge(pre_made, c + 1)
                if not first:
                    act.wait_ge(slope_ready, c)
                s.activation(sig_h[:], wide(C)[:, :, 0:D], ACT.Sigmoid).then_inc(sig_ready, 1)

            def hidden_turned(c, par, first):
                act.wait_ge(hid_turned, c + 1)
                s.copy(KV[par][0:D, :, :], wide(C)[0:D, :, :]).then_inc(hid_turned_copied, 1)
                if not first:
                    output_norms(c - 1, first, 1)
                    act.wait_ge(o_squared, B * c)
                s.activation(squares[:, 0, :, :], hid[:], ACT.Square).then_inc(squared, 1)

            def gradients(c):
                act.wait_ge(dpre_ready, c + 1)
                s.activation(squares[:, 1, :, :], wide(C)[:, :, 0:D], ACT.Square).then_inc(squared, 1)
                s.activation(squares[:, 2, :, :], dpre[:], ACT.Square).then_inc(squared, 1)

            def second_hidden(c):
                act.wait_ge(pre2_made, c + 1)
                s.activation(sig_h2[:], wide(DD), ACT.Sigmoid).then_inc(sig2_ready, 1)

            def retrieve(c):
                act.wait_ge(ret_made, c + 1)
                s.copy(retrieved_high[:], wide(DD)[0:D, :, :]).then_inc(ret_copied, 1)

            def new_state(c, par):
                act.wait_ge(state_made, c + 1)
                new = wide(C)
                s.copy(state[1 - par][:, :, 0:D], new[:, :, 0:D])
                s.copy(state[1 - par][:, :, D:3 * D], new).then_inc(state_copied, 1)
                s.copy(read_w[0:D, :, 0:D], new[0:D, :, D:P]).then_inc(state_copied, 1)

            def new_turned(n):
                act.wait_ge(state_turned, n + 1)
                s.mul(read_w[D:P, :, D:P], wide(C)[D:P, :, 0:D], -1.0).then_inc(w2_copied, 1)

            def new_gram(n):
                act.wait_ge(gram_made, n + 1)
                s.copy(read_w[0:D, :, D:P],
                       C[0:D, 0, :].rearrange("p (b n) -> p b n", n=D)).then_inc(gram_copied, 1)

            def output_norms(c, first, h):
                act.wait_ge(o_made, 2 * c + h + 1)
                if h or not first:
                    act.wait_ge(o_squared, B * c + HALF * h)
                if h == 0 and not first:
                    act.wait_ge(o_meaned, 2 * c)
                o = DD.rearrange("p a (b n) -> p (a b) n", n=H)
                for b in range(HALF):
                    bb = h * HALF + b
                    s.activation(o_sq[:, b, :], o[:, b, :], ACT.Square,
                                 accum_out=o_sum[:, bb:bb + 1]).then_inc(o_squared, 1)

            def result_turned(c, h):
                act.wait_ge(x2_turned, 2 * c + h + 1)
                s.copy(x2T[:, :, h * HW:(h + 1) * HW], DD).then_inc(x2_turned_copied, 1)

            def step(c, par, first, last, load=True):
                if not last:
                    turned(c + 1, False, load)
                hidden_turned(c, par, first)
                gradients(c)
                theta_logs(c)
                if not last:
                    kv_projection(c + 1)
                if not first:
                    result_turned(c - 1, 0)
                if not last:
                    last_tap(c + 1, 1 - par, first)
                    q_projection(c + 1, False)
                if not first:
                    result_turned(c - 1, 1)
                if not last:
                    sigmoids(c + 1, False)
                new_state(c, par)
                second_hidden(c)
                new_turned(c + 1)
                if not last:
                    rates(c + 1, False)
                new_gram(c + 1)
                retrieve(c)
                if not last:
                    thetas(c + 1, False)
                output_norms(c, first, 0)
                if not last:
                    keys(c + 1, False)
                    hidden(c + 1, False)
                if last:
                    output_norms(c, first, 1)

            new_turned(0)
            new_gram(0)
            turned(0, True)
            kv_projection(0)
            last_tap(0, 0, True)
            q_projection(0, True)
            sigmoids(0, True)
            rates(0, True)
            keys(0, True)
            thetas(0, True)
            hidden(0, True)
            step(0, 0, True, False)
            with act.Fori(0, NCH // 2 - 2) as i:
                step(i * 2 + 1, 1, False, False)
                step(i * 2 + 2, 0, False, False)
            step(NCH - 3, 1, False, False)
            step(NCH - 2, 0, False, False, load=False)
            step(NCH - 1, 1, False, True)
            result_turned(NCH - 1, 0)
            result_turned(NCH - 1, 1)

        @block.tensor
        def _(pe):
            mm = nc.tensor.matmul

            def turn_x(c, first):
                for h, dst in enumerate((A, BB)):
                    pe.wait_ge(x_normed, B * c + HALF * (h + 1))
                    if not first:
                        pe.wait_ge(p1_ready if h == 0 else knorm_ready, c)
                    for b in range(HALF):
                        for k in range(KH):
                            last = nc.tensor.transpose(dst[:, k, b * CH:(b + 1) * CH],
                                                       x_norm[:, h * HALF + b, k * P:(k + 1) * P], t["ident"][:])
                    last.then_inc(x_turned, 1)

            def passes(dst, high_l, low_l, high_r, low_r, start, stop):
                mm(dst, high_l, high_r, start=start, stop=False)
                mm(dst, high_l, low_r, start=False, stop=False)
                return mm(dst, low_l, high_r, start=False, stop=stop)

            def project(c, dst, cols, done):
                for h in range(2):
                    n = slice(h * HW, (h + 1) * HW)
                    for k in range(KH):
                        last = passes(dst[:, h, :], w_high[:, k, cols], w_low[:, k, cols], xT_high[:, k, n],
                                      xT_low[:, k, n], k == 0, k == KH - 1)
                last.then_inc(done, 1)

            def kv_projection(c):
                pe.wait_ge(x_turned_split, 2 * c + 2)
                project(c, A, KV_COLS, kv_made)

            def q_projection(c):
                project(c, BB, QQ_COLS, q_made)

            def ae_projection(c):
                pe.wait_ge(kv_copied, c + 1)
                project(c, A, AE_COLS, ae_made)

            def rates(c):
                pe.wait_ge(ae_split, c + 1)
                pe.wait_ge(q_copied, c + 1)
                for dst, w in ((BB, mean_a), (A, mean_e)):
                    for h in range(2):
                        n = slice(h * HW, (h + 1) * HW)
                        mm(dst[:, h, :], w[:], sig_high[:, n], start=True, stop=False)
                        last = mm(dst[:, h, :], w[:], sig_low[:, n], start=False, stop=True)
                    last.then_inc(rates_made, 1)

            def gates(c, pairs, logits_too):
                for i in pairs:
                    dst = A if i % 2 else BB
                    if i == 0:
                        pe.wait_ge(keep_ready, c + 1)
                    elif i == 1:
                        pe.wait_ge(eta_ready, c + 1)
                    else:
                        pe.wait_ge(gate_read, 4 * c + i - 1)
                    for j in range(2):
                        b = 2 * i + j
                        n = slice(b * CH, (b + 1) * CH)
                        for k in range(KH):
                            last = passes(dst[:, j, 0:H + D], xT_high[:, k, n], xT_low[:, k, n],
                                          w_high[:, k, GT_COLS], w_low[:, k, GT_COLS], k == 0, k == KH - 1)
                    last.then_inc(gate_made, 1)
                    if logits_too:
                        logits(c - 2, (2 * i, 2 * i + 1))

            def keys(c, par):
                pe.wait_ge(kv_conv, TAPS * c + TAPS)
                pe.wait_ge(gate_read, 4 * c + 3)
                for b in range(B):
                    last = nc.tensor.transpose(wide(BB)[:, b, :], KV[par][:, b, :], t["ident"][:])
                last.then_inc(k_turned, 1)
                pe.wait_ge(q_conv, TAPS * c + TAPS)
                pe.wait_ge(gate_read, 4 * c + 4)
                for b in range(B):
                    last = mm(wide(A)[:, b, :], KV[par][0:D, b, :], Q[0:D, b, :], start=True, stop=True)
                last.then_inc(qk_made, 1)

            def hidden(c, par, first):
                pe.wait_ge(kv_conv, TAPS * c + TAPS)
                pe.wait_ge(gram_copied, c + 1)
                if not first:
                    pe.wait_ge(state_copied, 2 * c)
                    pe.wait_ge(lg_read, c)
                for b in range(B):
                    last = mm(wide(C)[:, b, :], KV[par][0:D, b, :], state[par][0:D, b, 0:2 * D], start=True, stop=True)
                last.then_inc(pre_made, 1)

            def hidden_turned(c):
                pe.wait_ge(consts, 16 * len(loads))
                pe.wait_ge(hid_ready, c + 1)
                for b in range(B):
                    last = nc.tensor.transpose(wide(C)[0:D, b, :], hid[:, b, :], t["ident"][:])
                last.then_inc(hid_turned, 1)

            def residual(c, par):
                pe.wait_ge(hid_turned_copied, c + 1)
                pe.wait_ge(gram_copied, c + 1)
                for b in range(B):
                    last = mm(wide(C)[:, b, :], KV[par][:, b, :], read_w[:, b, :], start=True, stop=True)
                last.then_inc(res_made, 1)

            def second_hidden(c, par, first):
                pe.wait_ge(grad_w1_ready, c + 1)
                pe.wait_ge(p1_ready, c + 1)
                pe.wait_ge(qab_ready, c + 1)
                if not first:
                    pe.wait_ge(x2_turned_copied, 2 * c)
                for b in range(B):
                    mm(wide(DD)[:, b, :], state[par][:, b, 0:2 * D], QAB[:, b, :], start=True, stop=False)
                    last = mm(wide(DD)[:, b, :], grad_w1[:, b, :, :].rearrange("p a n -> p (a n)"), P1[:, b, :],
                              start=False, stop=True)
                last.then_inc(pre2_made, 1)

            def second_scores(c, par):
                pe.wait_ge(hid2_ready, c + 1)
                for b in range(B):
                    last = mm(wide(DD)[:, b, :], KV[par][0:D, b, :], hid2[0:D, b, :], start=True, stop=True)
                last.then_inc(hh_made, 1)

            def retrieve(c, par):
                pe.wait_ge(hid2_ab_ready, c + 1)
                pe.wait_ge(p2_ready, c + 1)
                for b in range(B):
                    mm(wide(DD)[0:D, b, :], state[par][:, b, 2 * D:3 * D], hid2_ab[:, b, :], start=True, stop=False)
                    last = mm(wide(DD)[0:D, b, :], grad_w2[:, b, :], P2[:, b, :], start=False, stop=True)
                last.then_inc(ret_made, 1)

            def new_state(c, par):
                pe.wait_ge(mix_ready, 2 * c + 2)
                pe.wait_ge(km_ready, c + 1)
                pe.wait_ge(hid_m_ready, c + 1)
                pe.wait_ge(grad_w2_ready, c + 1)
                for b in range(B):
                    dst = wide(C)[:, b, :]
                    mm(dst, MIX[:, b, :], state[par][:, b, D:3 * D], start=True, stop=False, skip_group_check=True)
                    mm(dst[:, 0:D], KM[:, b, :, :].rearrange("p a n -> p (a n)"), grad_w1[:, b, 0, :],
                       start=False, stop=False, skip_group_check=True)
                    last = mm(dst[:, D:P], hid_m[:, b, :, :].rearrange("p a n -> p (a n)"), grad_w2[:, b, :],
                              start=False, stop=True, skip_group_check=True)
                last.then_inc(state_made, 1)

            def turn_state(st):
                for b in range(B):
                    last = nc.tensor.transpose(wide(C)[:, b, :], st[:, b, D:3 * D], t["ident"][:])
                last.then_inc(state_turned, 1)

            def gram(n):
                pe.wait_ge(consts, 16 * len(loads))
                pe.wait_ge(w2_copied, n + 1)
                for b in range(B):
                    w2 = read_w[D:P, b, D:P]
                    last = mm(C[0:D, 0, b * D:(b + 1) * D], w2, w2, start=True, stop=True)
                last.then_inc(gram_made, 1)

            def outputs(c, h):
                if h == 0:
                    pe.wait_ge(ret_split, c + 1)
                else:
                    pe.wait_ge(gated_ready, 2 * c + 1)
                for b in range(HALF):
                    last = passes(DD[:, b // 2, (b % 2) * H:(b % 2 + 1) * H], retrieved_high[:, h * HALF + b, :],
                                  retrieved_low[:, h * HALF + b, :], w_o_high[:], w_o_low[:], True, True)
                last.then_inc(o_made, 1)

            def turn_result(c, h):
                pe.wait_ge(x2_ready, 2 * c + h + 1)
                if h == 0:
                    pe.wait_ge(gated_ready, 2 * c + 2)
                else:
                    pe.wait_ge(x2_turned_copied, 2 * c + 1)
                for b in range(HALF):
                    for k in range(KH):
                        last = nc.tensor.transpose(DD[:, k, b * CH:(b + 1) * CH],
                                                   x_res[:, h * HALF + b, k * P:(k + 1) * P], t["ident"][:])
                last.then_inc(x2_turned, 1)

            def logits_start(c, grams):
                pe.wait_ge(x2_turned_copied, 2 * c + 2)
                pe.wait_ge(gram_copied, grams)

            def logits(c, batches):
                for b in batches:
                    for k in range(KH):
                        last = mm(C[:, 0, b * E:(b + 1) * E], x2T[:, k, b * CH:(b + 1) * CH], t["gate_c"][:, k, :],
                                  start=(k == 0), stop=(k == KH - 1))
                if B - 1 in batches:
                    last.then_inc(lg_made, 1)

            def step(c, par, first, last):
                if not last:
                    turn_x(c + 1, False)
                hidden_turned(c)
                if not first:
                    outputs(c - 1, 1)
                residual(c, par)
                if not last:
                    kv_projection(c + 1)
                if not first:
                    turn_result(c - 1, 0)
                if not last:
                    q_projection(c + 1)
                if not first:
                    turn_result(c - 1, 1)
                if not last:
                    ae_projection(c + 1)
                new_state(c, par)
                second_hidden(c, par, first)
                pe.wait_ge(state_copied, 2 * c + 2)
                turn_state(state[1 - par])
                if not last:
                    rates(c + 1)
                gram(c + 1)
                second_scores(c, par)
                if not first:
                    logits_start(c - 1, c + 2)
                if not last:
                    gates(c + 1, (0, 1), not first)
                elif not first:
                    logits(c - 1, range(HALF))
                retrieve(c, par)
                if not last:
                    gates(c + 1, (2, 3), not first)
                else:
                    logits(c - 1, range(HALF, B))
                outputs(c, 0)
                if not last:
                    keys(c + 1, 1 - par)
                    hidden(c + 1, 1 - par, False)
                else:
                    outputs(c, 1)

            pe.wait_ge(consts, 16 * len(loads))
            pe.wait_ge(folded, 5)
            pe.wait_ge(rounded, 6)
            turn_state(state[0])
            gram(0)
            turn_x(0, True)
            kv_projection(0)
            q_projection(0)
            ae_projection(0)
            rates(0)
            gates(0, range(4), False)
            keys(0, 0)
            hidden(0, 0, True)
            step(0, 0, True, False)
            with pe.Fori(0, NCH // 2 - 1) as i:
                step(i * 2 + 1, 1, False, False)
                step(i * 2 + 2, 0, False, False)
            step(NCH - 1, 1, False, True)
            turn_result(NCH - 1, 0)
            turn_result(NCH - 1, 1)
            pe.wait_ge(lg_read, NCH)
            logits_start(NCH - 1, NCH + 1)
            logits(NCH - 1, range(B))


def build(nc, d):
    with ExitStack() as sems, ExitStack() as whole:
        def keep(n, shape, dt=F32):
            return whole.enter_context(nc.sbuf_tensor(n, shape, dt))

        ps = whole.enter_context(nc.psum_tensor("ps", [P, 8, 512], F32))
        t = {
            "ident": keep("ident", [P, P]), "iota": keep("iota", [P, P]), "partition": keep("partition", [P, 1]),
            "rank_of_expert": keep("rank_of_expert", [P, E]), "gate_w": keep("gate_w", [P, KH, E]),
            "gate_c": keep("gate_c", [P, KH, E]), "mean_w": keep("mean_w", [P, P]),
            "upper": keep("upper", [P, P], BF16), "ones_bf": keep("ones_bf", [P, P], BF16),
            "ones_row": keep("ones_row", [P, P]), "minus_half": keep("minus_half", [P, B]), "logits": keep("logits", [P, NT, E]),
            "gather_index": keep("gather_index", [P, ST], I32), "scatter_index": keep("scatter_index", [P, ST], I32),
            "w1": d["w1"], "w2": d["w2"],
        }
        for n in ("ident", "iota", "partition", "rank", "gate_w", "upper", "mean_w", "ones"):
            t["d_" + n] = d[n]
        x1 = nc.dram_tensor("x1", (TOK, H), F32, kind="Internal").ap()
        first = Semaphores(nc, sems, "first_")
        moe = Semaphores(nc, sems, "moe_")
        att = Semaphores(nc, sems, "att_")
        given = AttentionInputs(nc, whole, att, d)
        with ExitStack() as ctx:
            first_logits(nc, first, ctx, ps[:], t, d["x"], d["xT"], x1)
        with ExitStack() as outer:
            weights = Weights(nc, outer, moe, t, "weights1")
            with ExitStack() as ctx:
                route(nc, moe, ctx, ps[:], t, "route1", weights)
            with ExitStack() as ctx:
                experts(nc, moe, ctx, ps[:], t, "moe1", weights, d["x"], x1, first["x_copied"], given)
        with ExitStack() as ctx:
            memory_attention(nc, att, ctx, ps[:], t, x1, d["out"], given)
        with nc.Block() as block:
            @block.sync
            def _(sp):
                for n, s in moe.items():
                    if not n.startswith("pool_dma"):
                        sp.sem_clear(s)
        with ExitStack() as outer:
            weights = Weights(nc, outer, moe, t, "weights2")
            with ExitStack() as ctx:
                route(nc, moe, ctx, ps[:], t, "route2", weights)
            with ExitStack() as ctx:
                experts(nc, moe, ctx, ps[:], t, "moe2", weights, d["out"], d["out"])


def kernel(**inputs):
    import numpy as np
    import concourse.bacc as bacc
    from concourse.bass_utils import run_bass_kernel_spmd

    a = {k.replace("L0_attn_", ""): np.asarray(v) for k, v in inputs.items()}
    x = a["hidden"].reshape(TOK, H)
    f = np.float32
    eye = np.eye(P, dtype=f)

    def over_partitions(row):
        return np.broadcast_to(row[None, :], (P, row.shape[0]))

    low = np.arange(P) >= D
    arrays = {
        "x": x, "xT": x.T,
        "gate_w": a["L0_ffn_gate_w"], "w1": a["L0_ffn_w1"], "w2": a["L0_ffn_w2"],
        "w_x": np.concatenate([a[n].T for n in ("Wk", "Wv", "Wq", "Wq", "aW", "eW", "gW", "tW")], 1),
        "w_o": a["Wo"].T,
        "conv_kv": np.concatenate([np.concatenate([a["ckw"], a["ckb"][:, None]], 1),
                                   np.concatenate([a["cvw"], a["cvb"][:, None]], 1)], 0),
        "conv_q": np.concatenate([np.concatenate([a["cqw"], a["cqb"][:, None]], 1)] * 2, 0),
        "b_ae": np.concatenate([a["ab"], a["eb"]])[:, None],
        "b_t": over_partitions(a["tb"]), "b_g": over_partitions(a["gb"]), "norm_g": over_partitions(a["norm_g"]),
        "w1T": np.broadcast_to(a["mW1"].T[:, None, :], (D, B, D)),
        "w2T": np.broadcast_to(a["mW2"].T[:, None, :], (D, B, D)),
        "ident": eye, "iota": np.broadcast_to(np.arange(P, dtype=f)[None, :], (P, P)),
        "partition": np.arange(P, dtype=f)[:, None],
        "rank": np.broadcast_to((E - np.arange(E)).astype(f)[None, :], (P, E)),
        "upper": np.triu(np.ones((P, P), f)), "ones": np.ones((P, P), f), "mean_w": np.full((P, P), 1.0 / H, f),
        "mean_a": np.where(low, 0.0, 1.0 / D).astype(f)[:, None] * np.ones((1, P), f),
        "mean_e": np.where(low, 1.0 / D, 0.0).astype(f)[:, None] * np.ones((1, P), f),
        "fold": np.concatenate([eye[:D, :D]] * 2, 0), "fold_low": np.concatenate([0 * eye[:D, :D], eye[:D, :D]], 0),
        "minus_i": np.broadcast_to(-eye[:D, None, :D], (D, B, D)),
        "ab_start": np.where(low, 0.0, 1.0).astype(f)[:, None],
    }
    arrays = {k: np.ascontiguousarray(v) for k, v in arrays.items()}
    nc = bacc.Bacc("TRN2", target_bir_lowering=False, num_devices=1)
    d = {k: nc.dram_tensor("in_" + k, v.shape, F32, kind="ExternalInput").ap() for k, v in arrays.items()}
    d["out"] = nc.dram_tensor("out_x", (TOK, H), F32, kind="ExternalOutput").ap()
    build(nc, d)
    r = run_bass_kernel_spmd(nc, [{"in_" + k: v for k, v in arrays.items()}], core_ids=[0])
    return r.results[0]["out_x"].reshape(B, S, H)
```
